# Optimizing a Trainium2 kernel written in Bass

```python
import numpy as np
import jax
import jax.numpy as jnp

def _softmax(x, axis=-1):
    return jax.nn.softmax(x, axis=axis)

def _gelu(x):
    return jax.nn.gelu(x, approximate=True)

def _silu(x):
    return jax.nn.silu(x)

def _sigmoid(x):
    return jax.nn.sigmoid(x)

def _layernorm(x, axis=-1, eps=1e-05):
    m = jnp.mean(x, axis=axis, keepdims=True)
    v = jnp.var(x, axis=axis, keepdims=True)
    return (x - m) / jnp.sqrt(v + eps)

def _scatter_add(tgt, idx, src, axis=0):
    return tgt.at[idx].add(src)

def _segment_sum(src, seg, n):
    return jax.ops.segment_sum(src, seg, n)
kernel_name = 'mk_gnn_ffn_d1_gnn_r8_f3f018'

def setup_inputs(seed: int=0):
    np.random.seed(seed)
    _w = jnp.asarray

    def _rec_inputs():
        import jax
        import jax.numpy as jnp
        _gk = jax.random.key(seed)
        x = -0.0003713 + 1 * jax.random.normal(jax.random.fold_in(_gk, 1), (12500, 256), jnp.float32)
        src = jax.random.randint(jax.random.fold_in(_gk, 2), (200000,), 0, 12500, jnp.int32)
        dst = jax.random.randint(jax.random.fold_in(_gk, 3), (200000,), 0, 12500, jnp.int32)
        _o = jnp.argsort(dst, stable=True)
        src = src[_o]
        dst = dst[_o]
        edge_attr_128 = -5.16925e-05 + 1.00005 * jax.random.normal(jax.random.fold_in(_gk, 11), (200000, 128), jnp.float32)
        return (x, src, dst, edge_attr_128)
    x, src, dst, edge_attr_128 = _rec_inputs()

    def _L0_gnn_setup():
        import jax, jax.numpy as jnp
        import numpy as np
        N_NODES = 6250
        N_EDGES = 100000
        IN_DIM = 256
        OUT_DIM = 256
        HEADS = 1
        EDGE_DIM = 128
        NEG_SLOPE = 0.01
        key = jax.random.key(seed)
        ks = jax.random.split(key, 8)
        x = jax.random.normal(ks[0], (N_NODES, IN_DIM), dtype=jnp.float32)
        edge_index = jax.random.randint(ks[1], (2, N_EDGES), 0, N_NODES, dtype=jnp.int64)
        edge_attr = jax.random.normal(ks[2], (N_EDGES, EDGE_DIM), dtype=jnp.float32)
        hc = HEADS * OUT_DIM
        Wn = jax.random.normal(ks[3], (hc, IN_DIM), dtype=jnp.float32) / np.sqrt(IN_DIM)
        bn = jnp.zeros((hc,), dtype=jnp.float32)
        We = jax.random.normal(ks[4], (hc, EDGE_DIM), dtype=jnp.float32) / np.sqrt(EDGE_DIM)
        be = jnp.zeros((hc,), dtype=jnp.float32)
        attn = jax.random.normal(ks[5], (1, HEADS, OUT_DIM), dtype=jnp.float32) * np.sqrt(2.0 / (HEADS * OUT_DIM + 1))
        return {'x': x, 'edge_index': edge_index, 'edge_attr': edge_attr, 'Wn': Wn, 'bn': bn, 'We': We, 'be': be, 'attn': attn}
    _L0_gnn_all = _L0_gnn_setup()
    _L0_gnn_in = {k: v for k, v in _L0_gnn_all.items() if k in ('Wn', 'bn', 'We', 'be', 'attn')}
    del _L0_gnn_all

    def _L0_ffn_setup():
        import math
        import jax, jax.numpy as jnp
        import numpy as np
        CAPACITY_FACTOR = 1.25
        key = jax.random.key(seed)
        ks = jax.random.split(key, 5)
        B, L, D, F, E = (8, 1024, 256, 1024, 8)
        h = jax.random.normal(ks[0], (B, L, D), dtype=jnp.float32)
        gate_w = jax.random.normal(ks[1], (D, E), dtype=jnp.float32) * 0.02
        gate_b = jnp.zeros((E,), dtype=jnp.float32)
        w1 = jax.random.normal(ks[2], (E, D, F), dtype=jnp.float32) * (1.0 / math.sqrt(D))
        b1 = jnp.zeros((E, F), dtype=jnp.float32)
        w2 = jax.random.normal(ks[3], (E, F, D), dtype=jnp.float32) * (1.0 / math.sqrt(F))
        b2 = jnp.zeros((E, D), dtype=jnp.float32)
        return {'h': h, 'gate_w': gate_w, 'gate_b': gate_b, 'w1': w1, 'b1': b1, 'w2': w2, 'b2': b2}
    _L0_ffn_all = _L0_ffn_setup()
    _L0_ffn_in = {k: v for k, v in _L0_ffn_all.items() if k in ('gate_w', 'gate_b', 'w1', 'b1', 'w2', 'b2')}
    del _L0_ffn_all
    return {'x': x, 'src': src, 'dst': dst, 'edge_attr_128': edge_attr_128, 'L0_gnn_Wn': _L0_gnn_in['Wn'], 'L0_gnn_bn': _L0_gnn_in['bn'], 'L0_gnn_We': _L0_gnn_in['We'], 'L0_gnn_be': _L0_gnn_in['be'], 'L0_gnn_attn': _L0_gnn_in['attn'], 'L0_ffn_gate_w': _L0_ffn_in['gate_w'], 'L0_ffn_gate_b': _L0_ffn_in['gate_b'], 'L0_ffn_w1': _L0_ffn_in['w1'], 'L0_ffn_b1': _L0_ffn_in['b1'], 'L0_ffn_w2': _L0_ffn_in['w2'], 'L0_ffn_b2': _L0_ffn_in['b2']}

def reference(x, src, dst, edge_attr_128, L0_gnn_Wn, L0_gnn_bn, L0_gnn_We, L0_gnn_be, L0_gnn_attn, L0_ffn_gate_w, L0_ffn_gate_b, L0_ffn_w1, L0_ffn_b1, L0_ffn_w2, L0_ffn_b2):
    import jax
    import jax.numpy as jnp

    def _L0_gnn_ref(x, edge_index, edge_attr, Wn, bn, We, be, attn):
        import jax, jax.numpy as jnp
        import numpy as np
        N_NODES = 6250
        N_EDGES = 100000
        IN_DIM = 256
        OUT_DIM = 256
        HEADS = 1
        EDGE_DIM = 128
        NEG_SLOPE = 0.01
        N = x.shape[0]
        H, C = (attn.shape[1], attn.shape[2])
        src, dst = (edge_index[0], edge_index[1])
        h = x @ Wn.T + bn
        e = edge_attr @ We.T + be
        xj = h[src].reshape(-1, H, C)
        ee = e.reshape(-1, H, C)
        a = jax.nn.leaky_relu(jnp.sum((xj + ee) * attn, axis=-1), NEG_SLOPE)
        m = jax.ops.segment_max(a, dst, num_segments=N)
        a = jnp.exp(a - m[dst])
        denom = jax.ops.segment_sum(a, dst, num_segments=N)
        a = a / (denom[dst] + 1e-16)
        msg = (xj * a[..., None]).reshape(-1, H * C)
        out = jax.ops.segment_sum(msg, dst, num_segments=N)
        return jax.nn.relu(out)

    def _L0_ffn_ref(h, gate_w, gate_b, w1, b1, w2, b2):
        import math
        import jax, jax.numpy as jnp
        import numpy as np
        CAPACITY_FACTOR = 1.25
        B, L, D = h.shape
        E = gate_w.shape[1]
        T = B * L
        C = max(1, math.ceil(CAPACITY_FACTOR * T / E))
        x = h.reshape(T, D)
        logits = x @ gate_w + gate_b
        probs = jax.nn.softmax(logits, axis=-1)
        idx = jnp.argmax(probs, axis=-1)
        prb = jnp.take_along_axis(probs, idx[:, None], axis=1)[:, 0]
        one_hot = jax.nn.one_hot(idx, E, dtype=jnp.float32)
        pos = (jnp.cumsum(one_hot, axis=0) * one_hot).sum(-1).astype(jnp.int32) - 1
        kept = pos < C
        pos_safe = jnp.where(kept, pos, C)
        buf = jnp.zeros((E, C, D), dtype=h.dtype).at[idx, pos_safe].set(x, mode='drop')
        hmid = jax.nn.relu(jnp.einsum('ecd,edf->ecf', buf, w1) + b1[:, None, :])
        ybuf = jnp.einsum('ecf,efd->ecd', hmid, w2) + b2[:, None, :]
        pos_g = jnp.minimum(pos, C - 1)
        y_tok = ybuf[idx, pos_g] * (prb * kept)[:, None]
        y = y_tok.reshape(B, L, D)
        y = jnp.nan_to_num(y, nan=0.0, posinf=10000.0, neginf=-10000.0)
        return y
    edge_index = jnp.stack([src, dst])
    x = x + _L0_gnn_ref(_layernorm(x, axis=-1), edge_index, edge_attr_128, L0_gnn_Wn, L0_gnn_bn, L0_gnn_We, L0_gnn_be, L0_gnn_attn)
    x = x + _L0_ffn_ref(_layernorm(x, axis=-1)[None], L0_ffn_gate_w, L0_ffn_gate_b, L0_ffn_w1, L0_ffn_b1, L0_ffn_w2, L0_ffn_b2)[0]
    return x

_drawn_inputs = setup_inputs


def setup_inputs(seed=0):
    import zlib

    import numpy as np

    out = dict(_drawn_inputs(seed))
    spreads = {'L0_gnn_bn': (0.0, 0.1),
     'L0_gnn_be': (0.0, 0.8),
     'L0_ffn_gate_b': (0.0, 0.1),
     'L0_ffn_b1': (0.0, 0.66),
     'L0_ffn_b2': (0.0, 0.465)}
    factors = {}
    for name, (base, spread) in spreads.items():
        noise = np.random.default_rng([zlib.crc32(name.encode()), seed]).standard_normal(out[name].shape)
        drawn = base * np.exp(spread * noise) if base else spread * noise
        out[name] = jnp.asarray(drawn.astype(out[name].dtype))
    for name, factor in factors.items():
        out[name] = (out[name] * factor).astype(out[name].dtype)
    return out
```

```python
from contextlib import ExitStack

import concourse.bass as bass
from concourse import mybir

F32 = mybir.dt.float32
BF16 = mybir.dt.bfloat16
I32 = mybir.dt.int32
ALU = mybir.AluOpType
ACT = mybir.ActivationFunctionType
AX = mybir.AxisListType
ds = bass.ds

P = 128
BIG = 1e30
CHUNK_TILES = 16
SLOPE = 0.01
EPS = 1e-5
F32_MAX = 3.4028234663852886e38


def ceil_div(a, b):
    return -(-a // b)


class Sizes:

    def __init__(self, x, src, edge_attr, w1):
        self.nodes, self.dim = x.shape
        self.edges = src.shape[1]
        self.edge_dim = edge_attr.shape[1]
        self.experts, _, self.hidden = w1.shape
        self.node_tiles = 2 * ceil_div(self.nodes, 2 * P)
        self.last_rows = self.nodes - (self.node_tiles - 1) * P
        assert 0 < self.last_rows < P and self.dim == 2 * P and self.edge_dim == P
        self.chunks = 2 * ceil_div(self.edges, 2 * CHUNK_TILES * P)
        self.tiles = self.chunks * CHUNK_TILES
        self.table_blocks = ceil_div(self.tiles, P)
        self.table_tiles = self.table_blocks * P
        self.pad_edges = self.table_tiles * P
        self.gathered = self.dim + 2
        self.row = self.dim + 4
        self.capacity = max(1, ceil_div(5 * self.nodes, 4 * self.experts))
        self.block = 512
        self.blocks = ceil_div(self.capacity, self.block)
        self.slots = self.blocks * self.block
        self.k1 = self.dim // P
        self.k2 = self.hidden // P
        self.turn = max(u for u in range(1, 8) if self.node_tiles % u == 0)




def edge_tables(nc, z, src, dst, T, D):
    B, TT, PE_ = z.table_blocks, z.table_tiles, z.pad_edges
    pad = PE_ - z.edges
    pad_node = z.node_tiles * P - 1
    with ExitStack() as ctx:
        sb = lambda name, shape, dt=F32: ctx.enter_context(nc.sbuf_tensor(name, shape, dt))
        sem = z.semaphore
        pads = sb("pads", [1, pad + 1], I32)
        zero_pads = sb("zero_pads", [1, pad], I32)
        rows_i = sb("rows_i", [P, B, P], I32)
        rows = sb("rows", [P, B, P])
        prev = sb("prev", [P, B, P])
        starts = sb("starts", [P, B, P])
        keep = sb("keep", [P, B, P])
        ranks = sb("ranks", [P, B, P])
        masks = sb("masks", [P, B, 3, P])
        bounds = sb("bounds", [P, B, 2])
        tri = sb("tri", [P, P])
        tot = sb("tot", [P, B])
        small = sb("small", [P, 10, B])
        small_i = sb("small_i", [P, 2, B], I32)
        offs_i = sb("offs_i", [B, P], I32)
        rels = sb("rels", [B, P])
        rel_all = keep[:].rearrange("q b i -> q (b i)")
        tiles_i = sb("tiles_i", [P, 2, TT], I32)
        ps = ctx.enter_context(nc.psum_tensor("table_ps", [P, 2, 512], F32))
        padded, loaded, consts, chain, saved, transposed, evacuated = (
            sem("padded"), sem("rows_loaded"), sem("consts_ready"), sem("table_chain"),
            sem("tables_saved"), sem("transposed"), sem("evacuated"))
        pad_set = sem("pads_set")
        tot_ready, pre_ready, tables_ready, rel_ready, rels_ready = (
            sem("tot_ready"), sem("pre_ready"), sem("tables_ready"), sem("rel_ready"),
            sem("rels_ready"))
        rel_loaded = sem("rel_loaded")
        src_rows_ready, rows_free = sem("src_rows_ready"), sem("rows_free")
        block = ctx.enter_context(nc.Block())

        @block.sync
        def _(sp):
            sp.wait_ge(pad_set, 3)
            sp.dma_start(D["dst"][0:1, 0:1], pads[0:1, pad:pad + 1]).then_inc(padded, 16)
            sp.dma_start(D["dst"][0:1, 1:1 + z.edges], dst).then_inc(padded, 16)
            sp.dma_start(D["dst"][0:1, 1 + z.edges:1 + PE_], pads[0:1, 0:pad]).then_inc(padded, 16)
            sp.dma_start(D["src"][0:1, 0:z.edges], src).then_inc(padded, 16)
            sp.dma_start(D["src"][0:1, z.edges:PE_], zero_pads[0:1, :]).then_inc(padded, 16)
            sp.wait_ge(padded, 80)
            view = lambda d, at: d[0, at:at + PE_].rearrange("(b q i) -> q b i", q=P, i=P)
            sp.dma_start(rows_i[:], view(D["dst"], 1)).then_inc(loaded, 16)
            sp.wait_ge(rows_free, 1)
            sp.dma_start(rows_i[:], view(D["dst"], 0)).then_inc(loaded, 16)
            sp.wait_ge(rows_free, 2)
            sp.dma_start(rows_i[:], view(D["src"], 0)).then_inc(loaded, 16)
            sp.wait_ge(tables_ready, 1)
            sp.dma_start(D["masks"].rearrange("(b q) m -> q b m", q=P),
                         masks[:].rearrange("q b m i -> q b (m i)")).then_inc(saved, 16)
            sp.dma_start(D["bounds"].rearrange("(b q) m -> q b m", q=P), bounds[:]).then_inc(saved, 16)
            sp.wait_ge(rels_ready, 2)
            sp.dma_start(D["offs"].rearrange("(b q) -> b q", q=P), offs_i[:]).then_inc(saved, 16)
            sp.dma_start(D["rels"].rearrange("(b q) -> b q", q=P), rels[:]).then_inc(saved, 16)
            sp.wait_ge(saved, 64)
            sp.dma_start(T["offs"][0:1, :], D["offs"].rearrange("(a t) -> a t", a=1)[:, 0:z.tiles]).then_inc(rel_loaded, 16)
            sp.dma_start(rel_all, D["rels"].rearrange("(a t) -> a t", a=1).to_broadcast([P, TT]))\
              .then_inc(rel_loaded, 16)
            sp.wait_ge(rel_loaded, 32)

        @block.gpsimd
        def _(pool):
            nc.gpsimd.iota(T["iota_i"][:], pattern=[[1, 2 * P]], base=0, channel_multiplier=0).then_inc(consts, 1)
            nc.gpsimd.iota(T["part_i"][:], pattern=[[0, 1]], base=0, channel_multiplier=1).then_inc(consts, 1)

        @block.vector
        def _(v):
            nc.vector.memset(pads[0:1, 0:pad], pad_node).then_inc(pad_set, 1)
            nc.vector.memset(pads[0:1, pad:pad + 1], -1).then_inc(pad_set, 1)
            nc.vector.memset(zero_pads[:], 0).then_inc(pad_set, 1)
            done = [0]

            def link(instruction):
                done[0] += 1
                instruction.then_inc(chain, 1)
                v.wait_ge(chain, done[0])

            v.wait_ge(consts, 2)
            link(nc.vector.memset(T["ones"][:], 1.0))
            link(nc.vector.tensor_copy(T["iota"][:], T["iota_i"][:]))
            link(nc.vector.tensor_copy(T["part"][:], T["part_i"][:]))
            link(nc.vector.tensor_scalar(T["ident"][:], T["iota"][:, 0:P], T["part"][:, 0:1], None, ALU.is_equal))
            link(nc.vector.tensor_scalar(tri[:], T["iota"][:, 0:P], T["part"][:, 0:1], None, ALU.is_gt))
            link(nc.vector.memset(keep[:], 1.0))
            link(nc.vector.memset(keep[:, :, 0:1], 0.0))
            v.wait_ge(loaded, 16)
            nc.vector.tensor_copy(rows[:], rows_i[:]).then_inc(rows_free, 1)
            v.wait_ge(loaded, 32)
            nc.vector.tensor_copy(prev[:], rows_i[:]).then_inc(rows_free, 1)
            v.wait_ge(rows_free, 2)
            link(nc.vector.tensor_tensor(starts[:], rows[:], prev[:], ALU.not_equal))
            link(nc.vector.tensor_scalar_mul(masks[:, :, 0, :], starts[:], -BIG))
            for b in range(B):
                for m, at in ((1, 0), (2, P - 1)):
                    link(nc.vector.tensor_scalar(masks[:, b, m, :], rows[:, b, :], rows[:, b, at:at + 1], -BIG,
                                                 ALU.not_equal, ALU.mult))
            link(nc.vector.tensor_copy(bounds[:, :, 0], masks[:, :, 0, 0]))
            nc.vector.tensor_copy(bounds[:, :, 1], masks[:, :, 1, P - 1]).then_inc(tables_ready, 1)
            link(nc.vector.tensor_tensor_scan(ranks[:].rearrange("q b i -> q (b i)"),
                                              keep[:].rearrange("q b i -> q (b i)"),
                                              starts[:].rearrange("q b i -> q (b i)"), 0.0, ALU.mult, ALU.add))
            nc.vector.tensor_copy(tot[:], ranks[:, :, P - 1]).then_inc(tot_ready, 1)
            v.wait_ge(pre_ready, 1)
            s = lambda n: small[:, n, :]
            link(nc.vector.tensor_copy(s(0), ps[:, 1, 0:B]))
            link(nc.vector.tensor_tensor_scan(s(1), T["ones"][:, 0:B], s(0), 0.0, ALU.mult, ALU.add))
            link(nc.vector.tensor_tensor(s(2), s(1), s(0), ALU.subtract))
            link(nc.vector.tensor_tensor(s(3), ps[:, 0, 0:B], s(2), ALU.add))
            link(nc.vector.scalar_tensor_tensor(out=s(4), in0=s(3), scalar=-1.0, in1=starts[:, :, 0],
                                                op0=ALU.add, op1=ALU.add))
            link(nc.vector.tensor_copy(small_i[:, 0, :], s(4)))
            link(nc.vector.tensor_scalar(small_i[:, 1, :], small_i[:, 0, :], 7, None, ALU.arith_shift_right))
            link(nc.vector.tensor_copy(s(5), small_i[:, 1, :]))
            link(nc.vector.scalar_tensor_tensor(out=s(6), in0=s(5), scalar=-float(P), in1=s(4),
                                                op0=ALU.mult, op1=ALU.add))
            link(nc.vector.tensor_scalar_mul(s(7), s(5), float(z.row)))
            nc.vector.tensor_tensor(s(8), s(6), starts[:, :, 0], ALU.subtract).then_inc(rel_ready, 1)
            v.wait_ge(rel_ready, 1)
            for b in range(B):
                link(nc.vector.tensor_scalar_add(ranks[:, b, :], ranks[:, b, :], small[:, 8, b:b + 1]))
            v.wait_ge(loaded, 48)
            nc.vector.tensor_copy(prev[:], rows_i[:]).then_inc(src_rows_ready, 1)
            v.wait_ge(transposed, 1)
            nc.vector.tensor_copy(offs_i[:], ps[0:B, 0, 0:P]).then_inc(rels_ready, 1)
            nc.vector.tensor_copy(rels[:], ps[0:B, 1, 0:P]).then_inc(rels_ready, 1)
            for b in range(B):
                for n in range(3):
                    k = 3 * b + n
                    v.wait_ge(transposed, k + 2)
                    got = ps[:, k % 2, 0:P]
                    w = min(P, z.tiles - b * P)
                    if n == 0:
                        nc.vector.tensor_scalar_mul(T["neg_pos"][:, b * P:b * P + w], got[:, 0:w], -1.0)\
                          .then_inc(evacuated, 1)
                    elif n == 1:
                        nc.vector.tensor_copy(T["src"][:, b * P:b * P + w], got[:, 0:w]).then_inc(evacuated, 1)
                    else:
                        nc.vector.tensor_copy(tiles_i[:, 0, b * P:(b + 1) * P], got).then_inc(evacuated, 1)
            v.wait_ge(evacuated, 3 * B)
            node = T["node"][:].rearrange("p (t two) -> p two t", two=2)
            link(nc.vector.tensor_scalar(tiles_i[:, 1, :], tiles_i[:, 0, :], 7, None, ALU.arith_shift_right))
            link(nc.vector.tensor_copy(node[:, 0, :], tiles_i[:, 1, 0:z.tiles]))
            link(nc.vector.tensor_scalar(tiles_i[:, 1, :], tiles_i[:, 0, :], P - 1, None, ALU.bitwise_and))
            link(nc.vector.tensor_copy(node[:, 1, :], tiles_i[:, 1, 0:z.tiles]))
            v.wait_ge(rel_loaded, 32)
            first = rel_all.rearrange("p (c g) -> p c g", g=CHUNK_TILES)[:, 0:z.chunks, 0]
            link(nc.vector.tensor_scalar(T["first_rank"][:], first, T["part"][:, 0:1], None, ALU.is_equal))
            link(nc.vector.tensor_scalar(T["other_rank"][:], first, T["part"][:, 0:1], None, ALU.not_equal))

        @block.tensor
        def _(pe):
            pe.wait_ge(tot_ready, 1)
            nc.tensor.matmul(ps[:, 0, 0:B], tri[:], tot[:], start=True, stop=True)
            nc.tensor.matmul(ps[:, 1, 0:B], T["ones"][:, 0:P], tot[:], start=True, stop=True).then_inc(pre_ready, 1)
            pe.wait_ge(rel_ready, 1)
            nc.tensor.transpose(ps[0:B, 0, 0:P], small[:, 7, :], T["ident"][:])
            nc.tensor.transpose(ps[0:B, 1, 0:P], small[:, 6, :], T["ident"][:]).then_inc(transposed, 1)
            pe.wait_ge(src_rows_ready, 1)
            for b in range(B):
                for n, table in enumerate((ranks, prev, rows)):
                    k = 3 * b + n
                    if k < 2:
                        pe.wait_ge(rels_ready, 2)
                    else:
                        pe.wait_ge(evacuated, k - 1)
                    nc.tensor.transpose(ps[:, k % 2, 0:P], table[:, b, :], T["ident"][:]).then_inc(transposed, 1)


def weights(nc, z, Wn, bn, We, be, attn, T):
    K = z.k1
    with ExitStack() as ctx:
        sb = lambda name, shape, dt=F32: ctx.enter_context(nc.sbuf_tensor(name, shape, dt))
        sem = z.semaphore
        wn = sb("wn", [P, K, z.dim])
        we = sb("we", [P, K, z.edge_dim])
        at = sb("attn_col", [P, K])
        at_wide = sb("attn_wide", [P, K, P])
        bnc, bec = sb("bn_col", [P, K]), sb("be_col", [P, K])
        bias_sum = sb("bias_sum", [P, K])
        ps = [ctx.enter_context(nc.psum_tensor(f"weight_ps{i}", [P, 512], F32)) for i in range(6)]
        loaded, ready, turned, chain = sem("weights_loaded"), sem("wide_ready"), sem("weights_turned"), sem("weight_chain")
        block = ctx.enter_context(nc.Block())

        @block.sync
        def _(sp):
            sp.dma_start(wn[:], Wn.rearrange("(k p) n -> p k n", p=P)).then_inc(loaded, 16)
            sp.dma_start(we[:], We.rearrange("(k p) n -> p k n", p=P)).then_inc(loaded, 16)
            with nc.allow_non_contiguous_dma(reason="three columns of 256 elements"):
                sp.dma_start(at[:], attn[0, 0, :].rearrange("(k p) -> p k", p=P)).then_inc(loaded, 16)
                sp.dma_start(bnc[:], bn.rearrange("(k p) -> p k", p=P)).then_inc(loaded, 16)
                sp.dma_start(bec[:], be.rearrange("(k p) -> p k", p=P)).then_inc(loaded, 16)
            sp.dma_start(T["bias"][:, 0:z.dim], bn.rearrange("(a n) -> a n", a=1).to_broadcast([P, z.dim])).then_inc(loaded, 16)

        @block.vector
        def _(v):
            done = [0]

            def link(instruction):
                done[0] += 1
                instruction.then_inc(chain, 1)
                v.wait_ge(chain, done[0])

            v.wait_ge(loaded, 96)
            for k in range(K):
                nc.vector.tensor_scalar_mul(at_wide[:, k, :], T["ones"][:, 0:P], at[:, k:k + 1]).then_inc(ready, 1)
            nc.vector.tensor_tensor(bias_sum[:], bnc[:], bec[:], ALU.add).then_inc(ready, 1)
            nc.vector.memset(T["wn"][:, :, z.dim:z.dim + 1], 0.0)
            nc.vector.memset(T["bias"][:, z.dim:z.dim + 1], 1.0)
            nc.vector.memset(T["eps"][:], EPS)
            v.wait_ge(turned, 1)
            for k in range(K):
                nc.vector.tensor_copy(T["wn"][:, k, 0:z.dim], ps[k][:, 0:z.dim])
                nc.vector.tensor_copy(T["wn"][:, k, z.dim + 1:z.dim + 2], ps[2 + k][:, 0:1])
            nc.vector.tensor_copy(T["we"][:], ps[4][:, 0:z.edge_dim])
            nc.vector.tensor_copy(T["bias"][:, z.dim + 1:z.dim + 2], ps[5][:, 0:1])

        @block.tensor
        def _(pe):
            pe.wait_ge(ready, K + 1)
            for k in range(K):
                for n in range(K):
                    nc.tensor.transpose(ps[k][:, n * P:(n + 1) * P], wn[:, n, k * P:(k + 1) * P], T["ident"][:])
                for n in range(K):
                    nc.tensor.matmul(ps[2 + k][:, 0:1], wn[:, n, k * P:(k + 1) * P], at[:, n:n + 1],
                                     start=(n == 0), stop=(n == K - 1))
            for n in range(K):
                nc.tensor.matmul(ps[4][:, 0:z.edge_dim], at_wide[:, n, :], we[:, n, :], start=(n == 0), stop=(n == K - 1))
            for n in range(K):
                last = nc.tensor.matmul(ps[5][:, 0:1], at_wide[:, n, :], bias_sum[:, n:n + 1],
                                        start=(n == 0), stop=(n == K - 1))
            last.then_inc(turned, 1)


def load_rows(sp, z, out, dram, t, last, sem):
    if last:
        sp.dma_start(out[0:z.last_rows], dram[(z.node_tiles - 1) * P:z.nodes, :]).then_inc(sem, 16)
    else:
        sp.dma_start(out, dram[ds(t * P, P), :]).then_inc(sem, 16)


def node_table(nc, z, x, T, D):
    K, W = z.k1, z.gathered
    turns = z.node_tiles // 2
    with ExitStack() as ctx:
        sb = lambda name, shape, dt=F32: ctx.enter_context(nc.sbuf_tensor(name, shape, dt))
        sem = z.semaphore
        pair = lambda name: [sem(f"{name}{i}") for i in range(2)]
        xt = [sb(f"node_x{i}", [P, z.dim]) for i in range(2)]
        stats = [sb(f"node_stats{i}", [P, 6]) for i in range(2)]
        mv = [sb(f"node_mv{i}", [P, 2]) for i in range(2)]
        std = [sb(f"node_std{i}", [P, 1]) for i in range(2)]
        rstd = [sb(f"node_rstd{i}", [P, 1]) for i in range(2)]
        xn = [sb(f"node_xn{i}", [P, z.dim]) for i in range(2)]
        xnT = [sb(f"node_xnT{i}", [P, K, P]) for i in range(2)]
        row = [sb(f"node_row{i}", [P, W]) for i in range(2)]
        zeros = sb("zeros", [P, 8, z.dim])
        psT = [ctx.enter_context(nc.psum_tensor(f"node_psT{i}", [P, K, P], F32)) for i in range(2)]
        psH = [ctx.enter_context(nc.psum_tensor(f"node_psH{i}", [P, 512], F32)) for i in range(2)]
        x_loaded, row_saved = pair("x_loaded"), pair("row_saved")
        (stats_ready, mv_ready, std_ready, rstd_ready, xn_ready, xn_turned, xnT_ready, h_ready,
         row_ready) = map(sem, ("stats_ready", "mv_ready", "std_ready", "rstd_ready", "xn_ready", "xn_turned",
                                 "xnT_ready", "h_ready", "row_ready"))
        zeros_set, zeroed = sem("zeros_set"), sem("zeroed")
        block = ctx.enter_context(nc.Block())

        @block.sync
        def _(sp):
            def load(i, n, last=False):
                load_rows(sp, z, xt[i][:], x, 2 * n + i, last, x_loaded[i])

            load(0, 0)
            load(1, 0)
            with sp.Fori(1, turns - 1) as n:
                for i in range(2):
                    sp.wait_ge(xn_ready, 2 * n + i - 1)
                    load(i, n)
            sp.wait_ge(xn_ready, 2 * turns - 3)
            load(0, turns - 1)
            sp.wait_ge(xn_ready, 2 * turns - 2)
            load(1, turns - 1, last=True)

        @block.gpsimd
        def _(pool):
            nc.gpsimd.memset(zeros[:], 0.0).then_inc(zeros_set, 1)
            pool.wait_ge(zeros_set, 1)
            total = 0
            for table, n_rows in ((D["gnn"], z.node_tiles * P), (D["buf"], z.experts * z.slots)):
                at = 0
                while at < n_rows:
                    n = min(8, (n_rows - at) // P)
                    pool.dma_start(table[at:at + n * P, :].rearrange("(p k) n -> p k n", k=n), zeros[:, 0:n, :])\
                        .then_inc(zeroed, 16)
                    at += n * P
                    total += 16
            pool.wait_ge(zeroed, total)

        @block.scalar
        def _(act):
            def store(i, n, last=False):
                act.wait_ge(row_ready, 2 * n + i + 1)
                if last:
                    act.dma_start(D["table"][(z.node_tiles - 1) * P:z.nodes, :], row[i][0:z.last_rows, :])\
                       .then_inc(row_saved[i], 16)
                else:
                    act.dma_start(D["table"][ds((2 * n + i) * P, P), :], row[i][:]).then_inc(row_saved[i], 16)

            def tile_std(i, n):
                act.wait_ge(mv_ready, 2 * n + i + 1)
                nc.scalar.activation(std[i][:], mv[i][:, 1:2], ACT.Sqrt, bias=T["eps"][:, 0:1]).then_inc(std_ready, 1)

            def tile_turn(i, n):
                act.wait_ge(xn_turned, 2 * n + i + 1)
                nc.scalar.copy(xnT[i][:], psT[i][:]).then_inc(xnT_ready, 1)

            def turn(n, last=False):
                for i in range(2):
                    tile_std(i, n)
                for i in range(2):
                    tile_turn(i, n)
                for i in range(2):
                    store(i, n, last and i == 1)

            with act.Fori(0, turns - 1) as n:
                turn(n)
            turn(turns - 1, True)
            for i in range(2):
                act.wait_ge(row_saved[i], 16 * turns)

        @block.vector
        def _(v):
            def turn(n, first=False):
                for i in range(2):
                    v.wait_ge(x_loaded[i], 16 * n + 16)
                    nc.vector.bn_stats(stats[i][:], xt[i][:]).then_inc(stats_ready, 1)
                for i in range(2):
                    v.wait_ge(stats_ready, 2 * n + i + 1)
                    v.sem_inc(z.passed, 1)
                    nc.vector.bn_aggr(mv[i][:], stats[i][:]).then_inc(mv_ready, 1)
                for i in range(2):
                    v.wait_ge(std_ready, 2 * n + i + 1)
                    nc.vector.reciprocal(rstd[i][:], std[i][:]).then_inc(rstd_ready, 1)
                for i in range(2):
                    v.wait_ge(rstd_ready, 2 * n + i + 1)
                    if not first:
                        v.wait_ge(xn_turned, 2 * n + i - 1)
                    nc.vector.tensor_scalar(xn[i][:], xt[i][:], mv[i][:, 0:1], rstd[i][:, 0:1],
                                            ALU.subtract, ALU.mult).then_inc(xn_ready, 1)
                for i in range(2):
                    v.wait_ge(h_ready, 2 * n + i + 1)
                    if not first:
                        v.wait_ge(row_saved[i], 16 * n)
                    nc.vector.tensor_tensor(row[i][:], psH[i][:, 0:W], T["bias"][:], ALU.add)\
                             .then_inc(row_ready, 1)

            turn(0, True)
            with v.Fori(1, turns) as n:
                turn(n)

        @block.tensor
        def _(pe):
            def turn(n, first=False):
                for i in range(2):
                    pe.wait_ge(xn_ready, 2 * n + i + 1)
                    if not first:
                        pe.wait_ge(xnT_ready, 2 * n + i - 1)
                    for k in range(K):
                        last = nc.tensor.transpose(psT[i][:, k, :], xn[i][:, k * P:(k + 1) * P], T["ident"][:])
                    last.then_inc(xn_turned, 1)
                for i in range(2):
                    pe.wait_ge(xnT_ready, 2 * n + i + 1)
                    if not first:
                        pe.wait_ge(row_ready, 2 * n + i - 1)
                    for k in range(K):
                        last = nc.tensor.matmul(psH[i][:, 0:W], xnT[i][:, k, :], T["wn"][:, k, :],
                                                start=(k == 0), stop=(k == K - 1))
                    last.then_inc(h_ready, 1)

            turn(0, True)
            with pe.Fori(1, turns) as n:
                turn(n)


def edges(nc, z, edge_attr, T, D, acc):
    C, G, R, W = z.chunks, CHUNK_TILES, z.row, z.gathered
    turns = C // 2
    RING = 4
    H = G // 2
    with ExitStack() as ctx:
        sb = lambda name, shape, dt=F32: ctx.enter_context(nc.sbuf_tensor(name, shape, dt))
        ps = lambda name, shape: ctx.enter_context(nc.psum_tensor(name, shape, F32))
        sem = z.semaphore
        pair = lambda name: [sem(f"{name}{i}") for i in range(2)]
        rows = [sb(f"gathered{i}", [P, G, R]) for i in range(2)]
        idx = [sb(f"chunk_src{i}", [P, G], I32) for i in range(2)]
        ea = [sb(f"edge_rows{i}", [P, G, P]) for i in range(2)]
        dot_out = sb("dot_out", [P, G, P])
        masks = [sb(f"chunk_masks{i}", [G, 3, P]) for i in range(2)]
        bounds = [sb(f"chunk_bounds{i}", [1, 2 * G + 1]) for i in range(2)]
        dots, raw, score = sb("dots", [P, G]), sb("raw_score", [P, G]), sb("score", [P, G])
        fwd, seg = sb("fwd_max", [G, P]), sb("seg_max", [G, P])
        ends_fwd = [sb(f"ends_fwd{i}", [1, 2 * G]) for i in range(2)]
        ends = sb("ends_max", [1, 2 * G])
        cols = sb("end_cols", [G, 2])
        seg_a, seg_b, centred, expd = (sb(n, [G, P]) for n in ("seg_a", "seg_b", "centred", "expd"))
        goes_on, rise, rise_on = sb("goes_on", [1, 1]), sb("rise", [1, 1]), sb("rise_on", [1, 1])
        rescale, factor = sb("rescale", [P, 1]), sb("factor", [P, 1])
        prob = [sb(f"prob{i}", [P, G]) for i in range(2)]
        neg_prob = [sb(f"neg_prob{i}", [P, G]) for i in range(2)]
        dist = sb("dist", [P, 2, 2 * P])
        onehot = sb("onehot", [P, RING, 2, P])
        psA, psE = ps("psA", [G, 512]), ps("psE", [P, 512])
        psX, psY = ps("psX", [1, 512]), ps("psY", [P, 512])
        sums = [ps(f"sums{i}", [P, 2, 512]) for i in range(2)]

        src_staged, gathered = sem("src_staged"), pair("gathered")
        ea_loaded, masks_loaded = pair("ea_loaded"), pair("masks_loaded")
        (dots_ready, raw_ready, score_ready, score_rows, fwd_ready, seg_ready, ends_rows, ends_fwd_ready,
         ends_ready, on_ready, rise_ready, rise_on_ready, cols_ready, cols_copied, seg_a_ready, seg_b_ready,
         centred_ready, exp_ready, exp_cols, prob_ready, neg_ready, rescale_ready, factor_ready, rescaled,
         node_set) = map(sem, (
             "dots_ready", "raw_ready", "score_ready", "score_rows", "fwd_ready", "seg_ready", "ends_rows",
             "ends_fwd_ready", "ends_ready", "on_ready", "rise_ready", "rise_on_ready", "cols_ready",
             "cols_copied", "seg_a_ready", "seg_b_ready", "centred_ready", "exp_ready", "exp_cols", "prob_ready",
             "neg_ready", "rescale_ready", "factor_ready", "rescaled", "node_set"))
        dist_ready, onehot_ready, tile_summed, tile_added = (
            sem("dist_ready"), sem("onehot_ready"), sem("tile_summed"), sem("tile_added"))
        acc_zero, carry_set = sem("acc_zero"), sem("carry_set")
        no_max = sb("no_max", [1, 1])
        block = ctx.enter_context(nc.Block())

        @block.gpsimd
        def _(pool):
            def chunk(i, c, first=False):
                for g in range(G):
                    if g % 4 == 0 and not first:
                        pool.wait_ge(tile_summed, (c - 2) * G + g + 4)
                    if g == 0:
                        nc.gpsimd.tensor_copy(idx[i][:], T["src"][:, ds(c * G, G)]).then_inc(src_staged, 1)
                        pool.wait_ge(src_staged, c + 1)
                    if g % 4 == 0:
                        pool.sem_inc(z.passed, 1)
                    pool.indirect_dma_start(rows[i][:, g, 0:W], None, D["table"][:, :],
                                            bass.IndirectOffsetOnAxis(idx[i][:, g:g + 1], 0)).then_inc(gathered[i], 16)

            for i in range(2):
                chunk(i, i, True)
            with pool.Fori(1, turns) as n:
                for i in range(2):
                    chunk(i, 2 * n + i)

        @block.sync
        def _(sp):
            view = edge_attr[0:z.edges // P * P, :].rearrange("(t p) n -> p t n", p=P)
            masks_v = D["masks"].rearrange("t (m i) -> t m i", m=3)
            flat = D["bounds"].rearrange("t m -> (t m)").rearrange("(a n) -> a n", a=1)

            def chunk(i, c, first=False, last=False):
                if not first:
                    sp.wait_ge(dots_ready, c - 1)
                if last:
                    full = z.edges // P - c * G
                    rest = z.edges % P
                    assert 0 < full < G and rest
                    sp.dma_start(ea[i][:, 0:full, :], view[:, c * G:c * G + full, :]).then_inc(ea_loaded[i], 16)
                    if rest:
                        sp.dma_start(ea[i][0:rest, full, :], edge_attr[z.edges - rest:z.edges, :]).then_inc(ea_loaded[i], 16)
                else:
                    for half in range(2):
                        sp.dma_start(ea[i][:, half * H:half * H + H, :], view[:, ds(c * G + half * H, H), :])\
                          .then_inc(ea_loaded[i], 16)
                if not first:
                    sp.wait_ge(seg_b_ready, c - 1)
                    sp.wait_ge(on_ready, c - 1)
                    sp.wait_ge(ends_ready, c - 1)
                sp.dma_start(masks[i][:], masks_v[ds(c * G, G)]).then_inc(masks_loaded[i], 16)
                sp.dma_start(bounds[i][:], flat[:, ds(c * 2 * G, 2 * G + 1)]).then_inc(masks_loaded[i], 16)

            for i in range(2):
                chunk(i, i, True)
            with sp.Fori(1, turns - 1) as n:
                for i in range(2):
                    chunk(i, 2 * n + i)
            chunk(0, C - 2)
            chunk(1, C - 1, last=True)

        @block.vector
        def _(v):
            def score_steps(i, c, n, first=False, last=False):
                def edge_dots(g0, g1):
                    if g0 == 0:
                        v.wait_ge(ea_loaded[i], 32 * n + 32)
                        if not first:
                            v.wait_ge(raw_ready, c)
                            v.wait_ge(dots_ready, c)
                    for g in range(g0, g1):
                        op = nc.vector.tensor_tensor_reduce(out=dot_out[:, g, :], in0=ea[i][:, g, :], in1=T["we"][:],
                                                            scale=1.0, scalar=0.0, op0=ALU.mult, op1=ALU.add,
                                                            accum_out=dots[:, g:g + 1])
                    if g1 == G:
                        op.then_inc(dots_ready, 1)

                def raw_scores():
                    v.wait_ge(gathered[i], 16 * G * (n + 1))
                    v.wait_ge(dots_ready, c + 1)
                    if not first:
                        v.wait_ge(score_ready, c)
                    nc.vector.tensor_tensor(raw[:], rows[i][:, :, W - 1], dots[:], ALU.add).then_inc(raw_ready, 1)

                def scores():
                    v.wait_ge(raw_ready, c + 1)
                    if not first:
                        v.wait_ge(score_rows, c)
                    nc.vector.scalar_tensor_tensor(out=score[:], in0=raw[:], scalar=SLOPE, in1=raw[:],
                                                   op0=ALU.mult, op1=ALU.max).then_inc(score_ready, 1)

                def node_columns():
                    if not first:
                        v.wait_ge(node_set, c)
                    nc.vector.tensor_copy(rows[i][:, :, W:R], T["node"][:, ds(c * 2 * G, 2 * G)]
                                          .rearrange("p (g two) -> p g two", two=2)).then_inc(node_set, 1)

                def forward():
                    v.wait_ge(score_rows, c + 1)
                    v.wait_ge(masks_loaded[i], 32 * (n + 1))
                    if not first:
                        v.wait_ge(seg_ready, c)
                    nc.vector.tensor_tensor_scan(fwd[:], masks[i][:, 0, :], psA[:, 0:P], -BIG, ALU.add, ALU.max)\
                             .then_inc(fwd_ready, 1)

                def backward():
                    v.wait_ge(fwd_ready, c + 1)
                    if not first:
                        v.wait_ge(seg_a_ready, c)
                    flat = masks[i][:].rearrange("g m i -> g (m i)")
                    nc.vector.tensor_tensor_scan(seg[:, ::-1], flat[:, P:0:-1], fwd[:, ::-1], -BIG, ALU.add, ALU.max)\
                             .then_inc(seg_ready, 1)

                def ends_forward():
                    v.wait_ge(ends_rows, c + 1)
                    if first:
                        v.wait_ge(carry_set, 1)
                    else:
                        v.wait_ge(ends_fwd_ready, c)
                        v.wait_ge(rise_ready, c)
                    carry = no_max[:, 0:1] if first else ends_fwd[1 - i][:, 2 * G - 1:2 * G]
                    nc.vector.tensor_tensor_scan(ends_fwd[i][:], bounds[i][:, 0:2 * G], psX[:, 0:2 * G], carry,
                                                 ALU.add, ALU.max).then_inc(ends_fwd_ready, 1)

                def ends_backward():
                    v.wait_ge(ends_fwd_ready, c + 1)
                    if not first:
                        v.wait_ge(cols_ready, c)
                        v.wait_ge(rise_ready, c)
                    nc.vector.tensor_tensor_scan(ends[:, ::-1], bounds[i][:, 2 * G:0:-1], ends_fwd[i][:, ::-1], -BIG,
                                                 ALU.add, ALU.max).then_inc(ends_ready, 1)

                def open_segment():
                    if not first:
                        v.wait_ge(rise_on_ready, c)
                    nc.vector.tensor_scalar(goes_on[:], bounds[i][:, 0:1], 0.0, None, ALU.is_equal).then_inc(on_ready, 1)
                    v.wait_ge(ends_ready, c + 1)
                    carry = no_max[:, 0:1] if first else ends_fwd[1 - i][:, 2 * G - 1:2 * G]
                    nc.vector.tensor_tensor(rise[:], carry, ends[:, 0:1], ALU.subtract).then_inc(rise_ready, 1)

                def open_rise():
                    v.wait_ge(rise_ready, c + 1)
                    v.wait_ge(on_ready, c + 1)
                    if not first:
                        v.wait_ge(cols_ready, c)
                    nc.vector.tensor_tensor(rise_on[:], rise[:], goes_on[:], ALU.mult).then_inc(rise_on_ready, 1)

                def end_columns():
                    v.wait_ge(cols_ready, c + 1)
                    if not first:
                        v.wait_ge(seg_b_ready, c)
                    nc.vector.tensor_copy(cols[:], psY[0:G, 0:2]).then_inc(cols_copied, 1)

                def first_segments():
                    v.wait_ge(cols_copied, c + 1)
                    v.wait_ge(seg_ready, c + 1)
                    if not first:
                        v.wait_ge(seg_b_ready, c)
                    nc.vector.scalar_tensor_tensor(out=seg_a[:], in0=masks[i][:, 1, :], scalar=cols[:, 0:1], in1=seg[:],
                                                   op0=ALU.add, op1=ALU.max).then_inc(seg_a_ready, 1)

                def last_segments():
                    v.wait_ge(seg_a_ready, c + 1)
                    if not first:
                        v.wait_ge(centred_ready, c)
                    nc.vector.scalar_tensor_tensor(out=seg_b[:], in0=masks[i][:, 2, :], scalar=cols[:, 1:2], in1=seg_a[:],
                                                   op0=ALU.add, op1=ALU.max).then_inc(seg_b_ready, 1)

                def centre():
                    v.wait_ge(seg_b_ready, c + 1)
                    if not first:
                        v.wait_ge(exp_ready, c)
                    nc.vector.tensor_tensor(centred[:], psA[:, 0:P], seg_b[:], ALU.subtract).then_inc(centred_ready, 1)

                return [lambda: edge_dots(0, 3), lambda: edge_dots(3, 6), lambda: edge_dots(6, 9),
                        lambda: edge_dots(9, 12), lambda: edge_dots(12, 14), lambda: edge_dots(14, G),
                        raw_scores, lambda: (scores(), node_columns()), forward, backward, ends_forward,
                        ends_backward, lambda: (open_segment(), open_rise()),
                        lambda: (end_columns(), first_segments()), last_segments, centre]

            def rescale_open(i, c, first=False):
                v.wait_ge(rescale_ready, c + 1)
                if not first:
                    v.wait_ge(rescaled, c)
                nc.vector.scalar_tensor_tensor(out=factor[:], in0=T["first_rank"][:, ds(c, 1)], scalar=rescale[:, 0:1],
                                               in1=T["other_rank"][:, ds(c, 1)], op0=ALU.mult, op1=ALU.add)\
                         .then_inc(factor_ready, 1)
                v.wait_ge(factor_ready, c + 1)

            def tiles(i, c, offs, steps, first=False):
                rescale_open(i, c, first)
                if first:
                    v.wait_ge(acc_zero, 2)
                else:
                    v.wait_ge(tile_added, c * G)
                nc.vector.tensor_scalar(acc[:, ds(offs[0], R)], acc[:, ds(offs[0], R)], factor[:, 0:1], None, ALU.mult)\
                         .then_inc(rescaled, 1)
                for g in range(G):
                    if g == 0:
                        v.wait_ge(rescaled, c + 1)
                    else:
                        v.wait_ge(tile_added, c * G + g)
                    v.wait_ge(tile_summed, c * G + g + 1)
                    at = acc[:, ds(offs[g], 2 * R)].rearrange("p (h r) -> p h r", h=2)
                    nc.vector.tensor_tensor(at, sums[g % 2][:, :, 0:R], at, ALU.add).then_inc(tile_added, 1)
                    if steps:
                        steps[g]()

            nc.vector.memset(no_max[:], -BIG).then_inc(carry_set, 1)
            half = acc.shape[1] // 2
            nc.vector.memset(acc[:, 0:half], 0.0).then_inc(acc_zero, 1)
            nc.vector.memset(acc[:, half:], 0.0).then_inc(acc_zero, 1)
            limit = (z.node_tiles - 1) * R
            regs = [v.alloc_register(f"offset_{g}") for g in range(G)]

            def load(c):
                v.load(regs, T["offs"][0:1, ds(c * G, G)])
                return [v.snap(r, min_val=0, max_val=limit) for r in regs]

            for step in score_steps(0, 0, 0, first=True):
                step()
            tiles(0, 0, load(0), score_steps(1, 1, 0), first=True)
            tiles(1, 1, load(1), score_steps(0, 2, 1))
            with v.Fori(1, turns - 1) as n:
                tiles(0, 2 * n, load(2 * n), score_steps(1, 2 * n + 1, n))
                tiles(1, 2 * n + 1, load(2 * n + 1), score_steps(0, 2 * n + 2, n + 1))
            tiles(0, C - 2, load(C - 2), score_steps(1, C - 1, turns - 1, last=True))
            tiles(1, C - 1, load(C - 1), None)

        @block.scalar
        def _(act):
            def exps(i, c, first=False):
                act.wait_ge(centred_ready, c + 1)
                if not first:
                    act.wait_ge(exp_cols, c)
                nc.scalar.activation(expd[:], centred[:], ACT.Exp).then_inc(exp_ready, 1)
                act.wait_ge(cols_ready, c + 1)
                if not first:
                    act.wait_ge(factor_ready, c)
                nc.scalar.activation(rescale[:], psY[:, 2:3], ACT.Exp).then_inc(rescale_ready, 1)

            def probs(i, c, first=False):
                act.wait_ge(exp_cols, c + 1)
                if not first:
                    act.wait_ge(onehot_ready, (c - 1) * G)
                nc.scalar.activation(prob[i][:], psE[:, 0:G], ACT.Copy).then_inc(prob_ready, 1)
                nc.scalar.activation(neg_prob[i][:], psE[:, 0:G], ACT.Copy, scale=-1.0).then_inc(neg_ready, 1)

            def distance(c, g, k, first=False):
                if not first:
                    act.wait_ge(onehot_ready, c * G + g - 1)
                nc.scalar.activation(dist[:, k % 2, :], T["iota"][:], ACT.Abs, bias=T["neg_pos"][:, ds(c * G + g, 1)])\
                         .then_inc(dist_ready, 1)

            def tile(i, c, g, first=False):
                act.wait_ge(dist_ready, c * G + g + 1)
                if g == 0:
                    act.wait_ge(prob_ready, c + 1)
                    act.wait_ge(neg_ready, c + 1)
                if not first:
                    act.wait_ge(tile_summed, c * G + g - RING + 1)
                nc.scalar.activation(onehot[:, g % RING, :, :].rearrange("p h r -> p (h r)"), dist[:, g % 2, :], ACT.Relu,
                                     scale=neg_prob[i][:, g:g + 1], bias=prob[i][:, g:g + 1]).then_inc(onehot_ready, 1)

            def chunk(i, c, first=False, last=False):
                for g in range(G):
                    if g + 1 < G:
                        distance(c, g + 1, g + 1, first and g + 1 < 2)
                    elif not last:
                        distance(c + 1, 0, 0)
                    tile(i, c, g, first and g < RING)
                if not last:
                    exps(1 - i, c + 1)
                    probs(1 - i, c + 1, first)

            exps(0, 0, True)
            probs(0, 0, True)
            distance(0, 0, 0, True)
            chunk(0, 0, first=True)
            chunk(1, 1)
            with act.Fori(1, turns - 1) as n:
                chunk(0, 2 * n)
                chunk(1, 2 * n + 1)
            chunk(0, C - 2)
            chunk(1, C - 1, last=True)

        @block.tensor
        def _(pe):
            def turn_scores(c, first=False):
                pe.wait_ge(score_ready, c + 1)
                if not first:
                    pe.wait_ge(centred_ready, c)
                nc.tensor.transpose(psA[:, 0:P], score[:], T["ident"][:]).then_inc(score_rows, 1)

            def turn_ends(c, first=False):
                pe.wait_ge(seg_ready, c + 1)
                if not first:
                    pe.wait_ge(ends_fwd_ready, c)
                pe.sem_inc(z.passed, 1)
                nc.tensor.transpose(psX[:, 0:2 * G:2], seg[:, 0:1], T["ident"][0:G, 0:G])
                nc.tensor.transpose(psX[:, 1:2 * G:2], seg[:, P - 1:P], T["ident"][0:G, 0:G]).then_inc(ends_rows, 1)

            def turn_back(c, first=False):
                pe.wait_ge(ends_ready, c + 1)
                pe.wait_ge(rise_on_ready, c + 1)
                if not first:
                    pe.wait_ge(cols_copied, c)
                    pe.wait_ge(rescale_ready, c)
                pe.sem_inc(z.passed, 1)
                for n in range(2):
                    nc.tensor.transpose(psY[0:G, n:n + 1], ends[:, n:2 * G:2], T["ident"][0:1, 0:1])
                nc.tensor.matmul(psY[:, 2:3], T["ones"][0:1, 0:P], rise_on[:], start=True, stop=True)\
                         .then_inc(cols_ready, 1)

            def turn_exps(c, first=False):
                pe.wait_ge(exp_ready, c + 1)
                if not first:
                    pe.wait_ge(prob_ready, c)
                    pe.wait_ge(neg_ready, c)
                pe.sem_inc(z.passed, 1)
                nc.tensor.transpose(psE[:, 0:G], expd[:], T["ident"][0:G, 0:G]).then_inc(exp_cols, 1)

            def tile(i, c, g, first=False):
                pe.wait_ge(onehot_ready, c * G + g + 1)
                if g == 0:
                    pe.wait_ge(node_set, c + 1)
                if not first:
                    pe.wait_ge(tile_added, c * G + g - 1)
                for h in range(2):
                    last = nc.tensor.matmul(sums[g % 2][:, h, 0:R], onehot[:, g % RING, h, :], rows[i][:, g, :],
                                            start=True, stop=True)
                last.then_inc(tile_summed, 1)

            def chunk(i, c, first=False, last=False):
                for g in range(G):
                    tile(i, c, g, first and g < 2)
                    if not last and g == 8:
                        turn_scores(c + 1)
                    if not last and g == 10:
                        turn_ends(c + 1)
                    if not last and g == 13:
                        turn_back(c + 1)
                if not last:
                    turn_exps(c + 1)

            turn_scores(0, True)
            turn_ends(0, True)
            turn_back(0, True)
            turn_exps(0, True)
            chunk(0, 0, first=True)
            chunk(1, 1)
            with pe.Fori(1, turns - 1) as n:
                chunk(0, 2 * n)
                chunk(1, 2 * n + 1)
            chunk(0, C - 2)
            chunk(1, C - 1, last=True)


def scatter_sums(nc, z, T, D, acc):
    NT, U, R = z.node_tiles, z.turn, z.row
    with ExitStack() as ctx:
        sb = lambda name, shape, dt=F32: ctx.enter_context(nc.sbuf_tensor(name, shape, dt))
        sem = z.semaphore
        den, inv, empty = sb("den", [P, NT]), sb("inv", [P, NT]), sb("empty", [P, NT])
        part = sb("node_part", [P, 2, NT])
        part_i = sb("node_part_i", [P, 2, NT], I32)
        part_f = sb("node_part_f", [P, 2, NT])
        node_f, node_i = sb("node_f", [P, NT]), sb("node_i", [P, NT], I32)
        out = [sb(f"gnn_row{u}", [P, z.dim]) for u in range(U)]
        idx = [sb(f"gnn_idx{u}", [P, 1], I32) for u in range(U)]
        chain, nodes_ready = sem("node_chain"), sem("nodes_ready")
        row_ready, idx_ready = sem("gnn_row_ready"), sem("gnn_idx_ready")
        sent = [sem(f"gnn_sent{u}") for u in range(U)]
        block = ctx.enter_context(nc.Block())
        col = lambda n: acc[:, 0:NT * R].rearrange("p (t r) -> p r t", r=R)[:, n, :]

        @block.vector
        def _(v):
            done = [0]

            def link(instruction):
                done[0] += 1
                instruction.then_inc(chain, 1)
                v.wait_ge(chain, done[0])

            link(nc.vector.tensor_scalar_add(den[:], col(z.dim), 1e-16))
            link(nc.vector.reciprocal(inv[:], den[:]))
            for n in range(2):
                link(nc.vector.tensor_tensor(part[:, n, :], col(z.dim + 2 + n), inv[:], ALU.mult))
            link(nc.vector.tensor_scalar_add(part_f[:], part[:], 0.25))
            link(nc.vector.tensor_copy(part_i[:], part_f[:]))
            link(nc.vector.tensor_copy(part[:], part_i[:]))
            link(nc.vector.tensor_scalar(empty[:], col(z.dim), 0.5, 1e6, ALU.is_lt, ALU.mult))
            link(nc.vector.scalar_tensor_tensor(out=node_f[:], in0=part[:, 0, :], scalar=float(P), in1=part[:, 1, :],
                                                op0=ALU.mult, op1=ALU.add))
            link(nc.vector.tensor_tensor(den[:], node_f[:], empty[:], ALU.add))
            nc.vector.tensor_copy(node_i[:], den[:]).then_inc(nodes_ready, 1)

        @block.scalar
        def _(act):
            def turn(n, first=False):
                for u in range(U):
                    if not first:
                        act.wait_ge(sent[u], 16 * n)
                    nc.scalar.activation(out[u][:], acc[:, ds((n * U + u) * R, z.dim)], ACT.Relu,
                                         scale=inv[:, ds(n * U + u, 1)]).then_inc(row_ready, 1)

            act.wait_ge(nodes_ready, 1)
            turn(0, True)
            if NT // U > 1:
                with act.Fori(1, NT // U) as n:
                    turn(n)

        @block.gpsimd
        def _(pool):
            def turn(n, first=False):
                for u in range(U):
                    if not first:
                        pool.wait_ge(sent[u], 16 * n)
                    nc.gpsimd.tensor_copy(idx[u][:], node_i[:, ds(n * U + u, 1)]).then_inc(idx_ready, 1)
                    pool.wait_ge(idx_ready, n * U + u + 1)
                    pool.wait_ge(row_ready, n * U + u + 1)
                    pool.sem_inc(z.passed, 1)
                    pool.indirect_dma_start(D["gnn"][:, :], bass.IndirectOffsetOnAxis(idx[u][:, 0:1], 0), out[u][:], None,
                                            bounds_check=NT * P - 1, oob_is_err=False).then_inc(sent[u], 16)

            pool.wait_ge(nodes_ready, 1)
            turn(0, True)
            if NT // U > 1:
                with pool.Fori(1, NT // U) as n:
                    turn(n)
            for u in range(U):
                pool.wait_ge(sent[u], 16 * (NT // U))


def gate(nc, z, x, gate_w, gate_b, T, D, x1):
    NT, E, K = z.node_tiles, z.experts, z.k1
    turns = NT // 2
    with ExitStack() as ctx:
        sb = lambda name, shape, dt=F32: ctx.enter_context(nc.sbuf_tensor(name, shape, dt))
        sem = z.semaphore
        pair = lambda name: [sem(f"{name}{i}") for i in range(2)]
        xt = [sb(f"gate_x{i}", [P, z.dim]) for i in range(2)]
        gt = [sb(f"gate_gnn{i}", [P, z.dim]) for i in range(2)]
        stats = [sb(f"gate_stats{i}", [P, 6]) for i in range(2)]
        mv = [sb(f"gate_mv{i}", [P, 2]) for i in range(2)]
        std = [sb(f"gate_std{i}", [P, 1]) for i in range(2)]
        xn = [sb(f"gate_xn{i}", [P, z.dim]) for i in range(2)]
        xnT = [sb(f"gate_xnT{i}", [P, K, P]) for i in range(2)]
        gw, gb = sb("gate_weights", [P, K, E]), sb("gate_bias", [P, E])
        logits = sb("logits", [P, NT, E])
        psT = [ctx.enter_context(nc.psum_tensor(f"gate_psT{i}", [P, K, P], F32)) for i in range(2)]
        psL = [ctx.enter_context(nc.psum_tensor(f"gate_psL{i}", [P, 512], F32)) for i in range(2)]
        psR = ctx.enter_context(nc.psum_tensor("route_ps", [P, 4, 512], F32))
        w_loaded, loaded = sem("gate_w_loaded"), pair("gate_loaded")
        (x1_ready, stats_ready, mv_ready, std_ready, rstd_ready, xn_ready, xn_turned, xnT_ready, l_ready,
         logit_ready) = map(sem, ("g_x1_ready", "g_stats_ready", "g_mv_ready", "g_std_ready", "g_rstd_ready",
                                   "g_xn_ready", "g_xn_turned", "g_xnT_ready", "g_l_ready", "g_logit_ready"))
        chain, shifted, exped, hot_ready, counted, tri_ready = (
            sem("route_chain"), sem("logits_shifted"), sem("logits_exp"), sem("hot_ready"), sem("counted"), sem("tri_ready"))
        tri = sb("tri_incl", [P, P])
        best, total, first_e = sb("best", [P, NT]), sb("total", [P, NT]), sb("first_e", [P, NT])
        w_a, w_b, w_c = sb("route_a", [P, NT, E]), sb("route_b", [P, NT, E]), sb("route_c", [P, NT, E])
        expert_no = sb("expert_no", [P, NT, E])
        hot = sb("hot", [P, E, NT])
        keep = sb("route_keep", [P, E, NT])
        before, after = sb("before", [P, E, NT]), sb("after", [P, E, NT])
        place, kept, slot_f = sb("place", [P, NT]), sb("kept", [P, NT]), sb("slot_f", [P, NT])
        block = ctx.enter_context(nc.Block())

        @block.sync
        def _(sp):
            sp.dma_start(gw[:], gate_w.rearrange("(k p) e -> p k e", p=P)).then_inc(w_loaded, 16)
            sp.dma_start(gb[:], gate_b.rearrange("(a e) -> a e", a=1).to_broadcast([P, E])).then_inc(w_loaded, 16)

            def load(i, n, last=False):
                load_rows(sp, z, xt[i][:], x, 2 * n + i, last, loaded[i])
                load_rows(sp, z, gt[i][:], D["gnn"], 2 * n + i, last, loaded[i])

            load(0, 0)
            load(1, 0)
            with sp.Fori(1, turns - 1) as n:
                for i in range(2):
                    sp.wait_ge(x1_ready, 2 * n + i - 1)
                    load(i, n)
            for i in range(2):
                sp.wait_ge(x1_ready, 2 * turns + i - 3)
                load(i, turns - 1, last=(i == 1))

        @block.scalar
        def _(act):
            with act.Fori(0, turns) as n:
                for i in range(2):
                    act.wait_ge(mv_ready, 2 * n + i + 1)
                    nc.scalar.activation(std[i][:], mv[i][:, 1:2], ACT.Sqrt, bias=T["eps"][:, 0:1]).then_inc(std_ready, 1)
                for i in range(2):
                    act.wait_ge(xn_turned, 2 * n + i + 1)
                    nc.scalar.copy(xnT[i][:], psT[i][:]).then_inc(xnT_ready, 1)
            act.wait_ge(shifted, 1)
            nc.scalar.activation(w_b[:], w_a[:], ACT.Exp).then_inc(exped, 1)

        @block.vector
        def _(v):
            def turn(n, first=False):
                t = lambda i: 2 * n + i
                for i in range(2):
                    v.wait_ge(loaded[i], 32 * n + 32)
                    nc.vector.tensor_tensor(x1[:, ds(t(i) * z.dim, z.dim)], xt[i][:], gt[i][:], ALU.add)\
                             .then_inc(x1_ready, 1)
                for i in range(2):
                    v.wait_ge(x1_ready, 2 * n + i + 1)
                    v.sem_inc(z.passed, 1)
                    nc.vector.bn_stats(stats[i][:], x1[:, ds(t(i) * z.dim, z.dim)]).then_inc(stats_ready, 1)
                for i in range(2):
                    v.wait_ge(stats_ready, 2 * n + i + 1)
                    v.sem_inc(z.passed, 1)
                    nc.vector.bn_aggr(mv[i][:], stats[i][:]).then_inc(mv_ready, 1)
                for i in range(2):
                    v.wait_ge(std_ready, 2 * n + i + 1)
                    nc.vector.reciprocal(T["rstd"][:, ds(t(i), 1)], std[i][:]).then_inc(rstd_ready, 1)
                    nc.vector.tensor_copy(T["mean"][:, ds(t(i), 1)], mv[i][:, 0:1])
                for i in range(2):
                    v.wait_ge(rstd_ready, 2 * n + i + 1)
                    if not first:
                        v.wait_ge(xn_turned, 2 * n + i - 1)
                    nc.vector.tensor_scalar(xn[i][:], x1[:, ds(t(i) * z.dim, z.dim)], mv[i][:, 0:1],
                                            T["rstd"][:, ds(t(i), 1)], ALU.subtract, ALU.mult).then_inc(xn_ready, 1)
                for i in range(2):
                    v.wait_ge(l_ready, 2 * n + i + 1)
                    v.wait_ge(xn_ready, 2 * n + i + 1)
                    nc.vector.tensor_tensor(logits[:, ds(t(i), 1), :].rearrange("p t e -> p (t e)"), psL[i][:, 0:E], gb[:],
                                            ALU.add).then_inc(logit_ready, 1)

            v.wait_ge(w_loaded, 32)
            turn(0, True)
            with v.Fori(1, turns) as n:
                turn(n)
            for i in range(2):
                v.wait_ge(logit_ready, 2 * turns)
            done = [0]

            def link(instruction):
                done[0] += 1
                instruction.then_inc(chain, 1)
                v.wait_ge(chain, done[0])

            wide = lambda t: t[:].unsqueeze(2).to_broadcast([P, NT, E])
            link(nc.vector.tensor_scalar(tri[:], T["iota"][:, 0:P], T["part"][:, 0:1], None, ALU.is_ge))
            link(nc.vector.memset(keep[:], 1.0))
            link(nc.vector.memset(keep[:, :, 0:1], 0.0))
            for e in range(E):
                nc.vector.memset(expert_no[:, :, e:e + 1], float(e))
            link(nc.vector.tensor_reduce(best[:], logits[:], AX.X, ALU.max))
            nc.vector.tensor_tensor(w_a[:], logits[:], wide(best), ALU.subtract).then_inc(shifted, 1)
            v.wait_ge(exped, 1)
            link(nc.vector.tensor_reduce(total[:], w_b[:], AX.X, ALU.add))
            link(nc.vector.reciprocal(T["weight"][:], total[:]))
            link(nc.vector.tensor_scalar(w_b[:], w_a[:], 0.0, float(E), ALU.not_equal, ALU.mult))
            link(nc.vector.tensor_tensor(w_c[:], w_b[:], expert_no[:], ALU.add))
            link(nc.vector.tensor_reduce(first_e[:], w_c[:], AX.X, ALU.min))
            link(nc.vector.tensor_tensor(hot[:].rearrange("p e t -> p t e"), expert_no[:], wide(first_e), ALU.is_equal))
            nc.vector.memset(place[:], 0.0).then_inc(hot_ready, 1)
            v.wait_ge(counted, 1)
            h = E // 2
            for n in range(2):
                link(nc.vector.tensor_copy(before[:, n * h:(n + 1) * h, :],
                                           psR[:, 2 + n, 0:h * NT].rearrange("p (e t) -> p e t", e=h)))
            f = lambda t: t[:].rearrange("p e t -> p (e t)")
            link(nc.vector.tensor_tensor_scan(f(after), f(keep), f(before), 0.0, ALU.mult, ALU.add))
            link(nc.vector.tensor_tensor(after[:], after[:], before[:], ALU.subtract))
            for n in range(2):
                link(nc.vector.tensor_tensor(before[:, n * h:(n + 1) * h, :], after[:, n * h:(n + 1) * h, :],
                                             psR[:, n, 0:h * NT].rearrange("p (e t) -> p e t", e=h), ALU.add))
            link(nc.vector.tensor_tensor(after[:], before[:], hot[:], ALU.mult))
            link(nc.vector.tensor_reduce(place[:], after[:].rearrange("p e t -> p t e"), AX.X, ALU.add))
            link(nc.vector.tensor_scalar(kept[:], place[:], z.capacity + 0.5, None, ALU.is_lt))
            link(nc.vector.tensor_tensor(T["weight"][:], T["weight"][:], kept[:], ALU.mult))
            link(nc.vector.scalar_tensor_tensor(out=slot_f[:], in0=first_e[:], scalar=float(z.slots), in1=place[:],
                                                op0=ALU.mult, op1=ALU.add))
            link(nc.vector.tensor_scalar(kept[:], kept[:], -1e6, 1e6 - 1, ALU.mult, ALU.add))
            link(nc.vector.tensor_tensor(slot_f[:], slot_f[:], kept[:], ALU.add))
            nc.vector.tensor_copy(T["slot"][:], slot_f[:])

        @block.tensor
        def _(pe):
            def turn(n, first=False):
                for i in range(2):
                    pe.wait_ge(xn_ready, 2 * n + i + 1)
                    if not first:
                        pe.wait_ge(xnT_ready, 2 * n + i - 1)
                    for k in range(K):
                        last = nc.tensor.transpose(psT[i][:, k, :], xn[i][:, k * P:(k + 1) * P], T["ident"][:])
                    last.then_inc(xn_turned, 1)
                for i in range(2):
                    pe.wait_ge(xnT_ready, 2 * n + i + 1)
                    if not first:
                        pe.wait_ge(logit_ready, 2 * n + i - 1)
                    for k in range(K):
                        last = nc.tensor.matmul(psL[i][:, 0:E], xnT[i][:, k, :], gw[:, k, :], start=(k == 0), stop=(k == K - 1))
                    last.then_inc(l_ready, 1)

            pe.wait_ge(w_loaded, 32)
            turn(0, True)
            with pe.Fori(1, turns) as n:
                turn(n)
            pe.wait_ge(hot_ready, 1)
            h = E // 2
            for n in range(2):
                half = hot[:, n * h:(n + 1) * h, :].rearrange("p e t -> p (e t)")
                nc.tensor.matmul(psR[:, n, 0:h * NT], tri[:], half, start=True, stop=True)
                last = nc.tensor.matmul(psR[:, 2 + n, 0:h * NT], T["ones"][:, 0:P], half, start=True, stop=True)
            last.then_inc(counted, 1)


def dispatch(nc, z, T, D, x1):
    NT, U = z.node_tiles, z.turn
    with ExitStack() as ctx:
        sb = lambda name, shape, dt=F32: ctx.enter_context(nc.sbuf_tensor(name, shape, dt))
        sem = z.semaphore
        out = [sb(f"sent_row{u}", [P, z.dim]) for u in range(U)]
        idx = [sb(f"sent_idx{u}", [P, 1], I32) for u in range(U)]
        row_ready, idx_ready = sem("sent_row_ready"), sem("sent_idx_ready")
        sent = [sem(f"row_sent{u}") for u in range(U)]
        block = ctx.enter_context(nc.Block())

        @block.vector
        def _(v):
            def turn(n, first=False):
                for u in range(U):
                    if not first:
                        v.wait_ge(sent[u], 16 * n)
                    t = n * U + u
                    nc.vector.tensor_scalar(out[u][:], x1[:, ds(t * z.dim, z.dim)], T["mean"][:, ds(t, 1)],
                                            T["rstd"][:, ds(t, 1)], ALU.subtract, ALU.mult).then_inc(row_ready, 1)

            turn(0, True)
            if NT // U > 1:
                with v.Fori(1, NT // U) as n:
                    turn(n)

        @block.gpsimd
        def _(pool):
            def turn(n, first=False):
                for u in range(U):
                    if not first:
                        pool.wait_ge(sent[u], 16 * n)
                    nc.gpsimd.tensor_copy(idx[u][:], T["slot"][:, ds(n * U + u, 1)]).then_inc(idx_ready, 1)
                    pool.wait_ge(idx_ready, n * U + u + 1)
                    pool.wait_ge(row_ready, n * U + u + 1)
                    pool.sem_inc(z.passed, 1)
                    pool.indirect_dma_start(D["buf"][:, :], bass.IndirectOffsetOnAxis(idx[u][:, 0:1], 0), out[u][:], None,
                                            bounds_check=z.experts * z.slots - 1, oob_is_err=False).then_inc(sent[u], 16)

            turn(0, True)
            if NT // U > 1:
                with pool.Fori(1, NT // U) as n:
                    turn(n)
            for u in range(U):
                pool.wait_ge(sent[u], 16 * (NT // U))


def experts(nc, z, w1, b1, w2, b2, T, D):
    E, NB, K1, K2, TB = z.experts, z.blocks, z.k1, z.k2, z.block // P
    HR = 4
    turns = E // 2
    with ExitStack() as ctx:
        sb = lambda name, shape, dt=F32: ctx.enter_context(nc.sbuf_tensor(name, shape, dt))
        sem = z.semaphore
        pair = lambda name: [sem(f"{name}{i}") for i in range(2)]
        ps = lambda name, k: [ctx.enter_context(nc.psum_tensor(f"{name}{i}", [P, 512], F32)) for i in range(k)]
        w1s = [sb(f"w1s{i}", [P, K1, z.hidden]) for i in range(2)]
        w2s = [sb(f"w2s{i}", [P, K2, z.dim]) for i in range(2)]
        b1s = [sb(f"b1s{i}", [P, K2]) for i in range(2)]
        b2s = [sb(f"b2s{i}", [P, z.dim]) for i in range(2)]
        xs = [sb(f"slot_rows{i}", [P, TB, z.dim]) for i in range(2)]
        xT = sb("slot_xT", [P, K1, z.block])
        hT = sb("slot_hT", [P, K2, z.block])
        ys = [sb(f"slot_y{i}", [P, TB, z.dim]) for i in range(2)]
        psT, psH, psY = ps("exp_psT", 2), ps("exp_psH", HR), ps("exp_psY", 2)
        w_loaded, x_loaded, y_saved = pair("w_loaded"), pair("slots_loaded"), pair("y_saved")
        x_turned, xT_ready, h_ready, hT_ready, y_ready, y_copied = (
            sem("x_turned"), sem("xT_ready"), sem("h_summed"), sem("hT_ready"), sem("y_summed"), sem("y_copied"))
        block = ctx.enter_context(nc.Block())

        def number(m, i, b):
            return 2 * NB * m + i * NB + b

        def uses(m, i, b):
            return NB * m + (i * NB + b) // 2 + 1

        def all_blocks(engine, one, before=None):
            for i in range(2):
                if before:
                    before(0, i, True)
                for b in range(NB):
                    one(0, i, b, True)
            with engine.Fori(1, turns) as m:
                for i in range(2):
                    if before:
                        before(m, i, False)
                    for b in range(NB):
                        one(m, i, b, False)

        @block.sync
        def _(sp):
            w1_v = w1.rearrange("e (k p) f -> (e k) p f", p=P)
            w2_v = w2.rearrange("e (k p) n -> (e k) p n", p=P)
            b1_v = b1.rearrange("e (k p) -> (e k) p", p=P)

            def load_w(m, i, first):
                e = 2 * m + i
                if not first:
                    sp.wait_ge(y_copied, (2 * m + i - 1) * NB * TB)
                sp.dma_start(w1s[i][:], w1_v[ds(e * K1, K1)].rearrange("k p f -> p k f")).then_inc(w_loaded[i], 16)
                sp.dma_start(w2s[i][:], w2_v[ds(e * K2, K2)].rearrange("k p n -> p k n")).then_inc(w_loaded[i], 16)
                with nc.allow_non_contiguous_dma(reason="1024 biases, one per partition and column"):
                    sp.dma_start(b1s[i][:], b1_v[ds(e * K2, K2)].rearrange("k p -> p k")).then_inc(w_loaded[i], 16)
                sp.dma_start(b2s[i][:], b2[ds(e, 1), :].to_broadcast([P, z.dim])).then_inc(w_loaded[i], 16)

            def load_x(m, i, b, first):
                i2 = (i * NB + b) % 2
                if not (first and i * NB + b < 2):
                    sp.wait_ge(x_turned, (number(m, i, b) - 1) * K1)
                sp.dma_start(xs[i2][:], D["buf"][ds(number(m, i, b) * z.block, z.block), :]
                             .rearrange("(t p) n -> p t n", p=P)).then_inc(x_loaded[i2], 16)

            all_blocks(sp, load_x, load_w)

        @block.tensor
        def _(pe):
            def one(m, i, b, first):
                blk, i2, start = number(m, i, b), (i * NB + b) % 2, first and i * NB + b == 0
                pe.wait_ge(x_loaded[i2], 16 * uses(m, i, b))
                for k in range(K1):
                    if not start:
                        pe.wait_ge(xT_ready, (blk - 1) * K1 + k + 1)
                    for t in range(TB):
                        last = nc.tensor.transpose(psT[k % 2][:, t * P:(t + 1) * P], xs[i2][:, t, k * P:(k + 1) * P],
                                                   T["ident"][:])
                    last.then_inc(x_turned, 1)
                if b == 0:
                    pe.wait_ge(w_loaded[i], 64 * (m + 1))
                pe.wait_ge(xT_ready, (blk + 1) * K1)
                for f in range(K2):
                    if not (start and f < HR):
                        pe.wait_ge(hT_ready, blk * K2 + f - HR + 1)
                    for k in range(K1):
                        last = nc.tensor.matmul(psH[f % HR][:], w1s[i][:, k, f * P:(f + 1) * P], xT[:, k, :],
                                                start=(k == 0), stop=(k == K1 - 1))
                    last.then_inc(h_ready, 1)
                pe.wait_ge(hT_ready, (blk + 1) * K2)
                for t in range(TB):
                    if not (start and t < 2):
                        pe.wait_ge(y_copied, blk * TB + t - 1)
                    for k in range(K2):
                        last = nc.tensor.matmul(psY[t % 2][:, 0:z.dim], hT[:, k, t * P:(t + 1) * P], w2s[i][:, k, :],
                                                start=(k == 0), stop=(k == K2 - 1))
                    last.then_inc(y_ready, 1)

            all_blocks(pe, one)

        @block.scalar
        def _(act):
            def one(m, i, b, first):
                blk = number(m, i, b)
                for f in range(K2):
                    act.wait_ge(h_ready, blk * K2 + f + 1)
                    if f == 0 and not (first and i * NB + b == 0):
                        act.wait_ge(y_ready, blk * TB)
                    nc.scalar.activation(hT[:, f, :], psH[f % HR][:], ACT.Relu, bias=b1s[i][:, f:f + 1])\
                             .then_inc(hT_ready, 1)

            all_blocks(act, one)

        @block.vector
        def _(v):
            def one(m, i, b, first):
                blk, i2 = number(m, i, b), (i * NB + b) % 2
                for k in range(K1):
                    v.wait_ge(x_turned, blk * K1 + k + 1)
                    if k == 0 and not (first and i * NB + b == 0):
                        v.wait_ge(h_ready, blk * K2)
                    nc.vector.tensor_copy(xT[:, k, :], psT[k % 2][:]).then_inc(xT_ready, 1)
                if not (first and i * NB + b < 2):
                    v.wait_ge(y_saved[i2], 16 * (uses(m, i, b) - 1))
                for t in range(TB):
                    v.wait_ge(y_ready, blk * TB + t + 1)
                    nc.vector.tensor_tensor(ys[i2][:, t, :], psY[t % 2][:, 0:z.dim], b2s[i][:], ALU.add).then_inc(y_copied, 1)

            all_blocks(v, one)

        @block.gpsimd
        def _(pool):
            def one(m, i, b, first):
                blk, i2 = number(m, i, b), (i * NB + b) % 2
                pool.wait_ge(y_copied, (blk + 1) * TB)
                pool.dma_start(D["y"][ds(blk * z.block, z.block), :].rearrange("(t p) n -> p t n", p=P), ys[i2][:])\
                    .then_inc(y_saved[i2], 16)

            all_blocks(pool, one)
            for i2 in range(2):
                pool.wait_ge(y_saved[i2], 16 * NB * turns)


def combine(nc, z, T, D, x1, out):
    NT, U = z.node_tiles, z.turn
    rounds = NT // U
    with ExitStack() as ctx:
        many = lambda name, shape, dt=F32: [ctx.enter_context(nc.sbuf_tensor(f"{name}{u}", shape, dt)) for u in range(U)]
        sem = z.semaphore
        sems = lambda name: [sem(f"{name}{u}") for u in range(U)]
        y, ty, low, side, res = (many(n, [P, z.dim]) for n in ("y", "ty", "y_low", "y_side", "res"))
        finite = many("finite", [P, z.dim], I32)
        idx = many("y_idx", [P, 1], I32)
        y_set, idx_ready, scaled, low_ready, side_ready, finite_ready, res_ready, picked, summed = map(
            sem, ("y_set", "y_idx_ready", "y_scaled", "y_low_ready", "y_side_ready", "y_finite_ready",
                  "res_ready", "y_picked", "res_summed"))
        got, saved = sems("y_got"), sems("res_saved")
        block = ctx.enter_context(nc.Block())

        def all_turns(engine, turn):
            turn(0, True)
            if rounds > 1:
                with engine.Fori(1, rounds) as n:
                    turn(n, False)

        @block.gpsimd
        def _(pool):
            def turn(n, first):
                for u in range(U):
                    if not first:
                        pool.wait_ge(scaled, (n - 1) * U + u + 1)
                    else:
                        nc.gpsimd.memset(y[u][:], 0.0).then_inc(y_set, 1)
                        pool.wait_ge(y_set, u + 1)
                    nc.gpsimd.tensor_copy(idx[u][:], T["slot"][:, ds(n * U + u, 1)]).then_inc(idx_ready, 1)
                    pool.wait_ge(idx_ready, n * U + u + 1)
                    pool.sem_inc(z.passed, 1)
                    pool.indirect_dma_start(y[u][:], None, D["y"][:, :], bass.IndirectOffsetOnAxis(idx[u][:, 0:1], 0),
                                            bounds_check=z.experts * z.slots - 1, oob_is_err=False).then_inc(got[u], 16)

            all_turns(pool, turn)

        @block.scalar
        def _(act):
            def turn(n, first):
                for u in range(U):
                    act.wait_ge(got[u], 16 * n + 16)
                    if not first:
                        act.wait_ge(picked, (n - 1) * U + u + 1)
                    nc.scalar.activation(ty[u][:], y[u][:], ACT.Copy, scale=T["weight"][:, ds(n * U + u, 1)])\
                             .then_inc(scaled, 1)
                for u in range(U):
                    act.wait_ge(side_ready, n * U + u + 1)
                    if not first:
                        act.wait_ge(summed, (n - 1) * U + u + 1)
                    nc.scalar.activation(res[u][:], side[u][:], ACT.Copy, scale=1e4).then_inc(res_ready, 1)

            all_turns(act, turn)

        @block.vector
        def _(v):
            def turn(n, first):
                for u in range(U):
                    v.wait_ge(scaled, n * U + u + 1)
                    if not first:
                        v.wait_ge(saved[u], 16 * n)
                    nc.vector.tensor_scalar(low[u][:], ty[u][:], -F32_MAX, None, ALU.is_lt).then_inc(low_ready, 1)
                    nc.vector.tensor_scalar(finite[u][:], ty[u][:], 0.0, 0.0, ALU.mult, ALU.is_equal)\
                             .then_inc(finite_ready, 1)
                for u in range(U):
                    v.wait_ge(low_ready, n * U + u + 1)
                    if not first:
                        v.wait_ge(res_ready, (n - 1) * U + u + 1)
                    nc.vector.scalar_tensor_tensor(out=side[u][:], in0=ty[u][:], scalar=F32_MAX, in1=low[u][:],
                                                   op0=ALU.is_gt, op1=ALU.subtract).then_inc(side_ready, 1)
                for u in range(U):
                    v.wait_ge(res_ready, n * U + u + 1)
                    v.wait_ge(finite_ready, n * U + u + 1)
                    v.sem_inc(z.passed, 1)
                    nc.vector.copy_predicated(res[u][:], finite[u][:], ty[u][:]).then_inc(picked, 1)
                for u in range(U):
                    v.wait_ge(picked, n * U + u + 1)
                    nc.vector.tensor_tensor(low[u][:], res[u][:], x1[:, ds((n * U + u) * z.dim, z.dim)], ALU.add)\
                             .then_inc(summed, 1)

            all_turns(v, turn)

        @block.sync
        def _(sp):
            def save(n, u, last=False):
                sp.wait_ge(summed, n * U + u + 1)
                if last:
                    sp.dma_start(out[(NT - 1) * P:z.nodes, :], low[u][0:z.last_rows, :]).then_inc(saved[u], 16)
                else:
                    sp.dma_start(out[ds((n * U + u) * P, P), :], low[u][:]).then_inc(saved[u], 16)

            if rounds > 1:
                with sp.Fori(0, rounds - 1) as n:
                    for u in range(U):
                        save(n, u)
            for u in range(U):
                save(rounds - 1, u, last=(u == U - 1))
            for u in range(U):
                sp.wait_ge(saved[u], 16 * rounds)


def gnn_moe(nc, x, src, dst, edge_attr, Wn, bn, We, be, attn, gate_w, gate_b, w1, b1, w2, b2, out):
    z = Sizes(x, src, edge_attr, w1)
    with ExitStack() as ctx:
        z.semaphore = lambda name: ctx.enter_context(nc.semaphore(name))
        z.passed = z.semaphore("passed")
        sb = lambda name, shape, dt=F32: ctx.enter_context(nc.sbuf_tensor(name, shape, dt))
        dram = lambda name, shape, dt=F32: nc.dram_tensor(name, shape, dt, kind="Internal").ap()
        D = {
            "src": dram("src_padded", [1, z.pad_edges], I32),
            "dst": dram("dst_padded", [1, 1 + z.pad_edges], I32),
            "masks": dram("segment_masks", [z.table_tiles, 3 * P]),
            "bounds": dram("row_bounds", [z.table_tiles, 2]),
            "offs": dram("sum_offsets", [z.table_tiles], I32),
            "rels": dram("first_positions", [z.table_tiles]),
            "table": dram("node_rows", [z.nodes, z.gathered]),
            "gnn": dram("gnn_rows", [z.node_tiles * P, z.dim]),
            "buf": dram("expert_rows", [z.experts * z.slots, z.dim]),
            "y": dram("expert_out", [z.experts * z.slots, z.dim]),
        }
        T = {
            "iota_i": sb("iota_i", [P, 2 * P], I32), "part_i": sb("part_i", [P, 1], I32),
            "iota": sb("iota", [P, 2 * P]), "part": sb("part", [P, 1]),
            "ones": sb("ones", [P, P]), "ident": sb("ident", [P, P]), "eps": sb("eps", [P, 1]),
            "mean": sb("mean", [P, z.node_tiles]), "rstd": sb("rstd", [P, z.node_tiles]),
            "weight": sb("expert_weight", [P, z.node_tiles]), "slot": sb("slot", [P, z.node_tiles], I32),
        }
        with ExitStack() as gnn:
            sb = lambda name, shape, dt=F32: gnn.enter_context(nc.sbuf_tensor(name, shape, dt))
            T |= {
                "neg_pos": sb("neg_pos", [P, z.tiles]), "src": sb("src_tiles", [P, z.tiles], I32),
                "node": sb("node_parts", [P, 2 * z.tiles], BF16), "offs": sb("offsets", [1, z.tiles], I32),
                "first_rank": sb("first_rank", [P, z.chunks]), "other_rank": sb("other_rank", [P, z.chunks]),
                "we": sb("we_attn", [P, z.edge_dim]),
            }
            edge_tables(nc, z, src, dst, T, D)
            with nc.sbuf_tensor("wn_t", [P, z.k1, z.gathered], F32) as wn_t, \
                    nc.sbuf_tensor("bias_row", [P, z.gathered], F32) as bias_row:
                T |= {"wn": wn_t, "bias": bias_row}
                weights(nc, z, Wn, bn, We, be, attn, T)
                node_table(nc, z, x, T, D)
            with nc.sbuf_tensor("rank_sums", [P, (z.node_tiles + 1) * z.row], F32) as acc:
                edges(nc, z, edge_attr, T, D, acc)
                scatter_sums(nc, z, T, D, acc)
        with nc.sbuf_tensor("x1", [P, z.node_tiles * z.dim], F32) as x1:
            gate(nc, z, x, gate_w, gate_b, T, D, x1)
            dispatch(nc, z, T, D, x1)
            experts(nc, z, w1, b1, w2, b2, T, D)
            combine(nc, z, T, D, x1, out)


INPUTS = ["x", "src", "dst", "edge_attr_128", "L0_gnn_Wn", "L0_gnn_bn", "L0_gnn_We", "L0_gnn_be", "L0_gnn_attn",
          "L0_ffn_gate_w", "L0_ffn_gate_b", "L0_ffn_w1", "L0_ffn_b1", "L0_ffn_w2", "L0_ffn_b2"]


def kernel(**inputs):
    import numpy as np
    import concourse.bacc as bacc
    from concourse.bass_utils import run_bass_kernel_spmd

    nc = bacc.Bacc("TRN2", target_bir_lowering=False, num_devices=1)
    arrays, args = {}, []
    for name in INPUTS:
        a = np.ascontiguousarray(inputs[name])
        if name in ("src", "dst"):
            a = a.reshape(1, -1)
        arrays[f"in_{name}"] = a
        args.append(nc.dram_tensor(f"in_{name}", a.shape, mybir.dt.from_np(a.dtype), kind="ExternalInput").ap())
    shape = inputs["x"].shape
    args.append(nc.dram_tensor("out", shape, F32, kind="ExternalOutput").ap())
    gnn_moe(nc, *args)
    r = run_bass_kernel_spmd(nc, [arrays], core_ids=[0])
    return r.results[0]["out"]
```

```python
from contextlib import ExitStack

import concourse.bass as bass
from concourse import mybir

F32 = mybir.dt.float32
BF16 = mybir.dt.bfloat16
I32 = mybir.dt.int32
ALU = mybir.AluOpType
ACT = mybir.ActivationFunctionType
AX = mybir.AxisListType
ds = bass.ds

P = 128
BIG = 1e30
CHUNK_STEPS = 16
SLOPE = 0.01
EPS = 1e-5
F32_MAX = 3.4028234663852886e38


def ceil_div(a, b):
    return -(-a // b)


class Sizes:

    def __init__(self, x, src, edge_attr, w1):
        self.nodes, self.dim = x.shape
        self.edges = src.shape[1]
        self.edge_dim = edge_attr.shape[1]
        self.experts, _, self.hidden = w1.shape
        self.node_tiles = 2 * ceil_div(self.nodes, 2 * P)
        self.last_rows = self.nodes - (self.node_tiles - 1) * P
        assert 0 < self.last_rows < P and self.dim == 2 * P and self.edge_dim == P
        self.tiles = ceil_div(self.edges, P)
        self.last_edges = self.edges - (self.tiles - 1) * P
        self.dot_chunks = 2 * ceil_div(self.tiles, 2 * CHUNK_STEPS)
        self.steps = self.tiles + self.node_tiles - 1
        self.chunks = 2 * ceil_div(self.steps, 2 * CHUNK_STEPS)
        assert self.last_edges < P and self.chunks > self.dot_chunks
        self.step_blocks = ceil_div(self.chunks * CHUNK_STEPS, P)
        self.table = self.step_blocks * P
        self.pad_edges = self.table * P
        self.row = self.dim + 2
        self.capacity = max(1, ceil_div(5 * self.nodes, 4 * self.experts))
        self.block = 512
        self.blocks = ceil_div(self.capacity, self.block)
        self.slots = self.blocks * self.block
        self.k1 = self.dim // P
        self.k2 = self.hidden // P
        self.turn = max(u for u in range(1, 8) if self.node_tiles % u == 0)
        self.turns = self.node_tiles // self.turn
        assert self.turns > 2




def step_tables(nc, z, src, dst, T, D):
    B, K = z.step_blocks, z.table
    pad = z.pad_edges - z.edges
    pad_node = z.node_tiles * P - 1
    with ExitStack() as ctx:
        sb = lambda name, shape, dt=F32: ctx.enter_context(nc.sbuf_tensor(name, shape, dt))
        sem = z.semaphore
        pad_m, pad_r = pad // P, pad % P
        pads = sb("pads", [P, max(pad_m, P)], I32)
        zero_pads = sb("zero_pads", [P, max(pad_m, P)], I32)
        number_i, number = sb("number_i", [P, B], I32), sb("number", [P, B])
        ends_i, ends = sb("tile_ends_i", [P, 2, B], I32), sb("tile_ends", [P, 3, B])
        turns_all = sb("turns_all", [P, K])
        less = sb("less", [P, K])
        tile_f, tile_i = sb("tile_of_step", [P, B]), sb("tile_of_step_i", [P, B], I32)
        block_f, shift, at_f = sb("block_of_step", [P, B]), sb("shift", [P, B]), sb("first_at", [P, B])
        near, near_i = sb("near", [P, B]), sb("near_i", [P, B], I32)
        before = sb("tail_before", [P, B])
        rows_i = sb("rows_i", [P, 2, B, P], I32)
        rows = sb("rows", [P, 2, B, P])
        starts = sb("starts", [P, B, P])
        masks = sb("masks", [P, B, 3, P])
        bounds = sb("bounds", [P, B, 2])
        ps = ctx.enter_context(nc.psum_tensor("table_ps", [P, 4, 512], F32))
        pad_set, padded, ends_loaded, chain, turns_ready, turns_saved, turns_loaded, index_ready = map(sem, (
            "pads_set", "padded", "ends_loaded", "table_chain", "turns_ready", "turns_saved", "turns_loaded",
            "index_ready"))
        rows_loaded, tails_ready, tails_saved, before_loaded, masks_ready, saved, small_ready, rel_loaded = map(sem, (
            "rows_loaded", "tails_ready", "tails_saved", "before_loaded", "masks_ready", "tables_saved",
            "small_ready", "small_loaded"))
        consts, pos_ready, turned, evacuated = map(sem, ("consts_ready", "pos_ready", "turned", "evacuated"))
        block = ctx.enter_context(nc.Block())
        by_q = lambda d, at=0: d[at:at + K].rearrange("(b q) -> q b", q=P)
        row = lambda d: d.rearrange("(a t) -> a t", a=1)

        @block.sync
        def _(sp):
            sp.wait_ge(pad_set, 3)
            sp.dma_start(D["dst"][0:1, 0:z.edges], dst).then_inc(padded, 16)
            sp.dma_start(D["src"][0:1, 0:z.edges], src).then_inc(padded, 16)
            sent = 32
            for d, value in ((D["dst"], pads), (D["src"], zero_pads)):
                at = z.edges + P * pad_m
                sp.dma_start(d[0, z.edges:at].rearrange("(p m) -> p m", p=P), value[:, 0:pad_m]).then_inc(padded, 16)
                sent += 16
                if pad_r:
                    sp.dma_start(d[0:1, at:at + pad_r], value[0:1, 0:pad_r]).then_inc(padded, 16)
                    sent += 16
            sp.dma_start(row(D["tails"])[:, 0:1], T["ones"][0:1, 0:1]).then_inc(padded, 16)
            sp.wait_ge(padded, sent + 16)
            with nc.allow_non_contiguous_dma(reason="one element per tile or step"):
                sp.dma_start(ends_i[:, 0, :], D["dst"][0, :].rearrange("(b q i) -> q b i", q=P, i=P)[:, :, P - 1])\
                  .then_inc(ends_loaded, 16)
                sp.wait_ge(turns_ready, 1)
                sp.dma_start(by_q(D["turns"]), ends[:, 2, :]).then_inc(turns_saved, 16)
                sp.wait_ge(turns_saved, 16)
                sp.dma_start(turns_all[:], row(D["turns"]).to_broadcast([P, K])).then_inc(turns_loaded, 16)
                sp.wait_ge(tails_ready, 1)
                sp.dma_start(by_q(D["tails"], 1), ends[:, 0, :]).then_inc(tails_saved, 16)
                sp.wait_ge(tails_saved, 16)
                sp.dma_start(before[:], by_q(D["tails"])).then_inc(before_loaded, 16)
                sp.wait_ge(small_ready, 2)
                sp.dma_start(by_q(D["offs"]), near_i[:]).then_inc(saved, 16)
                sp.dma_start(by_q(D["rels"]), at_f[:]).then_inc(saved, 16)
            sp.wait_ge(masks_ready, 1)
            sp.dma_start(D["masks"].rearrange("(b q) m -> q b m", q=P),
                         masks[:].rearrange("q b m i -> q b (m i)")).then_inc(saved, 16)
            sp.dma_start(D["bounds"][0:K].rearrange("(b q) m -> q b m", q=P), bounds[:]).then_inc(saved, 16)
            sp.dma_start(D["bounds"][K:K + 1], T["ones"][0:1, 0:2]).then_inc(saved, 16)
            sp.wait_ge(saved, 80)
            sp.dma_start(T["offs"][0:1, :], row(D["offs"])).then_inc(rel_loaded, 16)
            sp.dma_start(less[:], row(D["rels"]).to_broadcast([P, K])).then_inc(rel_loaded, 16)
            sp.wait_ge(rel_loaded, 32)

        @block.gpsimd
        def _(pool):
            nc.gpsimd.iota(T["iota_i"][:], pattern=[[1, P]], base=0, channel_multiplier=0).then_inc(consts, 1)
            nc.gpsimd.iota(T["part_i"][:], pattern=[[0, 1]], base=0, channel_multiplier=1).then_inc(consts, 1)
            nc.gpsimd.iota(number_i[:], pattern=[[P, B]], base=0, channel_multiplier=1).then_inc(consts, 1)
            pool.wait_ge(index_ready, 1)
            for n, d in enumerate((D["dst"], D["src"])):
                table = d[0, :].rearrange("(t i) -> t i", i=P)
                for b in range(B):
                    pool.indirect_dma_start(rows_i[:, n, b, :], None, table,
                                            bass.IndirectOffsetOnAxis(tile_i[:, b:b + 1], 0)).then_inc(rows_loaded, 16)

        @block.vector
        def _(v):
            nc.vector.memset(pads[:], pad_node).then_inc(pad_set, 1)
            nc.vector.memset(T["ones"][:], 1.0).then_inc(pad_set, 1)
            nc.vector.memset(zero_pads[:], 0).then_inc(pad_set, 1)
            done = [0]

            def link(instruction):
                done[0] += 1
                instruction.then_inc(chain, 1)
                v.wait_ge(chain, done[0])

            v.wait_ge(consts, 3)
            link(nc.vector.tensor_copy(T["iota"][:], T["iota_i"][:]))
            link(nc.vector.tensor_copy(T["part"][:], T["part_i"][:]))
            link(nc.vector.tensor_copy(number[:], number_i[:]))
            link(nc.vector.tensor_scalar(T["ident"][:], T["iota"][:, 0:P], T["part"][:, 0:1], None, ALU.is_equal))
            v.wait_ge(ends_loaded, 16)
            link(nc.vector.tensor_scalar(ends_i[:, 1, :], ends_i[:, 0, :], 7, None, ALU.arith_shift_right))
            link(nc.vector.tensor_copy(ends[:, 0, :], ends_i[:, 1, :]))
            link(nc.vector.scalar_tensor_tensor(out=ends[:, 1, :], in0=number[:], scalar=1.0, in1=ends[:, 0, :],
                                                op0=ALU.add, op1=ALU.add))
            link(nc.vector.tensor_scalar(shift[:], number[:], z.tiles - 1.5, 1e6, ALU.is_gt, ALU.mult))
            nc.vector.tensor_tensor(ends[:, 2, :], ends[:, 1, :], shift[:], ALU.add).then_inc(turns_ready, 1)
            v.wait_ge(turns_loaded, 16)
            for b in range(B):
                link(nc.vector.tensor_scalar(less[:], turns_all[:], number[:, b:b + 1], None, ALU.is_le, ALU.add,
                                             accum_out=tile_f[:, b:b + 1]))
            nc.vector.tensor_copy(tile_i[:], tile_f[:]).then_inc(index_ready, 1)
            link(nc.vector.tensor_tensor(block_f[:], number[:], tile_f[:], ALU.subtract))
            link(nc.vector.tensor_scalar_min(near[:], block_f[:], float(z.node_tiles - 1)))
            nc.vector.tensor_copy(near_i[:], near[:]).then_inc(small_ready, 1)
            link(nc.vector.tensor_scalar_mul(shift[:], block_f[:], -float(P)))
            v.wait_ge(rows_loaded, 32 * B)
            link(nc.vector.tensor_copy(rows[:], rows_i[:]))
            d = rows[:, 0, :, :]
            nc.vector.tensor_copy(ends[:, 0, :], d[:, :, P - 1]).then_inc(tails_ready, 1)
            link(nc.vector.tensor_tensor(at_f[:], d[:, :, 0], shift[:], ALU.add))
            nc.vector.memset(near[:], 0.0).then_inc(small_ready, 1)
            for b in range(B):
                for m, at in ((1, 0), (2, P - 1)):
                    link(nc.vector.tensor_scalar(masks[:, b, m, :], d[:, b, :], d[:, b, at:at + 1], -BIG,
                                                 ALU.not_equal, ALU.mult))
            link(nc.vector.tensor_tensor(starts[:, :, 1:P], d[:, :, 1:P], d[:, :, 0:P - 1], ALU.not_equal))
            v.wait_ge(before_loaded, 16)
            link(nc.vector.tensor_tensor(starts[:, :, 0], d[:, :, 0], before[:], ALU.not_equal))
            link(nc.vector.memset(starts[0:1, 0, 0:1], 1.0))
            link(nc.vector.tensor_scalar_mul(masks[:, :, 0, :], starts[:], -BIG))
            link(nc.vector.tensor_copy(bounds[:, :, 0], masks[:, :, 0, 0]))
            nc.vector.tensor_copy(bounds[:, :, 1], masks[:, :, 1, P - 1]).then_inc(masks_ready, 1)
            v.wait_ge(masks_ready, 1)
            for b in range(B):
                last = nc.vector.tensor_scalar_add(starts[:, b, :], d[:, b, :], shift[:, b:b + 1])
            last.then_inc(pos_ready, 1)
            for b in range(B):
                for n in range(2):
                    k = 2 * b + n
                    v.wait_ge(turned, k + 1)
                    got = ps[:, k % 4, 0:P]
                    if n == 0:
                        nc.vector.tensor_scalar_mul(T["neg_pos"][:, b * P:(b + 1) * P], got, -1.0).then_inc(evacuated, 1)
                    else:
                        nc.vector.tensor_copy(T["src"][:, b * P:(b + 1) * P], got).then_inc(evacuated, 1)
            v.wait_ge(rel_loaded, 32)
            first = less[:, 0:z.chunks * CHUNK_STEPS].rearrange("p (c g) -> p c g", g=CHUNK_STEPS)[:, :, 0]
            link(nc.vector.tensor_scalar(T["open_node"][:], first, T["part"][:, 0:1], None, ALU.is_equal))
            link(nc.vector.tensor_scalar(T["other_node"][:], first, T["part"][:, 0:1], None, ALU.not_equal))

        @block.tensor
        def _(pe):
            pe.wait_ge(pos_ready, 1)
            for b in range(B):
                for n, table in enumerate((starts, rows)):
                    k = 2 * b + n
                    if k >= 4:
                        pe.wait_ge(evacuated, k - 3)
                    one = table[:, b, :] if n == 0 else table[:, 1, b, :]
                    nc.tensor.transpose(ps[:, k % 4, 0:P], one, T["ident"][:]).then_inc(turned, 1)


def weights(nc, z, Wn, bn, We, be, attn, T):
    K = z.k1
    with ExitStack() as ctx:
        sb = lambda name, shape, dt=F32: ctx.enter_context(nc.sbuf_tensor(name, shape, dt))
        sem = z.semaphore
        wn = sb("wn", [P, K, z.dim])
        we = sb("we", [P, K, z.edge_dim])
        at = sb("attn_col", [P, K])
        at_wide = sb("attn_wide", [P, K, P])
        bnc, bec = sb("bn_col", [P, K]), sb("be_col", [P, K])
        bias_sum = sb("bias_sum", [P, K])
        ps = [ctx.enter_context(nc.psum_tensor(f"weight_ps{i}", [P, 512], F32)) for i in range(6)]
        loaded, ready, turned, chain = sem("weights_loaded"), sem("wide_ready"), sem("weights_turned"), sem("weight_chain")
        block = ctx.enter_context(nc.Block())

        @block.sync
        def _(sp):
            sp.dma_start(wn[:], Wn.rearrange("(k p) n -> p k n", p=P)).then_inc(loaded, 16)
            sp.dma_start(we[:], We.rearrange("(k p) n -> p k n", p=P)).then_inc(loaded, 16)
            with nc.allow_non_contiguous_dma(reason="three columns of 256 elements"):
                sp.dma_start(at[:], attn[0, 0, :].rearrange("(k p) -> p k", p=P)).then_inc(loaded, 16)
                sp.dma_start(bnc[:], bn.rearrange("(k p) -> p k", p=P)).then_inc(loaded, 16)
                sp.dma_start(bec[:], be.rearrange("(k p) -> p k", p=P)).then_inc(loaded, 16)
            sp.dma_start(T["bias"][:, 0:z.dim], bn.rearrange("(a n) -> a n", a=1).to_broadcast([P, z.dim])).then_inc(loaded, 16)

        @block.vector
        def _(v):
            done = [0]

            def link(instruction):
                done[0] += 1
                instruction.then_inc(chain, 1)
                v.wait_ge(chain, done[0])

            v.wait_ge(loaded, 96)
            for k in range(K):
                nc.vector.tensor_scalar_mul(at_wide[:, k, :], T["ones"][:, 0:P], at[:, k:k + 1]).then_inc(ready, 1)
            nc.vector.tensor_tensor(bias_sum[:], bnc[:], bec[:], ALU.add).then_inc(ready, 1)
            nc.vector.memset(T["wn"][:, :, z.dim:z.dim + 1], 0.0)
            nc.vector.memset(T["bias"][:, z.dim:z.dim + 1], 1.0)
            nc.vector.memset(T["eps"][:], EPS)
            v.wait_ge(turned, 1)
            for k in range(K):
                nc.vector.tensor_copy(T["wn"][:, k, 0:z.dim], ps[k][:, 0:z.dim])
                nc.vector.tensor_copy(T["wn"][:, k, z.dim + 1:z.dim + 2], ps[2 + k][:, 0:1])
            nc.vector.tensor_copy(T["we"][:], ps[4][:, 0:z.edge_dim])
            nc.vector.tensor_copy(T["bias"][:, z.dim + 1:z.dim + 2], ps[5][:, 0:1])

        @block.tensor
        def _(pe):
            pe.wait_ge(ready, K + 1)
            for k in range(K):
                for n in range(K):
                    nc.tensor.transpose(ps[k][:, n * P:(n + 1) * P], wn[:, n, k * P:(k + 1) * P], T["ident"][:])
                for n in range(K):
                    nc.tensor.matmul(ps[2 + k][:, 0:1], wn[:, n, k * P:(k + 1) * P], at[:, n:n + 1],
                                     start=(n == 0), stop=(n == K - 1))
            for n in range(K):
                nc.tensor.matmul(ps[4][:, 0:z.edge_dim], at_wide[:, n, :], we[:, n, :], start=(n == 0), stop=(n == K - 1))
            for n in range(K):
                last = nc.tensor.matmul(ps[5][:, 0:1], at_wide[:, n, :], bias_sum[:, n:n + 1],
                                        start=(n == 0), stop=(n == K - 1))
            last.then_inc(turned, 1)


def load_rows(sp, z, out, dram, t, last, sem):
    if last:
        sp.dma_start(out[0:z.last_rows], dram[(z.node_tiles - 1) * P:z.nodes, :]).then_inc(sem, 16)
    else:
        sp.dma_start(out, dram[ds(t * P, P), :]).then_inc(sem, 16)


def behind(z, n, u, ring):
    if u >= ring:
        return n * z.turn + u - ring + 1
    return (n - 1) * z.turn + max(w for w in range(z.turn) if w % ring == u) + 1


def node_turns(engine, z, turn):
    turn(0, True)
    with engine.Fori(1, z.turns) as n:
        turn(n, False)


def node_table(nc, z, x, T, D):
    K, W, U = z.k1, z.row, z.turn
    RING, HR = 3, 5
    with ExitStack() as ctx:
        sem = z.semaphore
        many = lambda name, shape: [ctx.enter_context(nc.sbuf_tensor(f"{name}{u}", shape, F32)) for u in range(U)]
        xt, stats, mv, std, rstd, xn, xnT, row = map(many, (
            "node_x", "node_stats", "node_mv", "node_std", "node_rstd", "node_xn", "node_xnT", "node_row"), (
            [P, z.dim], [P, 6], [P, 2], [P, 1], [P, 1], [P, z.dim], [P, K, P], [P, W]))
        zeros = ctx.enter_context(nc.sbuf_tensor("zeros", [P, 8, z.dim], F32))
        psT = [ctx.enter_context(nc.psum_tensor(f"node_psT{i}", [P, K, P], F32)) for i in range(RING)]
        psH = [ctx.enter_context(nc.psum_tensor(f"node_psH{i}", [P, 512], F32)) for i in range(HR)]
        x_loaded, row_saved = z.rows_in, z.rows_out
        (stats_ready, mv_ready, std_ready, rstd_ready, xn_ready, xn_turned, xnT_ready, h_ready,
         row_ready) = map(sem, ("stats_ready", "mv_ready", "std_ready", "rstd_ready", "xn_ready", "xn_turned",
                                "xnT_ready", "h_ready", "row_ready"))
        zeros_set, zeroed = sem("zeros_set"), sem("zeroed")
        block = ctx.enter_context(nc.Block())

        @block.sync
        def _(sp):
            def turn(n, first, last=False):
                for u in range(U):
                    if not first:
                        sp.wait_ge(xn_ready, (n - 1) * U + u + 1)
                    load_rows(sp, z, xt[u][:], x, n * U + u, last and u == U - 1, x_loaded[u])

            turn(0, True)
            with sp.Fori(1, z.turns - 1) as n:
                turn(n, False)
            turn(z.turns - 1, False, True)

        @block.gpsimd
        def _(pool):
            nc.gpsimd.memset(zeros[:], 0.0).then_inc(zeros_set, 1)
            pool.wait_ge(zeros_set, 1)
            rows = z.experts * z.slots
            for at in range(0, rows, 8 * P):
                n = min(8, (rows - at) // P)
                pool.dma_start(D["buf"][at:at + n * P, :].rearrange("(p k) n -> p k n", k=n), zeros[:, 0:n, :])\
                    .then_inc(zeroed, 16)
            pool.wait_ge(zeroed, 16 * ceil_div(rows, 8 * P))

        @block.scalar
        def _(act):
            def store(n, u, last=False):
                act.wait_ge(row_ready, n * U + u + 1)
                if last:
                    act.dma_start(D["table"][(z.node_tiles - 1) * P:z.nodes, :], row[u][0:z.last_rows, :])\
                       .then_inc(row_saved[u], 16)
                else:
                    act.dma_start(D["table"][ds((n * U + u) * P, P), :], row[u][:]).then_inc(row_saved[u], 16)

            def turn(n, first):
                for u in range(U):
                    act.wait_ge(mv_ready, n * U + u + 1)
                    if not first:
                        act.wait_ge(rstd_ready, (n - 1) * U + u + 1)
                    nc.scalar.activation(std[u][:], mv[u][:, 1:2], ACT.Sqrt, bias=T["eps"][:, 0:1]).then_inc(std_ready, 1)
                for u in range(U):
                    act.wait_ge(xn_turned, n * U + u + 1)
                    if not first:
                        act.wait_ge(h_ready, (n - 1) * U + u + 1)
                    nc.scalar.copy(xnT[u][:], psT[u % RING][:]).then_inc(xnT_ready, 1)
                if not first:
                    for u in range(U):
                        store(n - 1, u)

            node_turns(act, z, turn)
            for u in range(U):
                store(z.turns - 1, u, last=(u == U - 1))
            for u in range(U):
                act.wait_ge(row_saved[u], 16 * z.turns)

        @block.vector
        def _(v):
            def rows(n, first=False):
                for u in range(U):
                    v.wait_ge(h_ready, n * U + u + 1)
                    if not first:
                        v.wait_ge(row_saved[u], 16 * n)
                    nc.vector.tensor_tensor(row[u][:], psH[u % HR][:, 0:W], T["bias"][:], ALU.add).then_inc(row_ready, 1)

            def turn(n, looped=False):
                first = not looped and n == 0
                for u in range(U):
                    v.wait_ge(x_loaded[u], 16 * n + 16)
                    v.sem_inc(z.passed, 1)
                    nc.vector.bn_stats(stats[u][:], xt[u][:]).then_inc(stats_ready, 1)
                for u in range(U):
                    v.wait_ge(stats_ready, n * U + u + 1)
                    v.sem_inc(z.passed, 1)
                    nc.vector.bn_aggr(mv[u][:], stats[u][:]).then_inc(mv_ready, 1)
                if not first:
                    rows(n - 1, not looped)
                for u in range(U):
                    v.wait_ge(std_ready, n * U + u + 1)
                    nc.vector.reciprocal(rstd[u][:], std[u][:]).then_inc(rstd_ready, 1)
                for u in range(U):
                    v.wait_ge(rstd_ready, n * U + u + 1)
                    if not first:
                        v.wait_ge(xn_turned, (n - 1) * U + u + 1)
                    nc.vector.tensor_scalar(xn[u][:], xt[u][:], mv[u][:, 0:1], rstd[u][:, 0:1],
                                            ALU.subtract, ALU.mult).then_inc(xn_ready, 1)

            turn(0)
            turn(1)
            with v.Fori(2, z.turns) as n:
                turn(n, looped=True)
            rows(z.turns - 1)

        @block.tensor
        def _(pe):
            def turn(n, first):
                for u in range(U):
                    pe.wait_ge(xn_ready, n * U + u + 1)
                    if not (first and u < RING):
                        pe.wait_ge(xnT_ready, behind(z, n, u, RING))
                    for k in range(K):
                        last = nc.tensor.transpose(psT[u % RING][:, k, :], xn[u][:, k * P:(k + 1) * P],
                                                   T["ident"][:])
                    last.then_inc(xn_turned, 1)
                for u in range(U):
                    pe.wait_ge(xnT_ready, n * U + u + 1)
                    if not (first and u < HR):
                        pe.wait_ge(row_ready, behind(z, n, u, HR))
                    for k in range(K):
                        last = nc.tensor.matmul(psH[u % HR][:, 0:W], xnT[u][:, k, :], T["wn"][:, k, :],
                                                start=(k == 0), stop=(k == K - 1))
                    last.then_inc(h_ready, 1)

            node_turns(pe, z, turn)


def edges(nc, z, edge_attr, T, D, acc):
    C, G, W, DC = z.chunks, CHUNK_STEPS, z.row, z.dot_chunks
    S = z.dim + 1
    turns = C // 2
    RING = 4
    H = G // 2
    LEAD = z.node_tiles
    with ExitStack() as ctx:
        sb = lambda name, shape, dt=F32: ctx.enter_context(nc.sbuf_tensor(name, shape, dt))
        ps = lambda name, shape: ctx.enter_context(nc.psum_tensor(name, shape, F32))
        sem = z.semaphore
        pair = lambda name: [sem(f"{name}{i}") for i in range(2)]
        rows = [sb(f"gathered{i}", [P, G, W]) for i in range(2)]
        idx = [sb(f"chunk_src{i}", [P, G], I32) for i in range(2)]
        ea = [sb(f"edge_rows{i}", [P, G, P]) for i in range(2)]
        dot_out = sb("dot_out", [P, G, P])
        masks = [sb(f"chunk_masks{i}", [G, 3, P]) for i in range(2)]
        bounds = [sb(f"chunk_bounds{i}", [1, 2 * G + 1]) for i in range(2)]
        dots, raw, score = sb("dots", [P, LEAD + C * G]), sb("raw_score", [P, G]), sb("score", [P, G])
        new_dots, new_dots_ready = sb("new_dots", [P, G]), sem("new_dots_ready")
        fwd, seg = sb("fwd_max", [G, P]), sb("seg_max", [G, P])
        ends_fwd = [sb(f"ends_fwd{i}", [1, 2 * G]) for i in range(2)]
        ends = sb("ends_max", [1, 2 * G])
        cols = sb("end_cols", [G, 2])
        seg_a, seg_b, centred, expd = (sb(n, [G, P]) for n in ("seg_a", "seg_b", "centred", "expd"))
        goes_on, rise, rise_on = sb("goes_on", [1, 1]), sb("rise", [1, 1]), sb("rise_on", [1, 1])
        rescale, factor = sb("rescale", [P, 1]), sb("factor", [P, 1])
        prob = [sb(f"prob{i}", [P, G]) for i in range(2)]
        neg_prob = [sb(f"neg_prob{i}", [P, G]) for i in range(2)]
        dist = sb("dist", [P, 2, P])
        onehot = sb("onehot", [P, RING, P])
        psA, psE = ps("psA", [G, 512]), ps("psE", [P, 512])
        psX, psY = ps("psX", [1, 512]), ps("psY", [P, 512])
        sums = [ps(f"sums{i}", [P, 512]) for i in range(RING)]

        src_staged, gathered = sem("src_staged"), pair("gathered")
        ea_loaded, masks_loaded = pair("ea_loaded"), pair("masks_loaded")
        (dots_ready, raw_ready, score_ready, score_rows, fwd_ready, seg_ready, ends_rows, ends_fwd_ready,
         ends_ready, on_ready, rise_ready, rise_on_ready, cols_ready, cols_copied, seg_a_ready, seg_b_ready,
         centred_ready, exp_ready, exp_cols, prob_ready, neg_ready, rescale_ready, factor_ready, rescaled) = map(sem, (
             "dots_ready", "raw_ready", "score_ready", "score_rows", "fwd_ready", "seg_ready", "ends_rows",
             "ends_fwd_ready", "ends_ready", "on_ready", "rise_ready", "rise_on_ready", "cols_ready",
             "cols_copied", "seg_a_ready", "seg_b_ready", "centred_ready", "exp_ready", "exp_cols", "prob_ready",
             "neg_ready", "rescale_ready", "factor_ready", "rescaled"))
        dist_ready, onehot_ready, step_summed, step_added = (
            sem("dist_ready"), sem("onehot_ready"), sem("step_summed"), sem("step_added"))
        acc_zero, carry_set = sem("acc_zero"), sem("carry_set")
        no_max = sb("no_max", [1, 1])
        block = ctx.enter_context(nc.Block())

        @block.gpsimd
        def _(pool):
            def chunk(i, c, first=False):
                for g in range(G):
                    if g % 4 == 0 and not first:
                        pool.wait_ge(step_summed, (c - 2) * G + g + 4)
                    if g == 0:
                        nc.gpsimd.tensor_copy(idx[i][:], T["src"][:, ds(c * G, G)]).then_inc(src_staged, 1)
                        pool.wait_ge(src_staged, c + 1)
                    if g % 4 == 0:
                        pool.sem_inc(z.passed, 1)
                    pool.indirect_dma_start(rows[i][:, g, 0:W], None, D["table"][:, :],
                                            bass.IndirectOffsetOnAxis(idx[i][:, g:g + 1], 0)).then_inc(gathered[i], 16)

            for i in range(2):
                chunk(i, i, True)
            with pool.Fori(1, turns) as n:
                for i in range(2):
                    chunk(i, 2 * n + i)

        @block.sync
        def _(sp):
            view = edge_attr[0:(z.tiles - 1) * P, :].rearrange("(t p) n -> p t n", p=P)
            masks_v = D["masks"].rearrange("t (m i) -> t m i", m=3)
            flat = D["bounds"].rearrange("t m -> (t m)").rearrange("(a n) -> a n", a=1)

            def edge_rows(i, c, first=False, last=False):
                if not first:
                    sp.wait_ge(dots_ready, c - 1)
                if last:
                    full = z.tiles - 1 - c * G
                    assert 0 < full < G
                    sp.dma_start(ea[i][:, 0:full, :], view[:, c * G:c * G + full, :]).then_inc(ea_loaded[i], 16)
                    sp.dma_start(ea[i][0:z.last_edges, full, :], edge_attr[z.edges - z.last_edges:z.edges, :])\
                      .then_inc(ea_loaded[i], 16)
                else:
                    for half in range(2):
                        sp.dma_start(ea[i][:, half * H:half * H + H, :], view[:, ds(c * G + half * H, H), :])\
                          .then_inc(ea_loaded[i], 16)

            def chunk_masks(i, c, first=False):
                if not first:
                    sp.wait_ge(seg_b_ready, c - 1)
                    sp.wait_ge(on_ready, c - 1)
                    sp.wait_ge(ends_ready, c - 1)
                sp.dma_start(masks[i][:], masks_v[ds(c * G, G)]).then_inc(masks_loaded[i], 16)
                sp.dma_start(bounds[i][:], flat[:, ds(c * 2 * G, 2 * G + 1)]).then_inc(masks_loaded[i], 16)

            for i in range(2):
                edge_rows(i, i, True)
                chunk_masks(i, i, True)
            with sp.Fori(1, DC // 2 - 1) as n:
                for i in range(2):
                    edge_rows(i, 2 * n + i)
                    chunk_masks(i, 2 * n + i)
            for i in range(2):
                edge_rows(i, DC - 2 + i, last=(i == 1))
                chunk_masks(i, DC - 2 + i)
            with sp.Fori(DC // 2, turns) as n:
                for i in range(2):
                    chunk_masks(i, 2 * n + i)

        @block.vector
        def _(v):
            def score_steps(i, c, n, js, first=False, with_dots=True):
                def edge_dots(g0, g1):
                    if g0 == 0:
                        v.wait_ge(ea_loaded[i], 32 * n + 32)
                        if not first:
                            v.wait_ge(new_dots_ready, c)
                            v.wait_ge(dots_ready, c)
                    for g in range(g0, g1):
                        op = nc.vector.tensor_tensor_reduce(out=dot_out[:, g, :], in0=ea[i][:, g, :], in1=T["we"][:],
                                                            scale=1.0, scalar=0.0, op0=ALU.mult, op1=ALU.add,
                                                            accum_out=new_dots[:, g:g + 1])
                    if g1 == G:
                        op.then_inc(new_dots_ready, 1)
                        v.wait_ge(new_dots_ready, c + 1)
                        nc.vector.tensor_copy(dots[:, ds(LEAD + c * G, G)], new_dots[:]).then_inc(dots_ready, 1)

                def raw_scores():
                    v.wait_ge(gathered[i], 16 * G * (n + 1))
                    v.wait_ge(dots_ready, c + 1 if with_dots else DC)
                    if not first:
                        v.wait_ge(score_ready, c)
                    for g in range(G):
                        op = nc.vector.tensor_tensor(raw[:, g:g + 1], rows[i][:, g, W - 1:W],
                                                     dots[:, ds(LEAD + c * G + g - js[g], 1)], ALU.add)
                    op.then_inc(raw_ready, 1)

                def scores():
                    v.wait_ge(raw_ready, c + 1)
                    if not first:
                        v.wait_ge(score_rows, c)
                    nc.vector.scalar_tensor_tensor(out=score[:], in0=raw[:], scalar=SLOPE, in1=raw[:],
                                                   op0=ALU.mult, op1=ALU.max).then_inc(score_ready, 1)

                def forward():
                    v.wait_ge(score_rows, c + 1)
                    v.wait_ge(masks_loaded[i], 32 * (n + 1))
                    if not first:
                        v.wait_ge(seg_ready, c)
                    nc.vector.tensor_tensor_scan(fwd[:], masks[i][:, 0, :], psA[:, 0:P], -BIG, ALU.add, ALU.max)\
                             .then_inc(fwd_ready, 1)

                def backward():
                    v.wait_ge(fwd_ready, c + 1)
                    if not first:
                        v.wait_ge(seg_a_ready, c)
                    flat = masks[i][:].rearrange("g m i -> g (m i)")
                    nc.vector.tensor_tensor_scan(seg[:, ::-1], flat[:, P:0:-1], fwd[:, ::-1], -BIG, ALU.add, ALU.max)\
                             .then_inc(seg_ready, 1)

                def ends_forward():
                    v.wait_ge(ends_rows, c + 1)
                    if first:
                        v.wait_ge(carry_set, 1)
                    else:
                        v.wait_ge(ends_fwd_ready, c)
                        v.wait_ge(rise_ready, c)
                    carry = no_max[:, 0:1] if first else ends_fwd[1 - i][:, 2 * G - 1:2 * G]
                    nc.vector.tensor_tensor_scan(ends_fwd[i][:], bounds[i][:, 0:2 * G], psX[:, 0:2 * G], carry,
                                                 ALU.add, ALU.max).then_inc(ends_fwd_ready, 1)

                def ends_backward():
                    v.wait_ge(ends_fwd_ready, c + 1)
                    if not first:
                        v.wait_ge(cols_ready, c)
                        v.wait_ge(rise_ready, c)
                    nc.vector.tensor_tensor_scan(ends[:, ::-1], bounds[i][:, 2 * G:0:-1], ends_fwd[i][:, ::-1], -BIG,
                                                 ALU.add, ALU.max).then_inc(ends_ready, 1)

                def open_segment():
                    if not first:
                        v.wait_ge(rise_on_ready, c)
                    nc.vector.tensor_scalar(goes_on[:], bounds[i][:, 0:1], 0.0, None, ALU.is_equal).then_inc(on_ready, 1)
                    v.wait_ge(ends_ready, c + 1)
                    carry = no_max[:, 0:1] if first else ends_fwd[1 - i][:, 2 * G - 1:2 * G]
                    nc.vector.tensor_tensor(rise[:], carry, ends[:, 0:1], ALU.subtract).then_inc(rise_ready, 1)

                def open_rise():
                    v.wait_ge(rise_ready, c + 1)
                    v.wait_ge(on_ready, c + 1)
                    if not first:
                        v.wait_ge(cols_ready, c)
                    nc.vector.tensor_tensor(rise_on[:], rise[:], goes_on[:], ALU.mult).then_inc(rise_on_ready, 1)

                def end_columns():
                    v.wait_ge(cols_ready, c + 1)
                    if not first:
                        v.wait_ge(seg_b_ready, c)
                    nc.vector.tensor_copy(cols[:], psY[0:G, 0:2]).then_inc(cols_copied, 1)

                def first_segments():
                    v.wait_ge(cols_copied, c + 1)
                    v.wait_ge(seg_ready, c + 1)
                    if not first:
                        v.wait_ge(seg_b_ready, c)
                    nc.vector.scalar_tensor_tensor(out=seg_a[:], in0=masks[i][:, 1, :], scalar=cols[:, 0:1], in1=seg[:],
                                                   op0=ALU.add, op1=ALU.max).then_inc(seg_a_ready, 1)

                def last_segments():
                    v.wait_ge(seg_a_ready, c + 1)
                    if not first:
                        v.wait_ge(centred_ready, c)
                    nc.vector.scalar_tensor_tensor(out=seg_b[:], in0=masks[i][:, 2, :], scalar=cols[:, 1:2], in1=seg_a[:],
                                                   op0=ALU.add, op1=ALU.max).then_inc(seg_b_ready, 1)

                def centre():
                    v.wait_ge(seg_b_ready, c + 1)
                    if not first:
                        v.wait_ge(exp_ready, c)
                    nc.vector.tensor_tensor(centred[:], psA[:, 0:P], seg_b[:], ALU.subtract).then_inc(centred_ready, 1)

                dot_steps = [lambda a=a, b=b: edge_dots(a, b) if with_dots else None
                             for a, b in ((0, 3), (3, 6), (6, 9), (9, 12), (12, 14), (14, G))]
                return dot_steps + [
                        raw_scores, scores, forward, backward, ends_forward,
                        ends_backward, lambda: (open_segment(), open_rise()),
                        lambda: (end_columns(), first_segments()), last_segments, centre]

            def rescale_open(i, c, first=False):
                v.wait_ge(rescale_ready, c + 1)
                if not first:
                    v.wait_ge(rescaled, c)
                nc.vector.scalar_tensor_tensor(out=factor[:], in0=T["open_node"][:, ds(c, 1)], scalar=rescale[:, 0:1],
                                               in1=T["other_node"][:, ds(c, 1)], op0=ALU.mult, op1=ALU.add)\
                         .then_inc(factor_ready, 1)
                v.wait_ge(factor_ready, c + 1)

            def steps(i, c, js, scoring, first=False):
                rescale_open(i, c, first)
                if first:
                    v.wait_ge(acc_zero, 3)
                else:
                    v.wait_ge(step_added, c * G)
                at = acc[:, ds(js[0] * W, S)]
                nc.vector.tensor_scalar(at, at, factor[:, 0:1], None, ALU.mult).then_inc(rescaled, 1)
                for g in range(G):
                    if g == 0:
                        v.wait_ge(rescaled, c + 1)
                    else:
                        v.wait_ge(step_added, c * G + g)
                    v.wait_ge(step_summed, c * G + g + 1)
                    at = acc[:, ds(js[g] * W, S)]
                    nc.vector.tensor_tensor(at, sums[g % RING][:, 0:S], at, ALU.add).then_inc(step_added, 1)
                    if scoring:
                        scoring[g]()

            nc.vector.memset(no_max[:], -BIG).then_inc(carry_set, 1)
            nc.vector.memset(dots[:, LEAD + DC * G:], 0.0).then_inc(acc_zero, 1)
            half = acc.shape[1] // 2
            nc.vector.memset(acc[:, 0:half], 0.0).then_inc(acc_zero, 1)
            nc.vector.memset(acc[:, half:], 0.0).then_inc(acc_zero, 1)
            regs = [[v.alloc_register(f"block_{i}_{g}") for g in range(G)] for i in range(2)]

            def load(i, c):
                v.load(regs[i], T["offs"][0:1, ds(c * G, G)])
                return [v.snap(r, min_val=0, max_val=z.node_tiles - 1) for r in regs[i]]

            def two_chunks(c, n, js, first=False, dots_0=True, dots_1=True, last=False):
                next_js = load(1, c + 1)
                steps(0, c, js, score_steps(1, c + 1, n, next_js, with_dots=dots_0), first)
                if last:
                    steps(1, c + 1, next_js, None)
                else:
                    js = load(0, c + 2)
                    steps(1, c + 1, next_js, score_steps(0, c + 2, n + 1, js, with_dots=dots_1))

            js = load(0, 0)
            for step in score_steps(0, 0, 0, js, first=True):
                step()
            two_chunks(0, 0, js, first=True)
            with v.Fori(1, DC // 2 - 1) as n:
                two_chunks(2 * n, n, load(0, 2 * n))
            two_chunks(DC - 2, DC // 2 - 1, load(0, DC - 2), dots_1=False)
            if turns - 1 > DC // 2:
                with v.Fori(DC // 2, turns - 1) as n:
                    two_chunks(2 * n, n, load(0, 2 * n), dots_0=False, dots_1=False)
            two_chunks(C - 2, turns - 1, load(0, C - 2), dots_0=False, last=True)

        @block.scalar
        def _(act):
            def exps(i, c, first=False):
                act.wait_ge(centred_ready, c + 1)
                if not first:
                    act.wait_ge(exp_cols, c)
                nc.scalar.activation(expd[:], centred[:], ACT.Exp).then_inc(exp_ready, 1)
                act.wait_ge(cols_ready, c + 1)
                if not first:
                    act.wait_ge(factor_ready, c)
                nc.scalar.activation(rescale[:], psY[:, 2:3], ACT.Exp).then_inc(rescale_ready, 1)

            def probs(i, c, first=False):
                act.wait_ge(exp_cols, c + 1)
                if not first:
                    act.wait_ge(onehot_ready, (c - 1) * G)
                nc.scalar.activation(prob[i][:], psE[:, 0:G], ACT.Copy).then_inc(prob_ready, 1)
                nc.scalar.activation(neg_prob[i][:], psE[:, 0:G], ACT.Copy, scale=-1.0).then_inc(neg_ready, 1)

            def distance(c, g, k, first=False):
                if not first:
                    act.wait_ge(onehot_ready, c * G + g - 1)
                nc.scalar.activation(dist[:, k % 2, :], T["iota"][:], ACT.Abs, bias=T["neg_pos"][:, ds(c * G + g, 1)])\
                         .then_inc(dist_ready, 1)

            def tile(i, c, g, first=False):
                act.wait_ge(dist_ready, c * G + g + 1)
                if g == 0:
                    act.wait_ge(prob_ready, c + 1)
                    act.wait_ge(neg_ready, c + 1)
                if not first:
                    act.wait_ge(step_summed, c * G + g - RING + 1)
                nc.scalar.activation(onehot[:, g % RING, :], dist[:, g % 2, :], ACT.Relu,
                                     scale=neg_prob[i][:, g:g + 1], bias=prob[i][:, g:g + 1]).then_inc(onehot_ready, 1)

            def chunk(i, c, first=False, last=False):
                for g in range(G):
                    if g + 1 < G:
                        distance(c, g + 1, g + 1, first and g + 1 < 2)
                    elif not last:
                        distance(c + 1, 0, 0)
                    tile(i, c, g, first and g < RING)
                if not last:
                    exps(1 - i, c + 1)
                    probs(1 - i, c + 1, first)

            exps(0, 0, True)
            probs(0, 0, True)
            distance(0, 0, 0, True)
            chunk(0, 0, first=True)
            chunk(1, 1)
            with act.Fori(1, turns - 1) as n:
                chunk(0, 2 * n)
                chunk(1, 2 * n + 1)
            chunk(0, C - 2)
            chunk(1, C - 1, last=True)

        @block.tensor
        def _(pe):
            def turn_scores(c, first=False):
                pe.wait_ge(score_ready, c + 1)
                if not first:
                    pe.wait_ge(centred_ready, c)
                nc.tensor.transpose(psA[:, 0:P], score[:], T["ident"][:]).then_inc(score_rows, 1)

            def turn_ends(c, first=False):
                pe.wait_ge(seg_ready, c + 1)
                if not first:
                    pe.wait_ge(ends_fwd_ready, c)
                pe.sem_inc(z.passed, 1)
                nc.tensor.transpose(psX[:, 0:2 * G:2], seg[:, 0:1], T["ident"][0:G, 0:G])
                nc.tensor.transpose(psX[:, 1:2 * G:2], seg[:, P - 1:P], T["ident"][0:G, 0:G]).then_inc(ends_rows, 1)

            def turn_back(c, first=False):
                pe.wait_ge(ends_ready, c + 1)
                pe.wait_ge(rise_on_ready, c + 1)
                if not first:
                    pe.wait_ge(cols_copied, c)
                    pe.wait_ge(rescale_ready, c)
                pe.sem_inc(z.passed, 1)
                for n in range(2):
                    nc.tensor.transpose(psY[0:G, n:n + 1], ends[:, n:2 * G:2], T["ident"][0:1, 0:1])
                nc.tensor.matmul(psY[:, 2:3], T["ones"][0:1, 0:P], rise_on[:], start=True, stop=True)\
                         .then_inc(cols_ready, 1)

            def turn_exps(c, first=False):
                pe.wait_ge(exp_ready, c + 1)
                if not first:
                    pe.wait_ge(prob_ready, c)
                    pe.wait_ge(neg_ready, c)
                pe.sem_inc(z.passed, 1)
                nc.tensor.transpose(psE[:, 0:G], expd[:], T["ident"][0:G, 0:G]).then_inc(exp_cols, 1)

            def tile(i, c, g, first=False):
                pe.wait_ge(onehot_ready, c * G + g + 1)
                if not first:
                    pe.wait_ge(step_added, c * G + g - RING + 1)
                nc.tensor.matmul(sums[g % RING][:, 0:S], onehot[:, g % RING, :], rows[i][:, g, 0:S],
                                 start=True, stop=True).then_inc(step_summed, 1)

            def chunk(i, c, first=False, last=False):
                for g in range(G):
                    tile(i, c, g, first and g < RING)
                    if not last and g == 8:
                        turn_scores(c + 1)
                    if not last and g == 10:
                        turn_ends(c + 1)
                    if not last and g == 13:
                        turn_back(c + 1)
                if not last:
                    turn_exps(c + 1)

            turn_scores(0, True)
            turn_ends(0, True)
            turn_back(0, True)
            turn_exps(0, True)
            chunk(0, 0, first=True)
            chunk(1, 1)
            with pe.Fori(1, turns - 1) as n:
                chunk(0, 2 * n)
                chunk(1, 2 * n + 1)
            chunk(0, C - 2)
            chunk(1, C - 1, last=True)


def gate(nc, z, x, gate_w, gate_b, T, acc):
    NT, E, K, U, W = z.node_tiles, z.experts, z.k1, z.turn, z.row
    RING = 3
    x1 = lambda t: acc[:, ds(t * W, z.dim)]
    with ExitStack() as ctx:
        sb = lambda name, shape, dt=F32: ctx.enter_context(nc.sbuf_tensor(name, shape, dt))
        many = lambda name, shape: [sb(f"{name}{u}", shape) for u in range(U)]
        sem = z.semaphore
        xt, gnn, stats, mv, std, xn, xnT = map(many, (
            "gate_x", "gate_gnn", "gate_stats", "gate_mv", "gate_std", "gate_xn", "gate_xnT"), (
            [P, z.dim], [P, z.dim], [P, 6], [P, 2], [P, 1], [P, z.dim], [P, K, P]))
        gw, gb = sb("gate_weights", [P, K, E]), sb("gate_bias", [P, U, E])
        den, inv = sb("den", [P, NT]), sb("inv", [P, NT])
        logits = sb("logits", [P, NT, E])
        psT = [ctx.enter_context(nc.psum_tensor(f"gate_psT{i}", [P, K, P], F32)) for i in range(RING)]
        psL = ctx.enter_context(nc.psum_tensor("gate_psL", [P, U, E], F32))
        psR = ctx.enter_context(nc.psum_tensor("route_ps", [P, 4, 512], F32))
        w_loaded, inv_ready = sem("gate_w_loaded"), sem("inv_ready")
        x_loaded, before_x = z.rows_in, 16 * z.turns
        (gnn_ready, x1_ready, stats_ready, mv_ready, std_ready, rstd_ready, mean_ready, xn_ready, xn_turned,
         xnT_ready, l_ready, logit_ready) = map(sem, (
             "g_gnn_ready", "g_x1_ready", "g_stats_ready", "g_mv_ready", "g_std_ready", "g_rstd_ready",
             "g_mean_ready", "g_xn_ready", "g_xn_turned", "g_xnT_ready", "g_l_ready", "g_logit_ready"))
        chain, shifted, exped, hot_ready, counted = (
            sem("route_chain"), sem("logits_shifted"), sem("logits_exp"), sem("hot_ready"), sem("counted"))
        tri = sb("tri_incl", [P, P])
        best, total, first_e = sb("best", [P, NT]), sb("total", [P, NT]), sb("first_e", [P, NT])
        w_a, w_b, w_c = sb("route_a", [P, NT, E]), sb("route_b", [P, NT, E]), sb("route_c", [P, NT, E])
        expert_no = sb("expert_no", [P, NT, E])
        hot = sb("hot", [P, E, NT])
        keep = sb("route_keep", [P, E, NT])
        before, after = sb("before", [P, E, NT]), sb("after", [P, E, NT])
        place, kept, slot_f = sb("place", [P, NT]), sb("kept", [P, NT]), sb("slot_f", [P, NT])
        block = ctx.enter_context(nc.Block())

        @block.sync
        def _(sp):
            sp.dma_start(gw[:], gate_w.rearrange("(k p) e -> p k e", p=P)).then_inc(w_loaded, 16)
            sp.dma_start(gb[:], gate_b.rearrange("(a b e) -> a b e", a=1, b=1).to_broadcast([P, U, E])).then_inc(w_loaded, 16)

            def turn(n, first, last=False):
                for u in range(U):
                    if not first:
                        sp.wait_ge(x1_ready, (n - 1) * U + u + 1)
                    load_rows(sp, z, xt[u][:], x, n * U + u, last and u == U - 1, x_loaded[u])

            turn(0, True)
            with sp.Fori(1, z.turns - 1) as n:
                turn(n, False)
            turn(z.turns - 1, False, True)

        @block.scalar
        def _(act):
            def relus(n, first):
                for u in range(U):
                    if not first:
                        act.wait_ge(x1_ready, (n - 1) * U + u + 1)
                    nc.scalar.activation(gnn[u][:], x1(n * U + u), ACT.Relu, scale=inv[:, ds(n * U + u, 1)])\
                             .then_inc(gnn_ready, 1)

            def turn(n, first, last=False):
                for u in range(U):
                    act.wait_ge(mv_ready, n * U + u + 1)
                    if not first:
                        act.wait_ge(rstd_ready, (n - 1) * U + u + 1)
                    nc.scalar.activation(std[u][:], mv[u][:, 1:2], ACT.Sqrt, bias=T["eps"][:, 0:1]).then_inc(std_ready, 1)
                if not last:
                    relus(n + 1, False)
                for u in range(U):
                    act.wait_ge(xn_turned, n * U + u + 1)
                    if not first:
                        act.wait_ge(l_ready, (n - 1) * U + u + 1)
                    nc.scalar.copy(xnT[u][:], psT[u % RING][:]).then_inc(xnT_ready, 1)

            act.wait_ge(inv_ready, 1)
            relus(0, True)
            turn(0, True)
            with act.Fori(1, z.turns - 1) as n:
                turn(n, False)
            turn(z.turns - 1, False, True)
            act.wait_ge(shifted, 1)
            nc.scalar.activation(w_b[:], w_a[:], ACT.Exp).then_inc(exped, 1)

        @block.vector
        def _(v):
            def add_bias(n):
                v.wait_ge(l_ready, (n + 1) * U)
                nc.vector.tensor_tensor(logits[:, ds(n * U, U), :], psL[:], gb[:], ALU.add).then_inc(logit_ready, 1)

            def turn(n, first):
                for u in range(U):
                    v.wait_ge(x_loaded[u], before_x + 16 * n + 16)
                    v.wait_ge(gnn_ready, n * U + u + 1)
                    nc.vector.tensor_tensor(x1(n * U + u), xt[u][:], gnn[u][:], ALU.add).then_inc(x1_ready, 1)
                for u in range(U):
                    v.wait_ge(x1_ready, n * U + u + 1)
                    v.sem_inc(z.passed, 1)
                    nc.vector.bn_stats(stats[u][:], x1(n * U + u)).then_inc(stats_ready, 1)
                for u in range(U):
                    v.wait_ge(stats_ready, n * U + u + 1)
                    v.sem_inc(z.passed, 1)
                    nc.vector.bn_aggr(mv[u][:], stats[u][:]).then_inc(mv_ready, 1)
                for u in range(U):
                    v.wait_ge(mv_ready, n * U + u + 1)
                    nc.vector.tensor_copy(T["mean"][:, ds(n * U + u, 1)], mv[u][:, 0:1]).then_inc(mean_ready, 1)
                if not first:
                    add_bias(n - 1)
                for u in range(U):
                    v.wait_ge(std_ready, n * U + u + 1)
                    nc.vector.reciprocal(T["rstd"][:, ds(n * U + u, 1)], std[u][:]).then_inc(rstd_ready, 1)
                for u in range(U):
                    v.wait_ge(mean_ready, n * U + u + 1)
                    v.wait_ge(rstd_ready, n * U + u + 1)
                    if not first:
                        v.wait_ge(xn_turned, (n - 1) * U + u + 1)
                    nc.vector.tensor_scalar(xn[u][:], x1(n * U + u), T["mean"][:, ds(n * U + u, 1)],
                                            T["rstd"][:, ds(n * U + u, 1)], ALU.subtract, ALU.mult).then_inc(xn_ready, 1)

            done = [0]

            def link(instruction):
                done[0] += 1
                instruction.then_inc(chain, 1)
                v.wait_ge(chain, done[0])

            link(nc.vector.tensor_scalar_add(den[:], acc[:].rearrange("p (t w) -> p w t", w=W)[:, z.dim, :], 1e-16))
            nc.vector.reciprocal(inv[:], den[:]).then_inc(inv_ready, 1)
            v.wait_ge(w_loaded, 32)
            node_turns(v, z, turn)
            add_bias(z.turns - 1)
            v.wait_ge(logit_ready, z.turns)
            wide = lambda t: t[:].unsqueeze(2).to_broadcast([P, NT, E])
            link(nc.vector.tensor_scalar(tri[:], T["iota"][:, 0:P], T["part"][:, 0:1], None, ALU.is_ge))
            link(nc.vector.memset(keep[:], 1.0))
            link(nc.vector.memset(keep[:, :, 0:1], 0.0))
            for e in range(E):
                nc.vector.memset(expert_no[:, :, e:e + 1], float(e))
            link(nc.vector.tensor_reduce(best[:], logits[:], AX.X, ALU.max))
            nc.vector.tensor_tensor(w_a[:], logits[:], wide(best), ALU.subtract).then_inc(shifted, 1)
            v.wait_ge(exped, 1)
            link(nc.vector.tensor_reduce(total[:], w_b[:], AX.X, ALU.add))
            link(nc.vector.reciprocal(T["weight"][:], total[:]))
            link(nc.vector.tensor_scalar(w_b[:], w_a[:], 0.0, float(E), ALU.not_equal, ALU.mult))
            link(nc.vector.tensor_tensor(w_c[:], w_b[:], expert_no[:], ALU.add))
            link(nc.vector.tensor_reduce(first_e[:], w_c[:], AX.X, ALU.min))
            link(nc.vector.tensor_tensor(hot[:].rearrange("p e t -> p t e"), expert_no[:], wide(first_e), ALU.is_equal))
            nc.vector.memset(place[:], 0.0).then_inc(hot_ready, 1)
            v.wait_ge(counted, 1)
            h = E // 2
            for n in range(2):
                link(nc.vector.tensor_copy(before[:, n * h:(n + 1) * h, :],
                                           psR[:, 2 + n, 0:h * NT].rearrange("p (e t) -> p e t", e=h)))
            f = lambda t: t[:].rearrange("p e t -> p (e t)")
            link(nc.vector.tensor_tensor_scan(f(after), f(keep), f(before), 0.0, ALU.mult, ALU.add))
            link(nc.vector.tensor_tensor(after[:], after[:], before[:], ALU.subtract))
            for n in range(2):
                link(nc.vector.tensor_tensor(before[:, n * h:(n + 1) * h, :], after[:, n * h:(n + 1) * h, :],
                                             psR[:, n, 0:h * NT].rearrange("p (e t) -> p e t", e=h), ALU.add))
            link(nc.vector.tensor_tensor(after[:], before[:], hot[:], ALU.mult))
            link(nc.vector.tensor_reduce(place[:], after[:].rearrange("p e t -> p t e"), AX.X, ALU.add))
            link(nc.vector.tensor_scalar(kept[:], place[:], z.capacity + 0.5, None, ALU.is_lt))
            link(nc.vector.tensor_tensor(T["weight"][:], T["weight"][:], kept[:], ALU.mult))
            link(nc.vector.scalar_tensor_tensor(out=slot_f[:], in0=first_e[:], scalar=float(z.slots), in1=place[:],
                                                op0=ALU.mult, op1=ALU.add))
            link(nc.vector.tensor_scalar(kept[:], kept[:], -1e6, 1e6 - 1, ALU.mult, ALU.add))
            link(nc.vector.tensor_tensor(slot_f[:], slot_f[:], kept[:], ALU.add))
            nc.vector.tensor_copy(T["slot"][:], slot_f[:])

        @block.tensor
        def _(pe):
            def turn(n, first):
                for u in range(U):
                    pe.wait_ge(xn_ready, n * U + u + 1)
                    if not (first and u < RING):
                        pe.wait_ge(xnT_ready, behind(z, n, u, RING))
                    for k in range(K):
                        last = nc.tensor.transpose(psT[u % RING][:, k, :], xn[u][:, k * P:(k + 1) * P],
                                                   T["ident"][:])
                    last.then_inc(xn_turned, 1)
                if not first:
                    pe.wait_ge(logit_ready, n)
                for u in range(U):
                    pe.wait_ge(xnT_ready, n * U + u + 1)
                    for k in range(K):
                        last = nc.tensor.matmul(psL[:, u, :], xnT[u][:, k, :], gw[:, k, :], start=(k == 0), stop=(k == K - 1))
                    last.then_inc(l_ready, 1)

            pe.wait_ge(w_loaded, 32)
            node_turns(pe, z, turn)
            pe.wait_ge(hot_ready, 1)
            h = E // 2
            for n in range(2):
                half = hot[:, n * h:(n + 1) * h, :].rearrange("p e t -> p (e t)")
                nc.tensor.matmul(psR[:, n, 0:h * NT], tri[:], half, start=True, stop=True)
                last = nc.tensor.matmul(psR[:, 2 + n, 0:h * NT], T["ones"][:, 0:P], half, start=True, stop=True)
            last.then_inc(counted, 1)


def dispatch(nc, z, T, D, x1):
    NT, U = z.node_tiles, z.turn
    with ExitStack() as ctx:
        sb = lambda name, shape, dt=F32: ctx.enter_context(nc.sbuf_tensor(name, shape, dt))
        sem = z.semaphore
        out = [sb(f"sent_row{u}", [P, z.dim]) for u in range(U)]
        idx = [sb(f"sent_idx{u}", [P, 1], I32) for u in range(U)]
        row_ready, idx_ready = sem("sent_row_ready"), sem("sent_idx_ready")
        sent = z.rows_pool
        block = ctx.enter_context(nc.Block())

        @block.vector
        def _(v):
            def turn(n, first):
                for u in range(U):
                    if not first:
                        v.wait_ge(sent[u], 16 * n)
                    t = n * U + u
                    nc.vector.tensor_scalar(out[u][:], x1[:, ds(t * z.row, z.dim)], T["mean"][:, ds(t, 1)],
                                            T["rstd"][:, ds(t, 1)], ALU.subtract, ALU.mult).then_inc(row_ready, 1)

            node_turns(v, z, turn)

        @block.gpsimd
        def _(pool):
            def turn(n, first):
                for u in range(U):
                    if not first:
                        pool.wait_ge(sent[u], 16 * n)
                    nc.gpsimd.tensor_copy(idx[u][:], T["slot"][:, ds(n * U + u, 1)]).then_inc(idx_ready, 1)
                    pool.wait_ge(idx_ready, n * U + u + 1)
                    pool.wait_ge(row_ready, n * U + u + 1)
                    pool.sem_inc(z.passed, 1)
                    pool.indirect_dma_start(D["buf"][:, :], bass.IndirectOffsetOnAxis(idx[u][:, 0:1], 0), out[u][:], None,
                                            bounds_check=z.experts * z.slots - 1, oob_is_err=False).then_inc(sent[u], 16)

            node_turns(pool, z, turn)
            for u in range(U):
                pool.wait_ge(sent[u], 16 * z.turns)


def experts(nc, z, w1, b1, w2, b2, T, D):
    E, NB, K1, K2, TB = z.experts, z.blocks, z.k1, z.k2, z.block // P
    HR = 4
    turns = E // 2
    with ExitStack() as ctx:
        sb = lambda name, shape, dt=F32: ctx.enter_context(nc.sbuf_tensor(name, shape, dt))
        sem = z.semaphore
        pair = lambda name: [sem(f"{name}{i}") for i in range(2)]
        ps = lambda name, k: [ctx.enter_context(nc.psum_tensor(f"{name}{i}", [P, 512], F32)) for i in range(k)]
        w1s = [sb(f"w1s{i}", [P, K1, z.hidden]) for i in range(2)]
        w2s = [sb(f"w2s{i}", [P, K2, z.dim]) for i in range(2)]
        b1s = [sb(f"b1s{i}", [P, K2]) for i in range(2)]
        b2s = [sb(f"b2s{i}", [P, z.dim]) for i in range(2)]
        xs = [sb(f"slot_rows{i}", [P, TB, z.dim]) for i in range(2)]
        xT = sb("slot_xT", [P, K1, z.block])
        hT = sb("slot_hT", [P, K2, z.block])
        ys = [sb(f"slot_y{i}", [P, TB, z.dim]) for i in range(2)]
        psT, psH, psY = ps("exp_psT", 2), ps("exp_psH", HR), ps("exp_psY", 2)
        w_loaded, x_loaded, y_saved = pair("w_loaded"), pair("slots_loaded"), pair("y_saved")
        x_turned, xT_ready, h_ready, hT_ready, y_ready, y_copied = (
            sem("x_turned"), sem("xT_ready"), sem("h_summed"), sem("hT_ready"), sem("y_summed"), sem("y_copied"))
        block = ctx.enter_context(nc.Block())

        def number(m, i, b):
            return 2 * NB * m + i * NB + b

        def uses(m, i, b):
            return NB * m + (i * NB + b) // 2 + 1

        def all_blocks(engine, one, before=None):
            for i in range(2):
                if before:
                    before(0, i, True)
                for b in range(NB):
                    one(0, i, b, True)
            with engine.Fori(1, turns) as m:
                for i in range(2):
                    if before:
                        before(m, i, False)
                    for b in range(NB):
                        one(m, i, b, False)

        @block.sync
        def _(sp):
            w1_v = w1.rearrange("e (k p) f -> (e k) p f", p=P)
            w2_v = w2.rearrange("e (k p) n -> (e k) p n", p=P)
            b1_v = b1.rearrange("e (k p) -> (e k) p", p=P)

            def load_w(m, i, first):
                e = 2 * m + i
                if not first:
                    sp.wait_ge(y_copied, (2 * m + i - 1) * NB * TB)
                sp.dma_start(w1s[i][:], w1_v[ds(e * K1, K1)].rearrange("k p f -> p k f")).then_inc(w_loaded[i], 16)
                sp.dma_start(w2s[i][:], w2_v[ds(e * K2, K2)].rearrange("k p n -> p k n")).then_inc(w_loaded[i], 16)
                with nc.allow_non_contiguous_dma(reason="1024 biases, one per partition and column"):
                    sp.dma_start(b1s[i][:], b1_v[ds(e * K2, K2)].rearrange("k p -> p k")).then_inc(w_loaded[i], 16)
                sp.dma_start(b2s[i][:], b2[ds(e, 1), :].to_broadcast([P, z.dim])).then_inc(w_loaded[i], 16)

            def load_x(m, i, b, first):
                i2 = (i * NB + b) % 2
                if not (first and i * NB + b < 2):
                    sp.wait_ge(x_turned, (number(m, i, b) - 1) * K1)
                sp.dma_start(xs[i2][:], D["buf"][ds(number(m, i, b) * z.block, z.block), :]
                             .rearrange("(t p) n -> p t n", p=P)).then_inc(x_loaded[i2], 16)

            all_blocks(sp, load_x, load_w)

        @block.tensor
        def _(pe):
            def one(m, i, b, first):
                blk, i2, start = number(m, i, b), (i * NB + b) % 2, first and i * NB + b == 0
                pe.wait_ge(x_loaded[i2], 16 * uses(m, i, b))
                for k in range(K1):
                    if not start:
                        pe.wait_ge(xT_ready, (blk - 1) * K1 + k + 1)
                    for t in range(TB):
                        last = nc.tensor.transpose(psT[k % 2][:, t * P:(t + 1) * P], xs[i2][:, t, k * P:(k + 1) * P],
                                                   T["ident"][:])
                    last.then_inc(x_turned, 1)
                if b == 0:
                    pe.wait_ge(w_loaded[i], 64 * (m + 1))
                pe.wait_ge(xT_ready, (blk + 1) * K1)
                for f in range(K2):
                    if not (start and f < HR):
                        pe.wait_ge(hT_ready, blk * K2 + f - HR + 1)
                    for k in range(K1):
                        last = nc.tensor.matmul(psH[f % HR][:], w1s[i][:, k, f * P:(f + 1) * P], xT[:, k, :],
                                                start=(k == 0), stop=(k == K1 - 1))
                    last.then_inc(h_ready, 1)
                pe.wait_ge(hT_ready, (blk + 1) * K2)
                for t in range(TB):
                    if not (start and t < 2):
                        pe.wait_ge(y_copied, blk * TB + t - 1)
                    for k in range(K2):
                        last = nc.tensor.matmul(psY[t % 2][:, 0:z.dim], hT[:, k, t * P:(t + 1) * P], w2s[i][:, k, :],
                                                start=(k == 0), stop=(k == K2 - 1))
                    last.then_inc(y_ready, 1)

            all_blocks(pe, one)

        @block.scalar
        def _(act):
            def one(m, i, b, first):
                blk = number(m, i, b)
                for f in range(K2):
                    act.wait_ge(h_ready, blk * K2 + f + 1)
                    if f == 0 and not (first and i * NB + b == 0):
                        act.wait_ge(y_ready, blk * TB)
                    nc.scalar.activation(hT[:, f, :], psH[f % HR][:], ACT.Relu, bias=b1s[i][:, f:f + 1])\
                             .then_inc(hT_ready, 1)

            all_blocks(act, one)

        @block.vector
        def _(v):
            def one(m, i, b, first):
                blk, i2 = number(m, i, b), (i * NB + b) % 2
                for k in range(K1):
                    v.wait_ge(x_turned, blk * K1 + k + 1)
                    if k == 0 and not (first and i * NB + b == 0):
                        v.wait_ge(h_ready, blk * K2)
                    nc.vector.tensor_copy(xT[:, k, :], psT[k % 2][:]).then_inc(xT_ready, 1)
                if not (first and i * NB + b < 2):
                    v.wait_ge(y_saved[i2], 16 * (uses(m, i, b) - 1))
                for t in range(TB):
                    v.wait_ge(y_ready, blk * TB + t + 1)
                    nc.vector.tensor_tensor(ys[i2][:, t, :], psY[t % 2][:, 0:z.dim], b2s[i][:], ALU.add).then_inc(y_copied, 1)

            all_blocks(v, one)

        @block.gpsimd
        def _(pool):
            def one(m, i, b, first):
                blk, i2 = number(m, i, b), (i * NB + b) % 2
                pool.wait_ge(y_copied, (blk + 1) * TB)
                pool.dma_start(D["y"][ds(blk * z.block, z.block), :].rearrange("(t p) n -> p t n", p=P), ys[i2][:])\
                    .then_inc(y_saved[i2], 16)

            all_blocks(pool, one)
            for i2 in range(2):
                pool.wait_ge(y_saved[i2], 16 * NB * turns)


def combine(nc, z, T, D, x1, out):
    NT, U = z.node_tiles, z.turn
    with ExitStack() as ctx:
        many = lambda name, shape, dt=F32: [ctx.enter_context(nc.sbuf_tensor(f"{name}{u}", shape, dt)) for u in range(U)]
        sem = z.semaphore
        y, ty, low, side, res = (many(n, [P, z.dim]) for n in ("y", "ty", "y_low", "y_side", "res"))
        finite = many("finite", [P, z.dim], I32)
        idx = many("y_idx", [P, 1], I32)
        y_set, idx_ready, scaled, low_ready, side_ready, finite_ready, res_ready, picked, summed = map(
            sem, ("y_set", "y_idx_ready", "y_scaled", "y_low_ready", "y_side_ready", "y_finite_ready",
                  "res_ready", "y_picked", "res_summed"))
        got, saved = z.rows_pool, z.rows_out
        before = 16 * z.turns
        block = ctx.enter_context(nc.Block())

        @block.gpsimd
        def _(pool):
            def turn(n, first):
                for u in range(U):
                    if not first:
                        pool.wait_ge(scaled, (n - 1) * U + u + 1)
                    else:
                        nc.gpsimd.memset(y[u][:], 0.0).then_inc(y_set, 1)
                        pool.wait_ge(y_set, u + 1)
                    nc.gpsimd.tensor_copy(idx[u][:], T["slot"][:, ds(n * U + u, 1)]).then_inc(idx_ready, 1)
                    pool.wait_ge(idx_ready, n * U + u + 1)
                    pool.sem_inc(z.passed, 1)
                    pool.indirect_dma_start(y[u][:], None, D["y"][:, :], bass.IndirectOffsetOnAxis(idx[u][:, 0:1], 0),
                                            bounds_check=z.experts * z.slots - 1, oob_is_err=False).then_inc(got[u], 16)

            node_turns(pool, z, turn)

        @block.scalar
        def _(act):
            def turn(n, first):
                for u in range(U):
                    act.wait_ge(got[u], before + 16 * n + 16)
                    if not first:
                        act.wait_ge(picked, (n - 1) * U + u + 1)
                    nc.scalar.activation(ty[u][:], y[u][:], ACT.Copy, scale=T["weight"][:, ds(n * U + u, 1)])\
                             .then_inc(scaled, 1)
                for u in range(U):
                    act.wait_ge(side_ready, n * U + u + 1)
                    if not first:
                        act.wait_ge(summed, (n - 1) * U + u + 1)
                    nc.scalar.activation(res[u][:], side[u][:], ACT.Copy, scale=1e4).then_inc(res_ready, 1)

            node_turns(act, z, turn)

        @block.vector
        def _(v):
            def turn(n, first):
                for u in range(U):
                    v.wait_ge(scaled, n * U + u + 1)
                    if not first:
                        v.wait_ge(saved[u], before + 16 * n)
                    nc.vector.tensor_scalar(low[u][:], ty[u][:], -F32_MAX, None, ALU.is_lt).then_inc(low_ready, 1)
                    nc.vector.tensor_scalar(finite[u][:], ty[u][:], 0.0, 0.0, ALU.mult, ALU.is_equal)\
                             .then_inc(finite_ready, 1)
                for u in range(U):
                    v.wait_ge(low_ready, n * U + u + 1)
                    if not first:
                        v.wait_ge(res_ready, (n - 1) * U + u + 1)
                    nc.vector.scalar_tensor_tensor(out=side[u][:], in0=ty[u][:], scalar=F32_MAX, in1=low[u][:],
                                                   op0=ALU.is_gt, op1=ALU.subtract).then_inc(side_ready, 1)
                for u in range(U):
                    v.wait_ge(res_ready, n * U + u + 1)
                    v.wait_ge(finite_ready, n * U + u + 1)
                    v.sem_inc(z.passed, 1)
                    nc.vector.copy_predicated(res[u][:], finite[u][:], ty[u][:]).then_inc(picked, 1)
                for u in range(U):
                    v.wait_ge(picked, n * U + u + 1)
                    nc.vector.tensor_tensor(low[u][:], res[u][:], x1[:, ds((n * U + u) * z.row, z.dim)], ALU.add)\
                             .then_inc(summed, 1)

            node_turns(v, z, turn)

        @block.sync
        def _(sp):
            def save(n, u, last=False):
                sp.wait_ge(summed, n * U + u + 1)
                if last:
                    sp.dma_start(out[(NT - 1) * P:z.nodes, :], low[u][0:z.last_rows, :]).then_inc(saved[u], 16)
                else:
                    sp.dma_start(out[ds((n * U + u) * P, P), :], low[u][:]).then_inc(saved[u], 16)

            with sp.Fori(0, z.turns - 1) as n:
                for u in range(U):
                    save(n, u)
            for u in range(U):
                save(z.turns - 1, u, last=(u == U - 1))
            for u in range(U):
                sp.wait_ge(saved[u], before + 16 * z.turns)


def gnn_moe(nc, x, src, dst, edge_attr, Wn, bn, We, be, attn, gate_w, gate_b, w1, b1, w2, b2, out):
    z = Sizes(x, src, edge_attr, w1)
    with ExitStack() as ctx:
        z.semaphore = lambda name: ctx.enter_context(nc.semaphore(name))
        z.passed = z.semaphore("passed")
        z.rows_in = [z.semaphore(f"rows_in{u}") for u in range(z.turn)]
        z.rows_pool = [z.semaphore(f"rows_pool{u}") for u in range(z.turn)]
        z.rows_out = [z.semaphore(f"rows_out{u}") for u in range(z.turn)]
        sb = lambda name, shape, dt=F32: ctx.enter_context(nc.sbuf_tensor(name, shape, dt))
        dram = lambda name, shape, dt=F32: nc.dram_tensor(name, shape, dt, kind="Internal").ap()
        D = {
            "src": dram("src_padded", [1, z.pad_edges], I32),
            "dst": dram("dst_padded", [1, z.pad_edges], I32),
            "turns": dram("tile_turns", [z.table]),
            "tails": dram("step_tails", [z.table + 1]),
            "masks": dram("segment_masks", [z.table, 3 * P]),
            "bounds": dram("row_bounds", [z.table + 1, 2]),
            "offs": dram("step_blocks", [z.table], I32),
            "rels": dram("first_positions", [z.table]),
            "table": dram("node_rows", [z.nodes, z.row]),
            "buf": dram("expert_rows", [z.experts * z.slots, z.dim]),
            "y": dram("expert_out", [z.experts * z.slots, z.dim]),
        }
        T = {
            "iota_i": sb("iota_i", [P, P], I32), "part_i": sb("part_i", [P, 1], I32),
            "iota": sb("iota", [P, P]), "part": sb("part", [P, 1]),
            "ones": sb("ones", [P, P]), "ident": sb("ident", [P, P]), "eps": sb("eps", [P, 1]),
            "mean": sb("mean", [P, z.node_tiles]), "rstd": sb("rstd", [P, z.node_tiles]),
            "weight": sb("expert_weight", [P, z.node_tiles]), "slot": sb("slot", [P, z.node_tiles], I32),
        }
        acc = sb("node_sums", [P, z.node_tiles * z.row])
        with ExitStack() as gnn:
            sb = lambda name, shape, dt=F32: gnn.enter_context(nc.sbuf_tensor(name, shape, dt))
            T |= {
                "neg_pos": sb("neg_pos", [P, z.table]), "src": sb("src_tiles", [P, z.table], I32),
                "offs": sb("node_blocks", [1, z.table], I32),
                "open_node": sb("open_node", [P, z.chunks]), "other_node": sb("other_node", [P, z.chunks]),
                "we": sb("we_attn", [P, z.edge_dim]),
            }
            step_tables(nc, z, src, dst, T, D)
            with nc.sbuf_tensor("wn_t", [P, z.k1, z.row], F32) as wn_t, \
                    nc.sbuf_tensor("bias_row", [P, z.row], F32) as bias_row:
                T |= {"wn": wn_t, "bias": bias_row}
                weights(nc, z, Wn, bn, We, be, attn, T)
                node_table(nc, z, x, T, D)
            edges(nc, z, edge_attr, T, D, acc)
        gate(nc, z, x, gate_w, gate_b, T, acc)
        dispatch(nc, z, T, D, acc)
        experts(nc, z, w1, b1, w2, b2, T, D)
        combine(nc, z, T, D, acc, out)


INPUTS = ["x", "src", "dst", "edge_attr_128", "L0_gnn_Wn", "L0_gnn_bn", "L0_gnn_We", "L0_gnn_be", "L0_gnn_attn",
          "L0_ffn_gate_w", "L0_ffn_gate_b", "L0_ffn_w1", "L0_ffn_b1", "L0_ffn_w2", "L0_ffn_b2"]


def kernel(**inputs):
    import numpy as np
    import concourse.bacc as bacc
    from concourse.bass_utils import run_bass_kernel_spmd

    nc = bacc.Bacc("TRN2", target_bir_lowering=False, num_devices=1)
    arrays, args = {}, []
    for name in INPUTS:
        a = np.ascontiguousarray(inputs[name])
        if name in ("src", "dst"):
            a = a.reshape(1, -1)
        arrays[f"in_{name}"] = a
        args.append(nc.dram_tensor(f"in_{name}", a.shape, mybir.dt.from_np(a.dtype), kind="ExternalInput").ap())
    shape = inputs["x"].shape
    args.append(nc.dram_tensor("out", shape, F32, kind="ExternalOutput").ap())
    gnn_moe(nc, *args)
    r = run_bass_kernel_spmd(nc, [arrays], core_ids=[0])
    return r.results[0]["out"]
```

```python
from contextlib import ExitStack

import concourse.bass as bass
from concourse import mybir

F32 = mybir.dt.float32
I32 = mybir.dt.int32
F32R = mybir.dt.float32r
ALU = mybir.AluOpType
ACT = mybir.ActivationFunctionType
AX = mybir.AxisListType
ds = bass.ds

P = 128
BIG = 1e30
CHUNK_STEPS = 16
SLOPE = 0.01
EPS = 1e-5
F32_MAX = 3.4028234663852886e38


def ceil_div(a, b):
    return -(-a // b)


class Sizes:

    def __init__(self, x, src, edge_attr, w1):
        self.nodes, self.dim = x.shape
        self.edges = src.shape[1]
        self.edge_dim = edge_attr.shape[1]
        self.experts, _, self.hidden = w1.shape
        self.node_tiles = 2 * ceil_div(self.nodes, 2 * P)
        self.last_rows = self.nodes - (self.node_tiles - 1) * P
        assert 0 < self.last_rows < P and self.dim == 2 * P and self.edge_dim == P
        self.tiles = ceil_div(self.edges, P)
        self.last_edges = self.edges - (self.tiles - 1) * P
        self.dot_chunks = ceil_div(self.tiles, CHUNK_STEPS)
        self.steps = self.tiles + self.node_tiles - 1
        self.chunks = ceil_div(self.steps, CHUNK_STEPS)
        assert self.last_edges < P and self.chunks > self.dot_chunks > 6
        self.step_blocks = ceil_div(self.chunks * CHUNK_STEPS, P)
        self.table = self.step_blocks * P
        self.pad_edges = self.table * P
        self.row = self.dim + 2
        self.capacity = max(1, ceil_div(5 * self.nodes, 4 * self.experts))
        self.block = 512
        self.blocks = ceil_div(self.capacity, self.block)
        self.slots = self.blocks * self.block
        self.k1 = self.dim // P
        self.k2 = self.hidden // P
        self.turn = max(u for u in range(1, 8) if self.node_tiles % u == 0)
        self.turns = self.node_tiles // self.turn
        assert self.turns > 2


def step_tables(nc, z, src, dst, T, D):
    B, K = z.step_blocks, z.table
    pad = z.pad_edges - z.edges
    pad_node = z.node_tiles * P - 1
    with ExitStack() as ctx:
        sb = lambda name, shape, dt=F32: ctx.enter_context(nc.sbuf_tensor(name, shape, dt))
        sem = z.semaphore
        pad_m, pad_r = pad // P, pad % P
        pads = sb("pads", [P, max(pad_m, P)], I32)
        zero_pads = sb("zero_pads", [P, max(pad_m, P)], I32)
        number_i, number = sb("number_i", [P, B], I32), sb("number", [P, B])
        ends_i, ends = sb("tile_ends_i", [P, 2, B], I32), sb("tile_ends", [P, 3, B])
        turns_all = sb("turns_all", [P, K])
        less = sb("less", [P, K])
        tile_f, tile_i = sb("tile_of_step", [P, B]), sb("tile_of_step_i", [P, B], I32)
        block_f, shift, at_f = sb("block_of_step", [P, B]), sb("shift", [P, B]), sb("first_at", [P, B])
        near, column = sb("near", [P, B]), sb("column", [P, B])
        near_i = sb("near_i", [P, 2, B], I32)
        before = sb("tail_before", [P, B])
        rows_i = sb("rows_i", [P, 2, B, P], I32)
        rows = sb("rows", [P, 2, B, P])
        starts = sb("starts", [P, B, P])
        masks = sb("masks", [P, B, 3, P])
        bounds = sb("bounds", [P, B, 2])
        src_cols = sb("src_cols", [P, K], I32)
        ps = ctx.enter_context(nc.psum_tensor("table_ps", [P, 4, 512], F32))
        pad_set, padded, ends_loaded, chain, turns_ready, turns_saved, turns_loaded, index_ready = map(sem, (
            "pads_set", "padded", "ends_loaded", "table_chain", "turns_ready", "turns_saved", "turns_loaded",
            "index_ready"))
        offs_saved = sem("offs_saved")
        rows_loaded, tails_ready, tails_saved, before_loaded, masks_ready, saved, small_ready, rel_loaded = map(sem, (
            "rows_loaded", "tails_ready", "tails_saved", "before_loaded", "masks_ready", "tables_saved",
            "small_ready", "small_loaded"))
        consts, pos_ready, turned, evacuated = map(sem, ("consts_ready", "pos_ready", "turned", "evacuated"))
        block = ctx.enter_context(nc.Block())
        by_q = lambda d, at=0: d[at:at + K].rearrange("(b q) -> q b", q=P)
        row = lambda d: d.rearrange("(a t) -> a t", a=1)

        @block.sync
        def _(sp):
            sp.wait_ge(pad_set, 3)
            sp.dma_start(D["dst"][0:1, 0:z.edges], dst).then_inc(padded, 16)
            sp.dma_start(D["src"][0:1, 0:z.edges], src).then_inc(padded, 16)
            sent = 32
            for d, value in ((D["dst"], pads), (D["src"], zero_pads)):
                at = z.edges + P * pad_m
                sp.dma_start(d[0, z.edges:at].rearrange("(p m) -> p m", p=P), value[:, 0:pad_m]).then_inc(padded, 16)
                sent += 16
                if pad_r:
                    sp.dma_start(d[0:1, at:at + pad_r], value[0:1, 0:pad_r]).then_inc(padded, 16)
                    sent += 16
            sp.dma_start(row(D["tails"])[:, 0:1], T["ones"][0:1, 0:1]).then_inc(padded, 16)
            sp.wait_ge(padded, sent + 16)
            with nc.allow_non_contiguous_dma(reason="one element per tile or step"):
                sp.dma_start(ends_i[:, 0, :], D["dst"][0, :].rearrange("(b q i) -> q b i", q=P, i=P)[:, :, P - 1])\
                  .then_inc(ends_loaded, 16)
                sp.wait_ge(turns_ready, 1)
                sp.dma_start(by_q(D["turns"]), ends[:, 2, :]).then_inc(turns_saved, 16)
                sp.wait_ge(turns_saved, 16)
                sp.dma_start(turns_all[:], row(D["turns"]).to_broadcast([P, K])).then_inc(turns_loaded, 16)
                sp.wait_ge(tails_ready, 1)
                sp.dma_start(by_q(D["tails"], 1), ends[:, 0, :]).then_inc(tails_saved, 16)
                sp.wait_ge(tails_saved, 16)
                sp.dma_start(before[:], by_q(D["tails"])).then_inc(before_loaded, 16)
                sp.wait_ge(small_ready, 2)
                G = CHUNK_STEPS
                for h in range(P // G):
                    for m in range(2):
                        at = D["offs"][1 - m + h:, m, :]
                        sp.dma_start(at[0:1 + (B - 1) * (P // G):P // G, :].rearrange("b g -> g b"),
                                     near_i[h * G:(h + 1) * G, m, :]).then_inc(offs_saved, 16)
                sp.wait_ge(offs_saved, 16 * 2 * (P // G))
                sp.dma_start(by_q(D["rels"]), at_f[:]).then_inc(saved, 16)
                sp.dma_start(D["offs"][0, 0:1, :], zero_pads[0:1, 0:G]).then_inc(saved, 16)
                sp.dma_start(D["offs"][K // G, 1:2, :], zero_pads[0:1, 0:G]).then_inc(saved, 16)
            sp.wait_ge(masks_ready, 1)
            sp.dma_start(D["masks"].rearrange("(b q) m -> q b m", q=P),
                         masks[:].rearrange("q b m i -> q b (m i)")).then_inc(saved, 16)
            sp.dma_start(D["bounds"][0:K].rearrange("(b q) m -> q b m", q=P), bounds[:]).then_inc(saved, 16)
            sp.dma_start(D["bounds"][K:K + 1], T["ones"][0:1, 0:2]).then_inc(saved, 16)
            sp.wait_ge(saved, 96)
            sp.dma_start(less[:], row(D["rels"]).to_broadcast([P, K])).then_inc(rel_loaded, 16)
            sp.wait_ge(rel_loaded, 16)
            sp.wait_ge(evacuated, 2 * B)
            sp.dma_start(D["src_cols"], src_cols[:]).then_inc(saved, 16)
            sp.wait_ge(saved, 112)

        @block.gpsimd
        def _(pool):
            nc.gpsimd.iota(T["iota_i"][:], pattern=[[1, P]], base=0, channel_multiplier=0).then_inc(consts, 1)
            nc.gpsimd.iota(T["part_i"][:], pattern=[[0, 1]], base=0, channel_multiplier=1).then_inc(consts, 1)
            nc.gpsimd.iota(number_i[:], pattern=[[P, B]], base=0, channel_multiplier=1).then_inc(consts, 1)
            pool.wait_ge(index_ready, 1)
            for n, d in enumerate((D["dst"], D["src"])):
                table = d[0, :].rearrange("(t i) -> t i", i=P)
                for b in range(B):
                    pool.indirect_dma_start(rows_i[:, n, b, :], None, table,
                                            bass.IndirectOffsetOnAxis(tile_i[:, b:b + 1], 0)).then_inc(rows_loaded, 16)

        @block.vector
        def _(v):
            nc.vector.memset(pads[:], pad_node).then_inc(pad_set, 1)
            nc.vector.memset(T["ones"][:], 1.0).then_inc(pad_set, 1)
            nc.vector.memset(zero_pads[:], 0).then_inc(pad_set, 1)
            done = [0]

            def link(instruction):
                done[0] += 1
                instruction.then_inc(chain, 1)
                v.wait_ge(chain, done[0])

            v.wait_ge(consts, 3)
            link(nc.vector.tensor_copy(T["iota"][:], T["iota_i"][:]))
            link(nc.vector.tensor_copy(T["part"][:], T["part_i"][:]))
            link(nc.vector.tensor_copy(number[:], number_i[:]))
            link(nc.vector.tensor_scalar(T["ident"][:], T["iota"][:, 0:P], T["part"][:, 0:1], None, ALU.is_equal))
            v.wait_ge(ends_loaded, 16)
            link(nc.vector.tensor_scalar(ends_i[:, 1, :], ends_i[:, 0, :], 7, None, ALU.arith_shift_right))
            link(nc.vector.tensor_copy(ends[:, 0, :], ends_i[:, 1, :]))
            link(nc.vector.scalar_tensor_tensor(out=ends[:, 1, :], in0=number[:], scalar=1.0, in1=ends[:, 0, :],
                                                op0=ALU.add, op1=ALU.add))
            link(nc.vector.tensor_scalar(shift[:], number[:], z.tiles - 1.5, 1e6, ALU.is_gt, ALU.mult))
            nc.vector.tensor_tensor(ends[:, 2, :], ends[:, 1, :], shift[:], ALU.add).then_inc(turns_ready, 1)
            v.wait_ge(turns_loaded, 16)
            for b in range(B):
                link(nc.vector.tensor_scalar(less[:], turns_all[:], number[:, b:b + 1], None, ALU.is_le, ALU.add,
                                             accum_out=tile_f[:, b:b + 1]))
            nc.vector.tensor_copy(tile_i[:], tile_f[:]).then_inc(index_ready, 1)
            link(nc.vector.tensor_tensor(block_f[:], number[:], tile_f[:], ALU.subtract))
            link(nc.vector.tensor_scalar_min(near[:], block_f[:], float(z.node_tiles - 1)))
            link(nc.vector.tensor_tensor(column[:], number[:], near[:], ALU.subtract))
            link(nc.vector.tensor_scalar_add(column[:], column[:], float(z.node_tiles)))
            link(nc.vector.tensor_copy(near_i[:, 1, :], column[:]))
            link(nc.vector.tensor_scalar_mul(near[:], near[:], float(z.row)))
            nc.vector.tensor_copy(near_i[:, 0, :], near[:]).then_inc(small_ready, 1)
            link(nc.vector.tensor_scalar_mul(shift[:], block_f[:], -float(P)))
            v.wait_ge(rows_loaded, 32 * B)
            link(nc.vector.tensor_copy(rows[:], rows_i[:]))
            d = rows[:, 0, :, :]
            nc.vector.tensor_copy(ends[:, 0, :], d[:, :, P - 1]).then_inc(tails_ready, 1)
            link(nc.vector.tensor_tensor(at_f[:], d[:, :, 0], shift[:], ALU.add))
            nc.vector.memset(near[:], 0.0).then_inc(small_ready, 1)
            for b in range(B):
                for m, at in ((1, 0), (2, P - 1)):
                    link(nc.vector.tensor_scalar(masks[:, b, m, :], d[:, b, :], d[:, b, at:at + 1], -BIG,
                                                 ALU.not_equal, ALU.mult))
            link(nc.vector.tensor_tensor(starts[:, :, 1:P], d[:, :, 1:P], d[:, :, 0:P - 1], ALU.not_equal))
            v.wait_ge(before_loaded, 16)
            link(nc.vector.tensor_tensor(starts[:, :, 0], d[:, :, 0], before[:], ALU.not_equal))
            link(nc.vector.memset(starts[0:1, 0, 0:1], 1.0))
            link(nc.vector.tensor_scalar_mul(masks[:, :, 0, :], starts[:], -BIG))
            link(nc.vector.tensor_copy(bounds[:, :, 0], masks[:, :, 0, 0]))
            nc.vector.tensor_copy(bounds[:, :, 1], masks[:, :, 1, P - 1]).then_inc(masks_ready, 1)
            v.wait_ge(masks_ready, 1)
            for b in range(B):
                last = nc.vector.tensor_scalar_add(starts[:, b, :], d[:, b, :], shift[:, b:b + 1])
            last.then_inc(pos_ready, 1)
            for b in range(B):
                for n in range(2):
                    k = 2 * b + n
                    v.wait_ge(turned, k + 1)
                    got = ps[:, k % 4, 0:P]
                    if n == 0:
                        nc.vector.tensor_scalar_mul(T["neg_pos"][:, b * P:(b + 1) * P], got, -1.0).then_inc(evacuated, 1)
                    else:
                        nc.vector.tensor_copy(src_cols[:, b * P:(b + 1) * P], got).then_inc(evacuated, 1)
            v.wait_ge(rel_loaded, 16)
            first = less[:, 0:z.chunks * CHUNK_STEPS].rearrange("p (c g) -> p c g", g=CHUNK_STEPS)[:, :, 0]
            link(nc.vector.tensor_scalar(T["open_node"][:], first, T["part"][:, 0:1], None, ALU.is_equal))
            link(nc.vector.tensor_scalar(T["other_node"][:], first, T["part"][:, 0:1], None, ALU.not_equal))

        @block.tensor
        def _(pe):
            pe.wait_ge(pos_ready, 1)
            for b in range(B):
                for n, table in enumerate((starts, rows)):
                    k = 2 * b + n
                    if k >= 4:
                        pe.wait_ge(evacuated, k - 3)
                    one = table[:, b, :] if n == 0 else table[:, 1, b, :]
                    nc.tensor.transpose(ps[:, k % 4, 0:P], one, T["ident"][:]).then_inc(turned, 1)


def weights(nc, z, Wn, bn, We, be, attn, T):
    K = z.k1
    with ExitStack() as ctx:
        sb = lambda name, shape, dt=F32: ctx.enter_context(nc.sbuf_tensor(name, shape, dt))
        sem = z.semaphore
        wn = sb("wn", [P, K, z.dim])
        we = sb("we", [P, K, z.edge_dim])
        at = sb("attn_col", [P, K])
        at_wide = sb("attn_wide", [P, K, P])
        bnc, bec = sb("bn_col", [P, K]), sb("be_col", [P, K])
        bias_sum = sb("bias_sum", [P, K])
        ps = [ctx.enter_context(nc.psum_tensor(f"weight_ps{i}", [P, 512], F32)) for i in range(6)]
        loaded, ready, turned, chain = sem("weights_loaded"), sem("wide_ready"), sem("weights_turned"), sem("weight_chain")
        block = ctx.enter_context(nc.Block())

        @block.sync
        def _(sp):
            sp.dma_start(wn[:], Wn.rearrange("(k p) n -> p k n", p=P)).then_inc(loaded, 16)
            sp.dma_start(we[:], We.rearrange("(k p) n -> p k n", p=P)).then_inc(loaded, 16)
            with nc.allow_non_contiguous_dma(reason="three columns of 256 elements"):
                sp.dma_start(at[:], attn[0, 0, :].rearrange("(k p) -> p k", p=P)).then_inc(loaded, 16)
                sp.dma_start(bnc[:], bn.rearrange("(k p) -> p k", p=P)).then_inc(loaded, 16)
                sp.dma_start(bec[:], be.rearrange("(k p) -> p k", p=P)).then_inc(loaded, 16)
            sp.dma_start(T["bias"][:, 0:z.dim], bn.rearrange("(a n) -> a n", a=1).to_broadcast([P, z.dim])).then_inc(loaded, 16)

        @block.vector
        def _(v):
            done = [0]

            def link(instruction):
                done[0] += 1
                instruction.then_inc(chain, 1)
                v.wait_ge(chain, done[0])

            v.wait_ge(loaded, 96)
            for k in range(K):
                nc.vector.tensor_scalar_mul(at_wide[:, k, :], T["ones"][:, 0:P], at[:, k:k + 1]).then_inc(ready, 1)
            nc.vector.tensor_tensor(bias_sum[:], bnc[:], bec[:], ALU.add).then_inc(ready, 1)
            nc.vector.memset(T["wn"][:, :, z.dim:z.dim + 1], 0.0)
            nc.vector.memset(T["bias"][:, z.dim:z.dim + 1], 1.0)
            nc.vector.memset(T["eps"][:], EPS)
            v.wait_ge(turned, 1)
            for k in range(K):
                nc.vector.tensor_copy(T["wn"][:, k, 0:z.dim], ps[k][:, 0:z.dim])
                nc.vector.tensor_copy(T["wn"][:, k, z.dim + 1:z.dim + 2], ps[2 + k][:, 0:1])
            nc.vector.tensor_copy(T["we"][:], ps[4][:, 0:z.edge_dim])
            nc.vector.tensor_copy(T["bias"][:, z.dim + 1:z.dim + 2], ps[5][:, 0:1])

        @block.tensor
        def _(pe):
            pe.wait_ge(ready, K + 1)
            for k in range(K):
                for n in range(K):
                    nc.tensor.transpose(ps[k][:, n * P:(n + 1) * P], wn[:, n, k * P:(k + 1) * P], T["ident"][:])
                for n in range(K):
                    nc.tensor.matmul(ps[2 + k][:, 0:1], wn[:, n, k * P:(k + 1) * P], at[:, n:n + 1],
                                     start=(n == 0), stop=(n == K - 1))
            for n in range(K):
                nc.tensor.matmul(ps[4][:, 0:z.edge_dim], at_wide[:, n, :], we[:, n, :], start=(n == 0), stop=(n == K - 1))
            for n in range(K):
                last = nc.tensor.matmul(ps[5][:, 0:1], at_wide[:, n, :], bias_sum[:, n:n + 1],
                                        start=(n == 0), stop=(n == K - 1))
            last.then_inc(turned, 1)


def load_rows(sp, z, out, dram, t, last, sem):
    if last:
        sp.dma_start(out[0:z.last_rows], dram[(z.node_tiles - 1) * P:z.nodes, :]).then_inc(sem, 16)
    else:
        sp.dma_start(out, dram[ds(t * P, P), :]).then_inc(sem, 16)


def behind(z, n, u, ring):
    if u >= ring:
        return n * z.turn + u - ring + 1
    return (n - 1) * z.turn + max(w for w in range(z.turn) if w % ring == u) + 1


def node_turns(engine, z, turn):
    turn(0, True)
    with engine.Fori(1, z.turns) as n:
        turn(n, False)


def node_table(nc, z, x, T, D, acc):
    K, W, U = z.k1, z.row, z.turn
    RING, HR = 3, 5
    with ExitStack() as ctx:
        sem = z.semaphore
        many = lambda name, shape: [ctx.enter_context(nc.sbuf_tensor(f"{name}{u}", shape, F32)) for u in range(U)]
        xt, stats, mv, std, rstd, xn, xnT, row = map(many, (
            "node_x", "node_stats", "node_mv", "node_std", "node_rstd", "node_xn", "node_xnT", "node_row"), (
            [P, z.dim], [P, 6], [P, 2], [P, 1], [P, 1], [P, z.dim], [P, K, P], [P, W]))
        zeros = ctx.enter_context(nc.sbuf_tensor("zeros", [P, 8, z.dim], F32))
        psT = [ctx.enter_context(nc.psum_tensor(f"node_psT{i}", [P, K, P], F32)) for i in range(RING)]
        psH = [ctx.enter_context(nc.psum_tensor(f"node_psH{i}", [P, 512], F32)) for i in range(HR)]
        x_loaded, row_saved = z.rows_in, z.rows_out
        (stats_ready, mv_ready, std_ready, rstd_ready, xn_ready, xn_turned, xnT_ready, h_ready,
         row_ready) = map(sem, ("stats_ready", "mv_ready", "std_ready", "rstd_ready", "xn_ready", "xn_turned",
                                "xnT_ready", "h_ready", "row_ready"))
        zeros_set, zeroed = sem("zeros_set"), sem("zeroed")
        block = ctx.enter_context(nc.Block())

        @block.sync
        def _(sp):
            def turn(n, first, last=False):
                for u in range(U):
                    if not first:
                        sp.wait_ge(xn_ready, (n - 1) * U + u + 1)
                    load_rows(sp, z, xt[u][:], x, n * U + u, last and u == U - 1, x_loaded[u])

            turn(0, True)
            with sp.Fori(1, z.turns - 1) as n:
                turn(n, False)
            turn(z.turns - 1, False, True)

        @block.gpsimd
        def _(pool):
            nc.gpsimd.memset(zeros[:], 0.0).then_inc(zeros_set, 1)
            pool.wait_ge(zeros_set, 1)
            rows = z.experts * z.slots
            for at in range(0, rows, 8 * P):
                n = min(8, (rows - at) // P)
                pool.dma_start(D["buf"][at:at + n * P, :].rearrange("(p k) n -> p k n", k=n), zeros[:, 0:n, :])\
                    .then_inc(zeroed, 16)
            nc.gpsimd.memset(acc[:], 0.0)
            pool.wait_ge(zeroed, 16 * ceil_div(rows, 8 * P))

        @block.scalar
        def _(act):
            def store(n, u, last=False):
                act.wait_ge(row_ready, n * U + u + 1)
                if last:
                    act.dma_start(D["table"][(z.node_tiles - 1) * P:z.nodes, :], row[u][0:z.last_rows, :])\
                       .then_inc(row_saved[u], 16)
                else:
                    act.dma_start(D["table"][ds((n * U + u) * P, P), :], row[u][:]).then_inc(row_saved[u], 16)

            def turn(n, first):
                for u in range(U):
                    act.wait_ge(mv_ready, n * U + u + 1)
                    if not first:
                        act.wait_ge(rstd_ready, (n - 1) * U + u + 1)
                    nc.scalar.activation(std[u][:], mv[u][:, 1:2], ACT.Sqrt, bias=T["eps"][:, 0:1]).then_inc(std_ready, 1)
                for u in range(U):
                    act.wait_ge(xn_turned, n * U + u + 1)
                    if not first:
                        act.wait_ge(h_ready, (n - 1) * U + u + 1)
                    nc.scalar.copy(xnT[u][:], psT[u % RING][:]).then_inc(xnT_ready, 1)
                if not first:
                    for u in range(U):
                        store(n - 1, u)

            node_turns(act, z, turn)
            for u in range(U):
                store(z.turns - 1, u, last=(u == U - 1))
            for u in range(U):
                act.wait_ge(row_saved[u], 16 * z.turns)

        @block.vector
        def _(v):
            def rows(n, tiles, first=False):
                for u in tiles:
                    v.wait_ge(h_ready, n * U + u + 1)
                    if not first:
                        v.wait_ge(row_saved[u], 16 * n)
                    nc.vector.tensor_tensor(row[u][:], psH[u % HR][:, 0:W], T["bias"][:], ALU.add).then_inc(row_ready, 1)

            def turn(n, looped=False):
                first = not looped and n == 0
                for u in range(U):
                    v.wait_ge(x_loaded[u], 16 * n + 16)
                    v.sem_inc(z.passed, 1)
                    nc.vector.bn_stats(stats[u][:], xt[u][:]).then_inc(stats_ready, 1)
                for u in range(U):
                    v.wait_ge(stats_ready, n * U + u + 1)
                    v.sem_inc(z.passed, 1)
                    nc.vector.bn_aggr(mv[u][:], stats[u][:]).then_inc(mv_ready, 1)
                if not first:
                    rows(n - 1, range(U // 2), not looped)
                for u in range(U):
                    v.wait_ge(std_ready, n * U + u + 1)
                    nc.vector.reciprocal(rstd[u][:], std[u][:]).then_inc(rstd_ready, 1)
                for u in range(U):
                    v.wait_ge(rstd_ready, n * U + u + 1)
                    if not first:
                        v.wait_ge(xn_turned, (n - 1) * U + u + 1)
                    nc.vector.tensor_scalar(xn[u][:], xt[u][:], mv[u][:, 0:1], rstd[u][:, 0:1],
                                            ALU.subtract, ALU.mult).then_inc(xn_ready, 1)
                if not first:
                    rows(n - 1, range(U // 2, U), not looped)

            turn(0)
            turn(1)
            with v.Fori(2, z.turns) as n:
                turn(n, looped=True)
            rows(z.turns - 1, range(U))

        @block.tensor
        def _(pe):
            def turn(n, first):
                for u in range(U):
                    pe.wait_ge(xn_ready, n * U + u + 1)
                    if not (first and u < RING):
                        pe.wait_ge(xnT_ready, behind(z, n, u, RING))
                    for k in range(K):
                        last = nc.tensor.transpose(psT[u % RING][:, k, :], xn[u][:, k * P:(k + 1) * P],
                                                   T["ident"][:])
                    last.then_inc(xn_turned, 1)
                for u in range(U):
                    pe.wait_ge(xnT_ready, n * U + u + 1)
                    if not (first and u < HR):
                        pe.wait_ge(row_ready, behind(z, n, u, HR))
                    for k in range(K):
                        last = nc.tensor.matmul(psH[u % HR][:, 0:W], xnT[u][:, k, :], T["wn"][:, k, :],
                                                start=(k == 0), stop=(k == K - 1))
                    last.then_inc(h_ready, 1)

            node_turns(pe, z, turn)


def early(c, k):
    return isinstance(c, int) and c < k


def in_threes(engine, start, end, group):
    numbered = lambda a, b: [(c % 3, c // 3, c) for c in range(a, b)]
    a, b = min(end, 3 * ceil_div(start, 3)), max(start, 3 * (end // 3))
    if start < a:
        group(numbered(start, a))
    if b - a > 3:
        with engine.Fori(a // 3, b // 3) as n:
            group([(i, n, 3 * n + i) for i in range(3)])
    elif a < b:
        group(numbered(a, b))
    if max(a, b) < end:
        group(numbered(max(a, b), end))


def edges(nc, z, edge_attr, T, D, acc):
    C, G, W, DC = z.chunks, CHUNK_STEPS, z.row, z.dot_chunks
    S = z.dim + 1
    RING = 4
    H = G // 2
    LEAD = z.node_tiles
    with ExitStack() as ctx:
        sb = lambda name, shape, dt=F32: ctx.enter_context(nc.sbuf_tensor(name, shape, dt))
        ps = lambda name, shape: ctx.enter_context(nc.psum_tensor(name, shape, F32))
        sem = z.semaphore
        three = lambda name: [sem(f"{name}{i}") for i in range(3)]
        rows = [sb(f"gathered{i}", [P, G, W]) for i in range(3)]
        idx = [sb(f"chunk_src{i}", [P, G], I32) for i in range(3)]
        ea = [sb(f"edge_rows{i}", [P, H, P]) for i in range(3)]
        masks = [sb(f"chunk_masks{i}", [G, 3, P]) for i in range(3)]
        bounds = [sb(f"chunk_bounds{i}", [1, 2 * G + 1]) for i in range(3)]
        offsets = [sb(f"chunk_offsets{i}", [1, 2 * G], I32) for i in range(4)]
        dots, raw, score = sb("dots", [P, LEAD + z.table]), sb("raw_score", [P, G]), sb("score", [P, G])
        new_dots, aligned = sb("new_dots", [P, G]), sb("aligned_dots", [P, G])
        half_dotted, aligned_ready = sem("half_dotted"), sem("aligned_ready")
        fwd, seg = sb("fwd_max", [G, P]), sb("seg_max", [G, P])
        ends_fwd = [sb(f"ends_fwd{i}", [1, 2 * G]) for i in range(3)]
        ends = sb("ends_max", [1, 2 * G])
        cols = sb("end_cols", [G, 2])
        seg_a, seg_b, centred, expd = (sb(n, [G, P]) for n in ("seg_a", "seg_b", "centred", "expd"))
        goes_on, rise, rise_on = sb("goes_on", [1, 1]), sb("rise", [1, 1]), sb("rise_on", [1, 1])
        rescale, factor = sb("rescale", [P, 1]), sb("factor", [P, 1])
        prob = [sb(f"prob{i}", [P, G]) for i in range(3)]
        neg_prob = [sb(f"neg_prob{i}", [P, G]) for i in range(3)]
        dist = sb("dist", [P, RING, P])
        onehot = sb("onehot", [P, RING, P])
        psA, psE = ps("psA", [G, 512]), ps("psE", [P, 512])
        psX, psY = ps("psX", [1, 512]), ps("psY", [P, 512])
        sums = [ps(f"sums{i}", [P, 512]) for i in range(RING)]

        idx_loaded, gathered = three("idx_loaded"), three("gathered")
        ea_loaded, masks_loaded = three("ea_loaded"), three("masks_loaded")
        (dots_ready, raw_ready, score_ready, score_rows, fwd_ready, seg_ready, ends_rows, ends_fwd_ready,
         ends_ready, on_ready, rise_ready, rise_on_ready, cols_ready, cols_copied, seg_a_ready, seg_b_ready,
         centred_ready, exp_ready, exp_cols, prob_ready, neg_ready, rescale_ready, factor_ready) = map(sem, (
             "dots_ready", "raw_ready", "score_ready", "score_rows", "fwd_ready", "seg_ready", "ends_rows",
             "ends_fwd_ready", "ends_ready", "on_ready", "rise_ready", "rise_on_ready", "cols_ready",
             "cols_copied", "seg_a_ready", "seg_b_ready", "centred_ready", "exp_ready", "exp_cols", "prob_ready",
             "neg_ready", "rescale_ready", "factor_ready"))
        dist_ready, onehot_ready, step_summed, step_added = (
            sem("dist_ready"), sem("onehot_ready"), sem("step_summed"), sem("step_added"))
        carry_set = sem("carry_set")
        first_offsets = sem("first_offsets")
        no_max = sb("no_max", [1, 1])
        block = ctx.enter_context(nc.Block())

        @block.gpsimd
        def _(pool):
            def group(chunks):
                for i, n, c in chunks:
                    pool.wait_ge(idx_loaded[i], 16 * n + 16)
                    for g in range(G):
                        if g % 4 == 0:
                            if not early(c, 3):
                                pool.wait_ge(step_summed, (c - 3) * G + g + 4)
                            pool.sem_inc(z.passed, 1)
                        pool.indirect_dma_start(rows[i][:, g, 0:W], None, D["table"][:, :],
                                                bass.IndirectOffsetOnAxis(idx[i][:, g:g + 1], 0)).then_inc(gathered[i], 16)

            in_threes(pool, 0, 3, group)
            in_threes(pool, 3, C, group)

        @block.sync
        def _(sp):
            view = edge_attr[0:(z.tiles - 1) * P, :].rearrange("(t p) n -> p t n", p=P)
            masks_v = D["masks"].rearrange("t (m i) -> t m i", m=3)
            offs_v = D["offs"].rearrange("c m g -> c (m g)")
            flat = D["bounds"].rearrange("t m -> (t m)").rearrange("(a n) -> a n", a=1)

            def indices(i, n, c):
                if not early(c, 3):
                    sp.wait_ge(gathered[i], 16 * G * n)
                with nc.allow_non_contiguous_dma(reason="16 indices of each partition"):
                    sp.dma_start(idx[i][:], D["src_cols"][:, ds(c * G, G)]).then_inc(idx_loaded[i], 16)

            def edge_rows(i, n, c):
                for half in range(2):
                    r = (2 * i + half) % 3
                    if not early(2 * c + half, 3):
                        sp.wait_ge(half_dotted, 2 * c + half - 2)
                    at = c * G + half * H
                    if early(c, DC - 1) or not isinstance(c, int):
                        sp.dma_start(ea[r][:], view[:, ds(at, H), :]).then_inc(ea_loaded[r], 16)
                    else:
                        full = min(H, z.tiles - 1 - at)
                        if full > 0:
                            sp.dma_start(ea[r][:, 0:full, :], view[:, at:at + full, :]).then_inc(ea_loaded[r], 16)
                        if 0 <= full < H:
                            sp.dma_start(ea[r][0:z.last_edges, full, :], edge_attr[z.edges - z.last_edges:z.edges, :])\
                              .then_inc(ea_loaded[r], 16)

            def chunk_masks(i, n, c):
                if not early(c, 3):
                    sp.wait_ge(seg_b_ready, c - 2)
                    sp.wait_ge(on_ready, c - 2)
                    sp.wait_ge(ends_ready, c - 2)
                    sp.wait_ge(step_added, (c - 3) * G + 1)
                sp.dma_start(masks[i][:], masks_v[ds(c * G, G)]).then_inc(masks_loaded[i], 16)
                sp.dma_start(bounds[i][:], flat[:, ds(c * 2 * G, 2 * G + 1)]).then_inc(masks_loaded[i], 16)
                sp.dma_start(offsets[i][:], offs_v[ds(c + 1, 1), :]).then_inc(masks_loaded[i], 16)

            def with_edges(chunks):
                for chunk in chunks:
                    indices(*chunk)
                    edge_rows(*chunk)
                    chunk_masks(*chunk)

            def without_edges(chunks):
                for chunk in chunks:
                    indices(*chunk)
                    chunk_masks(*chunk)

            sp.dma_start(offsets[3][:], offs_v[0:1, :]).then_inc(first_offsets, 16)
            in_threes(sp, 0, 3, with_edges)
            in_threes(sp, 3, DC - 1, with_edges)
            in_threes(sp, DC - 1, DC, with_edges)
            in_threes(sp, DC, C, without_edges)

        @block.vector
        def _(v):
            def edge_dots(i, n, c, g0, g1):
                for g in range(g0, g1):
                    r, half = (2 * i + g // H) % 3, g // H
                    if g % H == 0:
                        partial = isinstance(c, int) and c == DC - 1
                        at = (DC - 1) * G + half * H
                        pieces = (min(H, z.tiles - 1 - at) > 0) + (0 <= z.tiles - 1 - at < H) if partial else 1
                        v.wait_ge(ea_loaded[r], 16 * (2 * n + (2 * i + half) // 3 + pieces))
                    if g == 0 and not early(c, 1):
                        v.wait_ge(dots_ready, c)
                    op = nc.vector.tensor_tensor_reduce(out=ea[r][:, g % H, :], in0=ea[r][:, g % H, :], in1=T["we"][:],
                                                        scale=1.0, scalar=0.0, op0=ALU.mult, op1=ALU.add,
                                                        accum_out=new_dots[:, g:g + 1])
                    if g % H == H - 1:
                        op.then_inc(half_dotted, 1)

            def keep_dots(c):
                v.wait_ge(half_dotted, 2 * c + 2)
                nc.vector.tensor_copy(dots[:, ds(LEAD + c * G, G)], new_dots[:]).then_inc(dots_ready, 1)

            def score_steps(i, n, c, columns, ahead):
                first = early(c, 1)

                def align(g0, g1):
                    if g0 == 0:
                        v.wait_ge(dots_ready, c + 1 if c_has_dots else DC)
                        if not first:
                            v.wait_ge(raw_ready, c)
                    for g in range(g0, g1):
                        if ahead:
                            edge_dots(*ahead, g, g + 1)
                        op = nc.vector.tensor_copy(aligned[:, g:g + 1], dots[:, ds(columns[g], 1)])
                    if g1 == G:
                        op.then_inc(aligned_ready, 1)

                c_has_dots = ahead or (isinstance(c, int) and c < DC)

                def raw_scores():
                    if ahead:
                        keep_dots(ahead[2])
                    v.wait_ge(gathered[i], 16 * G * (n + 1))
                    v.wait_ge(aligned_ready, c + 1)
                    if not first:
                        v.wait_ge(score_ready, c)
                    nc.vector.tensor_tensor(raw[:], rows[i][:, :, W - 1], aligned[:], ALU.add).then_inc(raw_ready, 1)

                def scores():
                    v.wait_ge(raw_ready, c + 1)
                    if not first:
                        v.wait_ge(score_rows, c)
                    nc.vector.scalar_tensor_tensor(out=score[:], in0=raw[:], scalar=SLOPE, in1=raw[:],
                                                   op0=ALU.mult, op1=ALU.max).then_inc(score_ready, 1)

                def forward():
                    v.wait_ge(score_rows, c + 1)
                    v.wait_ge(masks_loaded[i], 48 * (n + 1))
                    if not first:
                        v.wait_ge(seg_ready, c)
                    nc.vector.tensor_tensor_scan(fwd[:], masks[i][:, 0, :], psA[:, 0:P], -BIG, ALU.add, ALU.max)\
                             .then_inc(fwd_ready, 1)

                def backward():
                    v.wait_ge(fwd_ready, c + 1)
                    if not first:
                        v.wait_ge(seg_a_ready, c)
                    flat = masks[i][:].rearrange("g m i -> g (m i)")
                    nc.vector.tensor_tensor_scan(seg[:, ::-1], flat[:, P:0:-1], fwd[:, ::-1], -BIG, ALU.add, ALU.max)\
                             .then_inc(seg_ready, 1)

                def ends_forward():
                    v.wait_ge(ends_rows, c + 1)
                    if first:
                        v.wait_ge(carry_set, 2)
                    else:
                        v.wait_ge(ends_fwd_ready, c)
                        v.wait_ge(rise_ready, c)
                    carry = no_max[:, 0:1] if first else ends_fwd[(i + 2) % 3][:, 2 * G - 1:2 * G]
                    nc.vector.tensor_tensor_scan(ends_fwd[i][:], bounds[i][:, 0:2 * G], psX[:, 0:2 * G], carry,
                                                 ALU.add, ALU.max).then_inc(ends_fwd_ready, 1)

                def ends_backward():
                    v.wait_ge(ends_fwd_ready, c + 1)
                    if not first:
                        v.wait_ge(cols_ready, c)
                        v.wait_ge(rise_ready, c)
                    nc.vector.tensor_tensor_scan(ends[:, ::-1], bounds[i][:, 2 * G:0:-1], ends_fwd[i][:, ::-1], -BIG,
                                                 ALU.add, ALU.max).then_inc(ends_ready, 1)

                def open_segment():
                    if not first:
                        v.wait_ge(rise_on_ready, c)
                    nc.vector.tensor_scalar(goes_on[:], bounds[i][:, 0:1], 0.0, None, ALU.is_equal).then_inc(on_ready, 1)
                    v.wait_ge(ends_ready, c + 1)
                    carry = no_max[:, 0:1] if first else ends_fwd[(i + 2) % 3][:, 2 * G - 1:2 * G]
                    nc.vector.tensor_tensor(rise[:], carry, ends[:, 0:1], ALU.subtract).then_inc(rise_ready, 1)

                def open_rise():
                    v.wait_ge(rise_ready, c + 1)
                    v.wait_ge(on_ready, c + 1)
                    if not first:
                        v.wait_ge(cols_ready, c)
                    nc.vector.tensor_tensor(rise_on[:], rise[:], goes_on[:], ALU.mult).then_inc(rise_on_ready, 1)

                def end_columns():
                    v.wait_ge(cols_ready, c + 1)
                    if not first:
                        v.wait_ge(seg_b_ready, c)
                    nc.vector.tensor_copy(cols[:], psY[0:G, 0:2]).then_inc(cols_copied, 1)

                def first_segments():
                    v.wait_ge(cols_copied, c + 1)
                    v.wait_ge(seg_ready, c + 1)
                    if not first:
                        v.wait_ge(seg_b_ready, c)
                    nc.vector.scalar_tensor_tensor(out=seg_a[:], in0=masks[i][:, 1, :], scalar=cols[:, 0:1], in1=seg[:],
                                                   op0=ALU.add, op1=ALU.max).then_inc(seg_a_ready, 1)

                def last_segments():
                    v.wait_ge(seg_a_ready, c + 1)
                    if not first:
                        v.wait_ge(centred_ready, c)
                    nc.vector.scalar_tensor_tensor(out=seg_b[:], in0=masks[i][:, 2, :], scalar=cols[:, 1:2], in1=seg_a[:],
                                                   op0=ALU.add, op1=ALU.max).then_inc(seg_b_ready, 1)

                def centre():
                    v.wait_ge(seg_b_ready, c + 1)
                    if not first:
                        v.wait_ge(exp_ready, c)
                    nc.vector.tensor_tensor(centred[:], psA[:, 0:P], seg_b[:], ALU.subtract).then_inc(centred_ready, 1)

                quarters = [lambda a=a: align(a, a + G // 4) for a in range(0, G, G // 4)]
                nothing = lambda: None
                return quarters + [
                    lambda: (raw_scores(), scores()), forward, backward, ends_forward, ends_backward,
                    lambda: (open_segment(), open_rise()), lambda: (end_columns(), first_segments()), last_segments,
                    centre, nothing, nothing, nothing]

            def open_factor(c):
                v.wait_ge(rescale_ready, c + 1)
                if not early(c, 1):
                    v.wait_ge(step_added, (c - 1) * G + 1)
                nc.vector.scalar_tensor_tensor(out=factor[:], in0=T["open_node"][:, ds(c, 1)], scalar=rescale[:, 0:1],
                                               in1=T["other_node"][:, ds(c, 1)], op0=ALU.mult, op1=ALU.add)\
                         .then_inc(factor_ready, 1)

            def steps(c, places, scoring):
                for g in range(G):
                    if not (early(c, 1) and g == 0):
                        v.wait_ge(step_added, c * G + g)
                    v.wait_ge(step_summed, c * G + g + 1)
                    at = acc[:, ds(places[g], S)]
                    if g == 0:
                        v.wait_ge(factor_ready, c + 1)
                        nc.vector.scalar_tensor_tensor(out=at, in0=at, scalar=factor[:, 0:1], in1=sums[0][:, 0:S],
                                                       op0=ALU.mult, op1=ALU.add).then_inc(step_added, 1)
                    else:
                        nc.vector.tensor_tensor(at, sums[g % RING][:, 0:S], at, ALU.add).then_inc(step_added, 1)
                    if scoring:
                        scoring[g]()
                if scoring:
                    open_factor(c + 1)

            nc.vector.memset(no_max[:], -BIG).then_inc(carry_set, 1)
            nc.vector.memset(dots[:, LEAD + DC * G:], 0.0).then_inc(carry_set, 1)
            regs = [v.alloc_register(f"offset_{g}") for g in range(2 * G)]

            def load(table):
                v.load(regs, table[0:1, :])
                return ([v.snap(r, min_val=0, max_val=(z.node_tiles - 1) * W) for r in regs[0:G]],
                        [v.snap(r, min_val=0, max_val=LEAD + z.table - 1) for r in regs[G:]])

            def group(chunks, with_dots=True, with_scores=True):
                for i, n, c in chunks:
                    up = lambda by: ((i + by) % 3, n + (i + by) // 3, c + by)
                    v.wait_ge(masks_loaded[i], 48 * (n + 1))
                    v.sem_inc(z.passed, 1)
                    places, columns = load(offsets[i])
                    steps(c, places, score_steps(*up(1), columns, up(2) if with_dots else None) if with_scores else None)

            for c in range(2):
                edge_dots(c, 0, c, 0, G)
                keep_dots(c)
            v.wait_ge(first_offsets, 16)
            for step in score_steps(0, 0, 0, load(offsets[3])[1], None):
                step()
            open_factor(0)
            in_threes(v, 0, 3, group)
            in_threes(v, 3, DC - 3, group)
            in_threes(v, DC - 3, DC - 2, group)
            in_threes(v, DC - 2, DC - 1, lambda chunks: group(chunks, with_dots=False))
            in_threes(v, DC - 1, C - 1, lambda chunks: group(chunks, with_dots=False))
            in_threes(v, C - 1, C, lambda chunks: group(chunks, with_scores=False))

        @block.scalar
        def _(act):
            def exps(c):
                act.wait_ge(centred_ready, c + 1)
                if not early(c, 1):
                    act.wait_ge(exp_cols, c)
                nc.scalar.activation(expd[:], centred[:], ACT.Exp).then_inc(exp_ready, 1)
                act.wait_ge(cols_ready, c + 1)
                if not early(c, 1):
                    act.wait_ge(factor_ready, c)
                nc.scalar.activation(rescale[:], psY[:, 2:3], ACT.Exp).then_inc(rescale_ready, 1)

            def probs(i, c):
                act.wait_ge(exp_cols, c + 1)
                if not early(c, 3):
                    act.wait_ge(onehot_ready, (c - 2) * G)
                nc.scalar.activation(prob[i][:], psE[:, 0:G], ACT.Copy).then_inc(prob_ready, 1)
                nc.scalar.activation(neg_prob[i][:], psE[:, 0:G], ACT.Copy, scale=-1.0).then_inc(neg_ready, 1)

            def distance(c, g):
                if not (early(c, 1) and g < RING):
                    act.wait_ge(onehot_ready, c * G + g - RING + 1)
                nc.scalar.activation(dist[:, g % RING, :], T["iota"][:], ACT.Abs, bias=T["neg_pos"][:, ds(c * G + g, 1)])\
                         .then_inc(dist_ready, 1)

            def tile(i, c, g):
                act.wait_ge(dist_ready, c * G + g + 1)
                if g == 0:
                    act.wait_ge(prob_ready, c + 1)
                    act.wait_ge(neg_ready, c + 1)
                if not (early(c, 1) and g < RING):
                    act.wait_ge(step_summed, c * G + g - RING + 1)
                nc.scalar.activation(onehot[:, g % RING, :], dist[:, g % RING, :], ACT.Relu,
                                     scale=neg_prob[i][:, g:g + 1], bias=prob[i][:, g:g + 1]).then_inc(onehot_ready, 1)

            def group(chunks, last=False):
                for i, n, c in chunks:
                    for g in range(G):
                        if g + 1 < G:
                            distance(c, g + 1)
                        elif not last:
                            distance(c + 1, 0)
                        tile(i, c, g)
                    if not last:
                        exps(c + 1)
                        probs((i + 1) % 3, c + 1)

            exps(0)
            probs(0, 0)
            distance(0, 0)
            in_threes(act, 0, 3, group)
            in_threes(act, 3, C - 1, group)
            in_threes(act, C - 1, C, lambda chunks: group(chunks, last=True))

        @block.tensor
        def _(pe):
            def turn_scores(c):
                pe.wait_ge(score_ready, c + 1)
                if not early(c, 1):
                    pe.wait_ge(centred_ready, c)
                nc.tensor.transpose(psA[:, 0:P], score[:], T["ident"][:]).then_inc(score_rows, 1)

            def turn_ends(c):
                pe.wait_ge(seg_ready, c + 1)
                if not early(c, 1):
                    pe.wait_ge(ends_fwd_ready, c)
                pe.sem_inc(z.passed, 1)
                nc.tensor.transpose(psX[:, 0:2 * G:2], seg[:, 0:1], T["ident"][0:G, 0:G])
                nc.tensor.transpose(psX[:, 1:2 * G:2], seg[:, P - 1:P], T["ident"][0:G, 0:G]).then_inc(ends_rows, 1)

            def turn_back(c):
                pe.wait_ge(ends_ready, c + 1)
                pe.wait_ge(rise_on_ready, c + 1)
                if not early(c, 1):
                    pe.wait_ge(cols_copied, c)
                    pe.wait_ge(rescale_ready, c)
                pe.sem_inc(z.passed, 1)
                for n in range(2):
                    nc.tensor.transpose(psY[0:G, n:n + 1], ends[:, n:2 * G:2], T["ident"][0:1, 0:1])
                nc.tensor.matmul(psY[:, 2:3], T["ones"][0:1, 0:P], rise_on[:], start=True, stop=True)\
                         .then_inc(cols_ready, 1)

            def turn_exps(c):
                pe.wait_ge(exp_ready, c + 1)
                if not early(c, 1):
                    pe.wait_ge(prob_ready, c)
                    pe.wait_ge(neg_ready, c)
                pe.sem_inc(z.passed, 1)
                nc.tensor.transpose(psE[:, 0:G], expd[:], T["ident"][0:G, 0:G]).then_inc(exp_cols, 1)

            def tile(i, c, g):
                pe.wait_ge(onehot_ready, c * G + g + 1)
                if not (early(c, 1) and g < RING):
                    pe.wait_ge(step_added, c * G + g - RING + 1)
                nc.tensor.matmul(sums[g % RING][:, 0:S], onehot[:, g % RING, :], rows[i][:, g, 0:S],
                                 start=True, stop=True).then_inc(step_summed, 1)

            def group(chunks, last=False):
                for i, n, c in chunks:
                    for g in range(G):
                        tile(i, c, g)
                        if not last and g == 8:
                            turn_scores(c + 1)
                        if not last and g == 9:
                            turn_ends(c + 1)
                        if not last and g == 12:
                            turn_back(c + 1)
                    if not last:
                        turn_exps(c + 1)

            turn_scores(0)
            turn_ends(0)
            turn_back(0)
            turn_exps(0)
            in_threes(pe, 0, 3, group)
            in_threes(pe, 3, C - 1, group)
            in_threes(pe, C - 1, C, lambda chunks: group(chunks, last=True))


def gate(nc, z, x, gate_w, gate_b, T, acc):
    NT, E, K, U, W = z.node_tiles, z.experts, z.k1, z.turn, z.row
    RING = 3
    x1 = lambda t: acc[:, ds(t * W, z.dim)]
    with ExitStack() as ctx:
        sb = lambda name, shape, dt=F32: ctx.enter_context(nc.sbuf_tensor(name, shape, dt))
        many = lambda name, shape: [sb(f"{name}{u}", shape) for u in range(U)]
        sem = z.semaphore
        xt, gnn, stats, mv, std, xn, xnT = map(many, (
            "gate_x", "gate_gnn", "gate_stats", "gate_mv", "gate_std", "gate_xn", "gate_xnT"), (
            [P, z.dim], [P, z.dim], [P, 6], [P, 2], [P, 1], [P, z.dim], [P, K, P]))
        gw, gb = sb("gate_weights", [P, K, E]), sb("gate_bias", [P, U, E])
        den, inv = sb("den", [P, NT]), sb("inv", [P, NT])
        logits = sb("logits", [P, NT, E])
        psT = [ctx.enter_context(nc.psum_tensor(f"gate_psT{i}", [P, K, P], F32)) for i in range(RING)]
        psL = ctx.enter_context(nc.psum_tensor("gate_psL", [P, U, E], F32))
        psR = ctx.enter_context(nc.psum_tensor("route_ps", [P, 4, 512], F32))
        w_loaded, inv_ready = sem("gate_w_loaded"), sem("inv_ready")
        x_loaded, before_x = z.rows_in, 16 * z.turns
        (gnn_ready, x1_ready, stats_ready, mv_ready, std_ready, rstd_ready, mean_ready, xn_ready, xn_turned,
         xnT_ready, l_ready, logit_ready) = map(sem, (
             "g_gnn_ready", "g_x1_ready", "g_stats_ready", "g_mv_ready", "g_std_ready", "g_rstd_ready",
             "g_mean_ready", "g_xn_ready", "g_xn_turned", "g_xnT_ready", "g_l_ready", "g_logit_ready"))
        chain, shifted, exped, hot_ready, counted = (
            sem("route_chain"), sem("logits_shifted"), sem("logits_exp"), sem("hot_ready"), sem("counted"))
        tri = sb("tri_incl", [P, P])
        best, total, first_e = sb("best", [P, NT]), sb("total", [P, NT]), sb("first_e", [P, NT])
        w_a, w_b, w_c = sb("route_a", [P, NT, E]), sb("route_b", [P, NT, E]), sb("route_c", [P, NT, E])
        expert_no = sb("expert_no", [P, NT, E])
        hot = sb("hot", [P, E, NT])
        keep = sb("route_keep", [P, E, NT])
        before, after = sb("before", [P, E, NT]), sb("after", [P, E, NT])
        place, kept, slot_f = sb("place", [P, NT]), sb("kept", [P, NT]), sb("slot_f", [P, NT])
        block = ctx.enter_context(nc.Block())

        @block.sync
        def _(sp):
            sp.dma_start(gw[:], gate_w.rearrange("(k p) e -> p k e", p=P)).then_inc(w_loaded, 16)
            sp.dma_start(gb[:], gate_b.rearrange("(a b e) -> a b e", a=1, b=1).to_broadcast([P, U, E])).then_inc(w_loaded, 16)

            def turn(n, first, last=False):
                for u in range(U):
                    if not first:
                        sp.wait_ge(x1_ready, (n - 1) * U + u + 1)
                    load_rows(sp, z, xt[u][:], x, n * U + u, last and u == U - 1, x_loaded[u])

            turn(0, True)
            with sp.Fori(1, z.turns - 1) as n:
                turn(n, False)
            turn(z.turns - 1, False, True)

        @block.scalar
        def _(act):
            def relus(n, first):
                for u in range(U):
                    if not first:
                        act.wait_ge(x1_ready, (n - 1) * U + u + 1)
                    nc.scalar.activation(gnn[u][:], x1(n * U + u), ACT.Relu, scale=inv[:, ds(n * U + u, 1)])\
                             .then_inc(gnn_ready, 1)

            def turn(n, first, last=False):
                for u in range(U):
                    act.wait_ge(mv_ready, n * U + u + 1)
                    if not first:
                        act.wait_ge(rstd_ready, (n - 1) * U + u + 1)
                    nc.scalar.activation(std[u][:], mv[u][:, 1:2], ACT.Sqrt, bias=T["eps"][:, 0:1]).then_inc(std_ready, 1)
                if not last:
                    relus(n + 1, False)
                for u in range(U):
                    act.wait_ge(xn_turned, n * U + u + 1)
                    if not first:
                        act.wait_ge(l_ready, (n - 1) * U + u + 1)
                    nc.scalar.copy(xnT[u][:], psT[u % RING][:]).then_inc(xnT_ready, 1)

            act.wait_ge(inv_ready, 1)
            relus(0, True)
            turn(0, True)
            with act.Fori(1, z.turns - 1) as n:
                turn(n, False)
            turn(z.turns - 1, False, True)
            act.wait_ge(shifted, 1)
            nc.scalar.activation(w_b[:], w_a[:], ACT.Exp).then_inc(exped, 1)

        @block.vector
        def _(v):
            def add_bias(n):
                v.wait_ge(l_ready, (n + 1) * U)
                nc.vector.tensor_tensor(logits[:, ds(n * U, U), :], psL[:], gb[:], ALU.add).then_inc(logit_ready, 1)

            def turn(n, first):
                for u in range(U):
                    v.wait_ge(x_loaded[u], before_x + 16 * n + 16)
                    v.wait_ge(gnn_ready, n * U + u + 1)
                    nc.vector.tensor_tensor(x1(n * U + u), xt[u][:], gnn[u][:], ALU.add).then_inc(x1_ready, 1)
                for u in range(U):
                    v.wait_ge(x1_ready, n * U + u + 1)
                    v.sem_inc(z.passed, 1)
                    nc.vector.bn_stats(stats[u][:], x1(n * U + u)).then_inc(stats_ready, 1)
                for u in range(U):
                    v.wait_ge(stats_ready, n * U + u + 1)
                    v.sem_inc(z.passed, 1)
                    nc.vector.bn_aggr(mv[u][:], stats[u][:]).then_inc(mv_ready, 1)
                for u in range(U):
                    v.wait_ge(mv_ready, n * U + u + 1)
                    nc.vector.tensor_copy(T["mean"][:, ds(n * U + u, 1)], mv[u][:, 0:1]).then_inc(mean_ready, 1)
                if not first:
                    add_bias(n - 1)
                for u in range(U):
                    v.wait_ge(std_ready, n * U + u + 1)
                    nc.vector.reciprocal(T["rstd"][:, ds(n * U + u, 1)], std[u][:]).then_inc(rstd_ready, 1)
                for u in range(U):
                    v.wait_ge(mean_ready, n * U + u + 1)
                    v.wait_ge(rstd_ready, n * U + u + 1)
                    if not first:
                        v.wait_ge(xn_turned, (n - 1) * U + u + 1)
                    nc.vector.tensor_scalar(xn[u][:], x1(n * U + u), T["mean"][:, ds(n * U + u, 1)],
                                            T["rstd"][:, ds(n * U + u, 1)], ALU.subtract, ALU.mult).then_inc(xn_ready, 1)

            done = [0]

            def link(instruction):
                done[0] += 1
                instruction.then_inc(chain, 1)
                v.wait_ge(chain, done[0])

            link(nc.vector.tensor_scalar_add(den[:], acc[:].rearrange("p (t w) -> p w t", w=W)[:, z.dim, :], 1e-16))
            nc.vector.reciprocal(inv[:], den[:]).then_inc(inv_ready, 1)
            v.wait_ge(w_loaded, 32)
            node_turns(v, z, turn)
            add_bias(z.turns - 1)
            v.wait_ge(logit_ready, z.turns)
            wide = lambda t: t[:].unsqueeze(2).to_broadcast([P, NT, E])
            link(nc.vector.tensor_scalar(tri[:], T["iota"][:, 0:P], T["part"][:, 0:1], None, ALU.is_ge))
            link(nc.vector.memset(keep[:], 1.0))
            link(nc.vector.memset(keep[:, :, 0:1], 0.0))
            for e in range(E):
                nc.vector.memset(expert_no[:, :, e:e + 1], float(e))
            link(nc.vector.tensor_reduce(best[:], logits[:], AX.X, ALU.max))
            nc.vector.tensor_tensor(w_a[:], logits[:], wide(best), ALU.subtract).then_inc(shifted, 1)
            v.wait_ge(exped, 1)
            link(nc.vector.tensor_reduce(total[:], w_b[:], AX.X, ALU.add))
            link(nc.vector.reciprocal(T["weight"][:], total[:]))
            link(nc.vector.tensor_scalar(w_b[:], w_a[:], 0.0, float(E), ALU.not_equal, ALU.mult))
            link(nc.vector.tensor_tensor(w_c[:], w_b[:], expert_no[:], ALU.add))
            link(nc.vector.tensor_reduce(first_e[:], w_c[:], AX.X, ALU.min))
            link(nc.vector.tensor_tensor(hot[:].rearrange("p e t -> p t e"), expert_no[:], wide(first_e), ALU.is_equal))
            nc.vector.memset(place[:], 0.0).then_inc(hot_ready, 1)
            v.wait_ge(counted, 1)
            h = E // 2
            for n in range(2):
                link(nc.vector.tensor_copy(before[:, n * h:(n + 1) * h, :],
                                           psR[:, 2 + n, 0:h * NT].rearrange("p (e t) -> p e t", e=h)))
            f = lambda t: t[:].rearrange("p e t -> p (e t)")
            link(nc.vector.tensor_tensor_scan(f(after), f(keep), f(before), 0.0, ALU.mult, ALU.add))
            link(nc.vector.tensor_tensor(after[:], after[:], before[:], ALU.subtract))
            for n in range(2):
                link(nc.vector.tensor_tensor(before[:, n * h:(n + 1) * h, :], after[:, n * h:(n + 1) * h, :],
                                             psR[:, n, 0:h * NT].rearrange("p (e t) -> p e t", e=h), ALU.add))
            link(nc.vector.tensor_tensor(after[:], before[:], hot[:], ALU.mult))
            link(nc.vector.tensor_reduce(place[:], after[:].rearrange("p e t -> p t e"), AX.X, ALU.add))
            link(nc.vector.tensor_scalar(kept[:], place[:], z.capacity + 0.5, None, ALU.is_lt))
            link(nc.vector.tensor_tensor(T["weight"][:], T["weight"][:], kept[:], ALU.mult))
            link(nc.vector.scalar_tensor_tensor(out=slot_f[:], in0=first_e[:], scalar=float(z.slots), in1=place[:],
                                                op0=ALU.mult, op1=ALU.add))
            link(nc.vector.tensor_scalar(kept[:], kept[:], -1e6, 1e6 - 1, ALU.mult, ALU.add))
            link(nc.vector.tensor_tensor(slot_f[:], slot_f[:], kept[:], ALU.add))
            nc.vector.tensor_copy(T["slot"][:], slot_f[:])

        @block.tensor
        def _(pe):
            def turn(n, first):
                for u in range(U):
                    pe.wait_ge(xn_ready, n * U + u + 1)
                    if not (first and u < RING):
                        pe.wait_ge(xnT_ready, behind(z, n, u, RING))
                    for k in range(K):
                        last = nc.tensor.transpose(psT[u % RING][:, k, :], xn[u][:, k * P:(k + 1) * P],
                                                   T["ident"][:])
                    last.then_inc(xn_turned, 1)
                if not first:
                    pe.wait_ge(logit_ready, n)
                for u in range(U):
                    pe.wait_ge(xnT_ready, n * U + u + 1)
                    for k in range(K):
                        last = nc.tensor.matmul(psL[:, u, :], xnT[u][:, k, :], gw[:, k, :], start=(k == 0), stop=(k == K - 1))
                    last.then_inc(l_ready, 1)

            pe.wait_ge(w_loaded, 32)
            node_turns(pe, z, turn)
            pe.wait_ge(hot_ready, 1)
            h = E // 2
            for n in range(2):
                half = hot[:, n * h:(n + 1) * h, :].rearrange("p e t -> p (e t)")
                nc.tensor.matmul(psR[:, n, 0:h * NT], tri[:], half, start=True, stop=True)
                last = nc.tensor.matmul(psR[:, 2 + n, 0:h * NT], T["ones"][:, 0:P], half, start=True, stop=True)
            last.then_inc(counted, 1)


def dispatch(nc, z, T, D, x1):
    NT, U = z.node_tiles, z.turn
    with ExitStack() as ctx:
        sb = lambda name, shape, dt=F32: ctx.enter_context(nc.sbuf_tensor(name, shape, dt))
        sem = z.semaphore
        out = [sb(f"sent_row{u}", [P, z.dim]) for u in range(U)]
        idx = [sb(f"sent_idx{u}", [P, 1], I32) for u in range(U)]
        row_ready, idx_ready = sem("sent_row_ready"), sem("sent_idx_ready")
        sent = z.rows_pool
        block = ctx.enter_context(nc.Block())

        @block.vector
        def _(v):
            def turn(n, first):
                for u in range(U):
                    if not first:
                        v.wait_ge(sent[u], 16 * n)
                    t = n * U + u
                    nc.vector.tensor_copy(idx[u][:], T["slot"][:, ds(t, 1)]).then_inc(idx_ready, 1)
                    nc.vector.tensor_scalar(out[u][:], x1[:, ds(t * z.row, z.dim)], T["mean"][:, ds(t, 1)],
                                            T["rstd"][:, ds(t, 1)], ALU.subtract, ALU.mult).then_inc(row_ready, 1)

            node_turns(v, z, turn)

        @block.gpsimd
        def _(pool):
            def turn(n, first):
                for u in range(U):
                    pool.wait_ge(idx_ready, n * U + u + 1)
                    pool.wait_ge(row_ready, n * U + u + 1)
                    pool.sem_inc(z.passed, 1)
                    pool.indirect_dma_start(D["buf"][:, :], bass.IndirectOffsetOnAxis(idx[u][:, 0:1], 0), out[u][:], None,
                                            bounds_check=z.experts * z.slots - 1, oob_is_err=False).then_inc(sent[u], 16)

            node_turns(pool, z, turn)
            for u in range(U):
                pool.wait_ge(sent[u], 16 * z.turns)


def experts(nc, z, w1, b1, w2, b2, T, D):
    E, NB, K1, K2, TB = z.experts, z.blocks, z.k1, z.k2, z.block // P
    HR, RAW = 4, 3
    turns = E // 2
    with ExitStack() as ctx:
        sb = lambda name, shape, dt=F32: ctx.enter_context(nc.sbuf_tensor(name, shape, dt))
        sem = z.semaphore
        pair = lambda name: [sem(f"{name}{i}") for i in range(2)]
        ps = lambda name, k: [ctx.enter_context(nc.psum_tensor(f"{name}{i}", [P, 512], F32)) for i in range(k)]
        assert K1 * z.hidden == K2 * z.dim and NB > 1
        w_raw = sb("w_raw", [P, K1 * z.hidden])
        w1s, w2s = (w_raw[:].rearrange("p (k n) -> p k n", k=k) for k in (K1, K2))
        w1_high, w1_low = sb("w1_high", [P, K1, z.hidden]), sb("w1_low", [P, K1, z.hidden])
        w2_high, w2_low = sb("w2_high", [P, K2, z.dim]), sb("w2_low", [P, K2, z.dim])
        b1s = [sb(f"b1s{i}", [P, K2]) for i in range(2)]
        b2s = [sb(f"b2s{i}", [P, z.dim]) for i in range(2)]
        xs = [sb(f"slot_rows{i}", [P, TB, z.dim]) for i in range(2)]
        x_high, x_low = sb("x_high", [P, K1, z.block]), sb("x_low", [P, K1, z.block])
        h_high, h_low = sb("h_high", [P, K2, z.block]), sb("h_low", [P, K2, z.block])
        h_raw = sb("h_raw", [P, RAW, z.block])
        ys = [sb(f"slot_y{i}", [P, TB, z.dim]) for i in range(2)]
        psT, psH, psY = ps("exp_psT", 2), ps("exp_psH", HR), ps("exp_psY", 2)
        w2_loaded, w1_masked, w1_split, w2_masked, w2_split, x_masked, relu_ready, h_masked = map(sem, (
            "w2_loaded", "w1_masked", "w1_split", "w2_masked", "w2_split", "x_masked", "relu_ready", "h_masked"))
        w_loaded, x_loaded, y_saved = pair("w_loaded"), pair("slots_loaded"), pair("y_saved")
        x_turned, xT_ready, h_ready, hT_ready, y_ready, y_copied = (
            sem("x_turned"), sem("xT_ready"), sem("h_summed"), sem("hT_ready"), sem("y_summed"), sem("y_copied"))
        block = ctx.enter_context(nc.Block())

        def number(m, i, b):
            return 2 * NB * m + i * NB + b

        def uses(m, i, b):
            return NB * m + (i * NB + b) // 2 + 1

        def following(m, i, b):
            return (m, i, b + 1) if b + 1 < NB else (m, 1, 0) if i == 0 else (m + 1, 0, 0)

        def all_blocks(engine, one, before=None):
            def turn(m, first=False, last=False):
                for i in range(2):
                    if before:
                        before(m, i, first)
                    for b in range(NB):
                        one(m, i, b, first, last and i == 1 and b == NB - 1)

            turn(0, first=True)
            with engine.Fori(1, turns - 1) as m:
                turn(m)
            turn(turns - 1, last=True)

        @block.sync
        def _(sp):
            w2_v = w2.rearrange("e (k p) n -> (e k) p n", p=P)
            w1_v = w1.rearrange("e (k p) f -> (e k) p f", p=P)
            b1_v = b1.rearrange("e (k p) -> (e k) p", p=P)

            def load_w(m, i, first):
                e = 2 * m + i
                if not first:
                    sp.wait_ge(y_copied, (2 * m + i - 1) * NB * TB)
                if not (first and i == 0):
                    sp.wait_ge(w2_split, e)
                    sp.sem_inc(z.passed, 1)
                sp.dma_start(w1s, w1_v[ds(e * K1, K1)].rearrange("k p f -> p k f")).then_inc(w_loaded[i], 16)
                with nc.allow_non_contiguous_dma(reason="1024 biases, one per partition and column"):
                    sp.dma_start(b1s[i][:], b1_v[ds(e * K2, K2)].rearrange("k p -> p k")).then_inc(w_loaded[i], 16)
                sp.dma_start(b2s[i][:], b2[ds(e, 1), :].to_broadcast([P, z.dim])).then_inc(w_loaded[i], 16)

            def load_w2(m, i):
                sp.wait_ge(w1_split, 2 * m + i + 1)
                sp.sem_inc(z.passed, 1)
                sp.dma_start(w2s, w2_v[ds((2 * m + i) * K2, K2)].rearrange("k p n -> p k n")).then_inc(w2_loaded, 16)

            def load_x(m, i, b, first, last):
                i2 = (i * NB + b) % 2
                if not (first and i * NB + b < 2):
                    sp.wait_ge(x_turned, (number(m, i, b) - 1) * K1)
                sp.dma_start(xs[i2][:], D["buf"][ds(number(m, i, b) * z.block, z.block), :]
                             .rearrange("(t p) n -> p t n", p=P)).then_inc(x_loaded[i2], 16)
                if b == 1:
                    load_w2(m, i)

            all_blocks(sp, load_x, load_w)

        @block.tensor
        def _(pe):
            def turn_rows(m, i, b, first):
                blk, i2 = number(m, i, b), (i * NB + b) % 2
                pe.wait_ge(x_loaded[i2], 16 * uses(m, i, b))
                for k in range(K1):
                    if not first:
                        pe.wait_ge(xT_ready, (blk - 1) * K1 + k + 1)
                    for t in range(TB):
                        op = nc.tensor.transpose(psT[k % 2][:, t * P:(t + 1) * P], xs[i2][:, t, k * P:(k + 1) * P],
                                                 T["ident"][:])
                    op.then_inc(x_turned, 1)

            def one(m, i, b, first, last):
                blk, i2, start = number(m, i, b), (i * NB + b) % 2, first and i * NB + b == 0
                if b == 0:
                    pe.wait_ge(w1_split, 2 * m + i + 1)
                pe.wait_ge(xT_ready, (blk + 1) * K1)
                for f in range(K2):
                    if not (start and f < HR):
                        pe.wait_ge(relu_ready, blk * K2 + f - HR + 1)
                    for k in range(K1):
                        for part, (w, xT) in enumerate(((w1_high, x_high), (w1_high, x_low), (w1_low, x_high))):
                            op = nc.tensor.matmul(psH[f % HR][:], w[:, k, f * P:(f + 1) * P].bitcast(F32R),
                                                  xT[:, k, :].bitcast(F32R), start=(k == 0 and part == 0),
                                                  stop=(k == K1 - 1 and part == 2))
                    op.then_inc(h_ready, 1)
                if not last:
                    turn_rows(*following(m, i, b), False)
                pe.wait_ge(hT_ready, (blk + 1) * K2)
                if b == 0:
                    pe.wait_ge(w2_split, 2 * m + i + 1)
                for t in range(TB):
                    if not (start and t < 2):
                        pe.wait_ge(y_copied, blk * TB + t - 1)
                    for k in range(K2):
                        for part, (h, w) in enumerate(((h_high, w2_high), (h_high, w2_low), (h_low, w2_high))):
                            op = nc.tensor.matmul(psY[t % 2][:, 0:z.dim], h[:, k, t * P:(t + 1) * P].bitcast(F32R),
                                                  w[:, k, :].bitcast(F32R), start=(k == 0 and part == 0),
                                                  stop=(k == K2 - 1 and part == 2))
                    op.then_inc(y_ready, 1)

            turn_rows(0, 0, 0, True)
            all_blocks(pe, one)

        @block.scalar
        def _(act):
            def one(m, i, b, first, last):
                blk, start = number(m, i, b), first and i * NB + b == 0
                if not start:
                    act.wait_ge(y_ready, blk * TB)
                if b == 0:
                    act.wait_ge(w_loaded[i], 48 * (m + 1))
                for f in range(K2):
                    act.wait_ge(h_ready, blk * K2 + f + 1)
                    if f >= RAW:
                        act.wait_ge(hT_ready, blk * K2 + f - RAW + 1)
                    nc.scalar.activation(h_raw[:, f % RAW, :], psH[f % HR][:], ACT.Relu, bias=b1s[i][:, f:f + 1])\
                             .then_inc(relu_ready, 1)

            all_blocks(act, one)

        @block.vector
        def _(v):
            def high(out, of):
                return nc.vector.tensor_copy(out.bitcast(F32R), of)

            def split_x(m, i, b, start):
                blk = number(m, i, b)
                for k in range(K1):
                    v.wait_ge(x_turned, blk * K1 + k + 1)
                    if k == 0 and not start:
                        v.wait_ge(h_ready, blk * K2)
                    high(x_high[:, k, :], psT[k % 2][:]).then_inc(x_masked, 1)
                for k in range(K1):
                    v.wait_ge(x_masked, blk * K1 + k + 1)
                    nc.vector.tensor_tensor(x_low[:, k, :].bitcast(F32R), psT[k % 2][:], x_high[:, k, :], ALU.subtract).then_inc(xT_ready, 1)

            def split_h(blk):
                for f in range(K2 + 1):
                    if f < K2:
                        v.wait_ge(relu_ready, blk * K2 + f + 1)
                        high(h_high[:, f, :], h_raw[:, f % RAW, :]).then_inc(h_masked, 1)
                    if f > 0:
                        v.wait_ge(h_masked, blk * K2 + f)
                        nc.vector.tensor_tensor(h_low[:, f - 1, :].bitcast(F32R), h_raw[:, (f - 1) % RAW, :], h_high[:, f - 1, :],
                                                ALU.subtract)\
                                 .then_inc(hT_ready, 1)

            def split_w1(m, i, start):
                e = 2 * m + i
                v.wait_ge(w_loaded[i], 48 * (m + 1))
                if not start:
                    v.wait_ge(h_ready, e * NB * K2)
                high(w1_high[:], w1s).then_inc(w1_masked, 1)
                v.wait_ge(w1_masked, e + 1)
                nc.vector.tensor_tensor(w1_low[:].bitcast(F32R), w1s, w1_high[:], ALU.subtract).then_inc(w1_split, 1)

            def split_w2(m, i, start):
                e = 2 * m + i
                v.wait_ge(w2_loaded, 16 * (e + 1))
                if not start:
                    v.wait_ge(y_ready, e * NB * TB)
                high(w2_high[:], w2s).then_inc(w2_masked, 1)
                v.wait_ge(w2_masked, e + 1)
                nc.vector.tensor_tensor(w2_low[:].bitcast(F32R), w2s, w2_high[:], ALU.subtract).then_inc(w2_split, 1)

            def one(m, i, b, first, last):
                blk, i2 = number(m, i, b), (i * NB + b) % 2
                split_h(blk)
                if b == 0:
                    split_w2(m, i, first and i == 0)
                if not last:
                    split_x(*following(m, i, b), False)
                    if b == NB - 1:
                        split_w1(*following(m, i, b)[0:2], False)
                if not (first and i * NB + b < 2):
                    v.wait_ge(y_saved[i2], 16 * (uses(m, i, b) - 1))
                for t in range(TB):
                    v.wait_ge(y_ready, blk * TB + t + 1)
                    nc.vector.tensor_tensor(ys[i2][:, t, :], psY[t % 2][:, 0:z.dim], b2s[i][:], ALU.add).then_inc(y_copied, 1)

            split_w1(0, 0, True)
            split_x(0, 0, 0, True)
            all_blocks(v, one)

        @block.gpsimd
        def _(pool):
            def one(m, i, b, first, last):
                blk, i2 = number(m, i, b), (i * NB + b) % 2
                pool.wait_ge(y_copied, (blk + 1) * TB)
                pool.dma_start(D["y"][ds(blk * z.block, z.block), :].rearrange("(t p) n -> p t n", p=P), ys[i2][:])\
                    .then_inc(y_saved[i2], 16)

            all_blocks(pool, one)
            for i2 in range(2):
                pool.wait_ge(y_saved[i2], 16 * NB * turns)


def combine(nc, z, T, D, x1, out):
    NT, U = z.node_tiles, z.turn
    with ExitStack() as ctx:
        many = lambda name, shape, dt=F32: [ctx.enter_context(nc.sbuf_tensor(f"{name}{u}", shape, dt)) for u in range(U)]
        sem = z.semaphore
        y, ty, low, side, res, total = (many(n, [P, z.dim]) for n in ("y", "ty", "y_low", "y_side", "res", "out_row"))
        finite = many("finite", [P, z.dim], I32)
        idx = many("y_idx", [P, 1], I32)
        y_set, idx_ready, scaled, low_ready, side_ready, finite_ready, res_ready, picked, summed = map(
            sem, ("y_set", "y_idx_ready", "y_scaled", "y_low_ready", "y_side_ready", "y_finite_ready",
                  "res_ready", "y_picked", "res_summed"))
        got, saved = z.rows_pool, z.rows_out
        before = 16 * z.turns
        block = ctx.enter_context(nc.Block())

        @block.gpsimd
        def _(pool):
            def turn(n, first):
                if first:
                    for u in range(U):
                        nc.gpsimd.memset(y[u][:], 0.0).then_inc(y_set, 1)
                for u in range(U):
                    if first:
                        pool.wait_ge(y_set, u + 1)
                    else:
                        pool.wait_ge(scaled, (n - 1) * U + u + 1)
                    pool.wait_ge(idx_ready, n * U + u + 1)
                    pool.sem_inc(z.passed, 1)
                    pool.indirect_dma_start(y[u][:], None, D["y"][:, :], bass.IndirectOffsetOnAxis(idx[u][:, 0:1], 0),
                                            bounds_check=z.experts * z.slots - 1, oob_is_err=False).then_inc(got[u], 16)

            node_turns(pool, z, turn)

        @block.scalar
        def _(act):
            def turn(n, first):
                for u in range(U):
                    act.wait_ge(got[u], before + 16 * n + 16)
                    if not first:
                        act.wait_ge(picked, (n - 1) * U + u + 1)
                    nc.scalar.activation(ty[u][:], y[u][:], ACT.Copy, scale=T["weight"][:, ds(n * U + u, 1)])\
                             .then_inc(scaled, 1)
                for u in range(U):
                    act.wait_ge(side_ready, n * U + u + 1)
                    if not first:
                        act.wait_ge(summed, (n - 1) * U + u + 1)
                    nc.scalar.activation(res[u][:], side[u][:], ACT.Copy, scale=1e4).then_inc(res_ready, 1)

            node_turns(act, z, turn)

        @block.vector
        def _(v):
            def next_index(n, u):
                nc.vector.tensor_copy(idx[u][:], T["slot"][:, ds(n * U + u, 1)]).then_inc(idx_ready, 1)

            def turn(n, first, last=False):
                for u in range(U):
                    v.wait_ge(scaled, n * U + u + 1)
                    if not last:
                        next_index(n + 1, u)
                    if not first:
                        v.wait_ge(side_ready, (n - 1) * U + u + 1)
                    nc.vector.tensor_scalar(low[u][:], ty[u][:], -F32_MAX, None, ALU.is_lt).then_inc(low_ready, 1)
                    nc.vector.tensor_scalar(finite[u][:], ty[u][:], 0.0, 0.0, ALU.mult, ALU.is_equal)\
                             .then_inc(finite_ready, 1)
                for u in range(U):
                    v.wait_ge(low_ready, n * U + u + 1)
                    if not first:
                        v.wait_ge(res_ready, (n - 1) * U + u + 1)
                    nc.vector.scalar_tensor_tensor(out=side[u][:], in0=ty[u][:], scalar=F32_MAX, in1=low[u][:],
                                                   op0=ALU.is_gt, op1=ALU.subtract).then_inc(side_ready, 1)
                for u in range(U):
                    v.wait_ge(res_ready, n * U + u + 1)
                    v.wait_ge(finite_ready, n * U + u + 1)
                    v.sem_inc(z.passed, 1)
                    nc.vector.copy_predicated(res[u][:], finite[u][:], ty[u][:]).then_inc(picked, 1)
                for u in range(U):
                    v.wait_ge(picked, n * U + u + 1)
                    if not first:
                        v.wait_ge(saved[u], before + 16 * n)
                    nc.vector.tensor_tensor(total[u][:], res[u][:], x1[:, ds((n * U + u) * z.row, z.dim)], ALU.add)\
                             .then_inc(summed, 1)

            for u in range(U):
                next_index(0, u)
            turn(0, True)
            with v.Fori(1, z.turns - 1) as n:
                turn(n, False)
            turn(z.turns - 1, False, last=True)

        @block.sync
        def _(sp):
            def save(n, u, last=False):
                sp.wait_ge(summed, n * U + u + 1)
                if last:
                    sp.dma_start(out[(NT - 1) * P:z.nodes, :], total[u][0:z.last_rows, :]).then_inc(saved[u], 16)
                else:
                    sp.dma_start(out[ds((n * U + u) * P, P), :], total[u][:]).then_inc(saved[u], 16)

            with sp.Fori(0, z.turns - 1) as n:
                for u in range(U):
                    save(n, u)
            for u in range(U):
                save(z.turns - 1, u, last=(u == U - 1))
            for u in range(U):
                sp.wait_ge(saved[u], before + 16 * z.turns)


def gnn_moe(nc, x, src, dst, edge_attr, Wn, bn, We, be, attn, gate_w, gate_b, w1, b1, w2, b2, out):
    z = Sizes(x, src, edge_attr, w1)
    with ExitStack() as ctx:
        z.semaphore = lambda name: ctx.enter_context(nc.semaphore(name))
        z.passed = z.semaphore("passed")
        z.rows_in = [z.semaphore(f"rows_in{u}") for u in range(z.turn)]
        z.rows_pool = [z.semaphore(f"rows_pool{u}") for u in range(z.turn)]
        z.rows_out = [z.semaphore(f"rows_out{u}") for u in range(z.turn)]
        sb = lambda name, shape, dt=F32: ctx.enter_context(nc.sbuf_tensor(name, shape, dt))
        dram = lambda name, shape, dt=F32: nc.dram_tensor(name, shape, dt, kind="Internal").ap()
        D = {
            "src": dram("src_padded", [1, z.pad_edges], I32),
            "dst": dram("dst_padded", [1, z.pad_edges], I32),
            "src_cols": dram("src_columns", [P, z.table], I32),
            "turns": dram("tile_turns", [z.table]),
            "tails": dram("step_tails", [z.table + 1]),
            "masks": dram("segment_masks", [z.table, 3 * P]),
            "bounds": dram("row_bounds", [z.table + 1, 2]),
            "offs": dram("step_offsets", [z.table // CHUNK_STEPS + 1, 2, CHUNK_STEPS], I32),
            "rels": dram("first_positions", [z.table]),
            "table": dram("node_rows", [z.nodes, z.row]),
            "buf": dram("expert_rows", [z.experts * z.slots, z.dim]),
            "y": dram("expert_out", [z.experts * z.slots, z.dim]),
        }
        T = {
            "iota_i": sb("iota_i", [P, P], I32), "part_i": sb("part_i", [P, 1], I32),
            "iota": sb("iota", [P, P]), "part": sb("part", [P, 1]),
            "ones": sb("ones", [P, P]), "ident": sb("ident", [P, P]), "eps": sb("eps", [P, 1]),
            "mean": sb("mean", [P, z.node_tiles]), "rstd": sb("rstd", [P, z.node_tiles]),
            "weight": sb("expert_weight", [P, z.node_tiles]), "slot": sb("slot", [P, z.node_tiles], I32),
        }
        acc = sb("node_sums", [P, z.node_tiles * z.row])
        with ExitStack() as gnn:
            sb = lambda name, shape, dt=F32: gnn.enter_context(nc.sbuf_tensor(name, shape, dt))
            T |= {
                "neg_pos": sb("neg_pos", [P, z.table]),
                "open_node": sb("open_node", [P, z.chunks]), "other_node": sb("other_node", [P, z.chunks]),
                "we": sb("we_attn", [P, z.edge_dim]),
            }
            step_tables(nc, z, src, dst, T, D)
            with nc.sbuf_tensor("wn_t", [P, z.k1, z.row], F32) as wn_t, \
                    nc.sbuf_tensor("bias_row", [P, z.row], F32) as bias_row:
                T |= {"wn": wn_t, "bias": bias_row}
                weights(nc, z, Wn, bn, We, be, attn, T)
                node_table(nc, z, x, T, D, acc)
            edges(nc, z, edge_attr, T, D, acc)
        gate(nc, z, x, gate_w, gate_b, T, acc)
        dispatch(nc, z, T, D, acc)
        experts(nc, z, w1, b1, w2, b2, T, D)
        combine(nc, z, T, D, acc, out)


INPUTS = ["x", "src", "dst", "edge_attr_128", "L0_gnn_Wn", "L0_gnn_bn", "L0_gnn_We", "L0_gnn_be", "L0_gnn_attn",
          "L0_ffn_gate_w", "L0_ffn_gate_b", "L0_ffn_w1", "L0_ffn_b1", "L0_ffn_w2", "L0_ffn_b2"]


def kernel(**inputs):
    import numpy as np
    import concourse.bacc as bacc
    from concourse.bass_utils import run_bass_kernel_spmd

    nc = bacc.Bacc("TRN2", target_bir_lowering=False, num_devices=1)
    arrays, args = {}, []
    for name in INPUTS:
        a = np.ascontiguousarray(inputs[name])
        if name in ("src", "dst"):
            a = a.reshape(1, -1)
        arrays[f"in_{name}"] = a
        args.append(nc.dram_tensor(f"in_{name}", a.shape, mybir.dt.from_np(a.dtype), kind="ExternalInput").ap())
    shape = inputs["x"].shape
    args.append(nc.dram_tensor("out", shape, F32, kind="ExternalOutput").ap())
    gnn_moe(nc, *args)
    r = run_bass_kernel_spmd(nc, [arrays], core_ids=[0])
    return r.results[0]["out"]
```
